# Optimizing a Trainium2 kernel written in Bass

```python
import numpy as np
import jax
import jax.numpy as jnp

def _softmax(x, axis=-1):
    return jax.nn.softmax(x, axis=axis)

def _gelu(x):
    return jax.nn.gelu(x, approximate=True)

def _silu(x):
    return jax.nn.silu(x)

def _sigmoid(x):
    return jax.nn.sigmoid(x)

def _layernorm(x, axis=-1, eps=1e-05):
    m = jnp.mean(x, axis=axis, keepdims=True)
    v = jnp.var(x, axis=axis, keepdims=True)
    return (x - m) / jnp.sqrt(v + eps)

def _scatter_add(tgt, idx, src, axis=0):
    return tgt.at[idx].add(src)

def _segment_sum(src, seg, n):
    return jax.ops.segment_sum(src, seg, n)
kernel_name = 'mk_decoder_postln_d2_seqx_r8_09cc19'

def setup_inputs(seed: int=0):
    np.random.seed(seed)
    _w = jnp.asarray

    def _rec_inputs():
        import jax
        import jax.numpy as jnp
        _rk = jax.random.key(seed)
        x = -0.0002928 + 1 * jax.random.normal(jax.random.fold_in(_rk, 1), (8, 256, 128), jnp.float32)
        _lenS = 256 - jax.random.randint(jax.random.fold_in(_rk, 7), (8,), 0, max(1, 256 // 4) + 1, jnp.int32)
        _lenS2 = 64 - jax.random.randint(jax.random.fold_in(_rk, 8), (8,), 0, max(1, 64 // 4) + 1, jnp.int32)
        _ctx_1024P = jax.random.normal(jax.random.fold_in(_rk, 11), (8, 16, 128), jnp.float32)
        _ctx_1024c = jax.random.dirichlet(jax.random.fold_in(_rk, 511), 0.3 * jnp.ones((16,), jnp.float32), (8, 64))
        _ctx_1024t = jnp.einsum('bsk,bkd->bsd', _ctx_1024c, _ctx_1024P)
        _ctx_1024t = _ctx_1024t * jax.lax.rsqrt(jnp.mean(jnp.square(_ctx_1024t)) + 1e-12) * 0.953939
        ctx_1024 = -1.39393e-06 + 0.999914 * (_ctx_1024t + 0.3 * jax.random.normal(jax.random.fold_in(_rk, 611), (8, 64, 128), jnp.float32))
        _validS = jnp.arange(256)[None, :] < _lenS[:, None]
        _validS2 = jnp.arange(64)[None, :] < _lenS2[:, None]
        _causal = jnp.tril(jnp.ones((256, 256), dtype=bool))
        mask_Bx1xSxS2_bf1 = jnp.ones((8, 1, 256, 64), dtype=bool)
        return (x, ctx_1024, mask_Bx1xSxS2_bf1)
    x, ctx_1024, mask_Bx1xSxS2_bf1 = _rec_inputs()

    def _L0_attn_setup():
        import jax, jax.numpy as jnp
        import numpy as np
        D = 128
        H = 16
        KVH = 4
        HD = D // H
        LAT = 32
        WIN = 32
        B, S = (1, 256)
        BASE_G, BASE_L = (1000000.0, 10000.0)
        EPS = 1e-06

        def rmsnorm(x, w):
            return x * jax.lax.rsqrt(jnp.mean(x * x, axis=-1, keepdims=True) + EPS) * w

        def qk_norm(x):
            return x * jax.lax.rsqrt(jnp.mean(x * x, axis=-1, keepdims=True) + EPS)

        def rope(x, base):
            s, hd = (x.shape[-2], x.shape[-1])
            inv_freq = 1.0 / base ** (jnp.arange(0, hd, 2, dtype=jnp.float32) / hd)
            freqs = jnp.arange(s, dtype=jnp.float32)[:, None] * inv_freq[None, :]
            cos, sin = (jnp.cos(freqs), jnp.sin(freqs))
            xe, xo = (x[..., ::2], x[..., 1::2])
            out = jnp.stack([xe * cos - xo * sin, xe * sin + xo * cos], axis=-1)
            return out.reshape(x.shape)

        def split_heads(x, n_heads):
            b, s, _ = x.shape
            return x.reshape(b, s, n_heads, HD).transpose(0, 2, 1, 3)

        def repeat_kv(x):
            return jnp.repeat(x, H // KVH, axis=1)

        def sdpa(q, k, v, mask):
            scores = jnp.einsum('bhqd,bhkd->bhqk', q, k) / np.sqrt(HD).astype(np.float32)
            scores = jnp.where(mask, scores, jnp.float32(-1e+30))
            probs = jax.nn.softmax(scores, axis=-1)
            return jnp.einsum('bhqk,bhkd->bhqd', probs, v)

        def merge_heads(x):
            b, h, s, hd = x.shape
            return x.transpose(0, 2, 1, 3).reshape(b, s, h * hd)

        def global_latent_attn(x, wq, w_kv_down, w_k_up, w_v_up, wo):
            q = split_heads(x @ wq, H)
            latent = x @ w_kv_down
            k = split_heads(latent @ w_k_up, KVH)
            v = split_heads(latent @ w_v_up, KVH)
            q, k = (rope(q, BASE_G), rope(k, BASE_G))
            q, k = (qk_norm(q), qk_norm(k))
            k, v = (repeat_kv(k), repeat_kv(v))
            i = jnp.arange(x.shape[1])
            causal = i[:, None] >= i[None, :]
            return merge_heads(sdpa(q, k, v, causal)) @ wo

        def local_gqa_attn(x, wq, wk, wv, wo):
            q = split_heads(x @ wq, H)
            k = split_heads(x @ wk, KVH)
            v = split_heads(x @ wv, KVH)
            q, k = (rope(q, BASE_L), rope(k, BASE_L))
            q, k = (qk_norm(q), qk_norm(k))
            k, v = (repeat_kv(k), repeat_kv(v))
            i = jnp.arange(x.shape[1])
            diff = i[:, None] - i[None, :]
            mask = (diff >= 0) & (diff < WIN)
            return merge_heads(sdpa(q, k, v, mask)) @ wo
        key = jax.random.key(seed)
        ks = jax.random.split(key, 12)
        std = 0.02
        return {'hidden': jax.random.normal(ks[0], (B, S, D), dtype=jnp.float32), 'norm1_w': jnp.ones((D,), jnp.float32), 'norm2_w': jnp.ones((D,), jnp.float32), 'g_wq': jax.random.normal(ks[1], (D, H * HD), jnp.float32) * std, 'g_kv_down': jax.random.normal(ks[2], (D, LAT), jnp.float32) * std, 'g_k_up': jax.random.normal(ks[3], (LAT, KVH * HD), jnp.float32) * std, 'g_v_up': jax.random.normal(ks[4], (LAT, KVH * HD), jnp.float32) * std, 'g_wo': jax.random.normal(ks[5], (D, D), jnp.float32) * std, 'l_wq': jax.random.normal(ks[6], (D, H * HD), jnp.float32) * std, 'l_wk': jax.random.normal(ks[7], (D, KVH * HD), jnp.float32) * std, 'l_wv': jax.random.normal(ks[8], (D, KVH * HD), jnp.float32) * std, 'l_wo': jax.random.normal(ks[9], (D, D), jnp.float32) * std}
    _L0_attn_all = _L0_attn_setup()
    _L0_attn_in = {k: v for k, v in _L0_attn_all.items() if k in ('norm1_w', 'norm2_w', 'g_wq', 'g_kv_down', 'g_k_up', 'g_v_up', 'g_wo', 'l_wq', 'l_wk', 'l_wv', 'l_wo')}
    del _L0_attn_all

    def _L0_xattn_setup():
        import jax, jax.numpy as jnp
        import numpy as np
        D_MODEL = 128
        NUM_HEADS = 16
        D_K = D_MODEL // NUM_HEADS
        B, S = (2, 256)
        key = jax.random.key(seed)
        ks = jax.random.split(key, 12)
        sc = 1.0 / np.sqrt(D_MODEL)
        inp = {'q': jax.random.normal(ks[0], (B, S, D_MODEL), jnp.float32), 'k': jax.random.normal(ks[1], (B, S, D_MODEL), jnp.float32), 'v': jax.random.normal(ks[2], (B, S, D_MODEL), jnp.float32), 'mask': jnp.ones((B, 1, S, S), dtype=bool), 'Wq': jax.random.normal(ks[3], (D_MODEL, D_MODEL), jnp.float32) * sc, 'bq': jnp.zeros((D_MODEL,), jnp.float32), 'Wk': jax.random.normal(ks[4], (D_MODEL, D_MODEL), jnp.float32) * sc, 'bk': jnp.zeros((D_MODEL,), jnp.float32), 'Wv': jax.random.normal(ks[5], (D_MODEL, D_MODEL), jnp.float32) * sc, 'bv': jnp.zeros((D_MODEL,), jnp.float32), 'Wo': jax.random.normal(ks[6], (D_MODEL, D_MODEL), jnp.float32) * sc, 'bo': jnp.zeros((D_MODEL,), jnp.float32)}
        return inp
    _L0_xattn_all = _L0_xattn_setup()
    _L0_xattn_in = {k: v for k, v in _L0_xattn_all.items() if k in ('Wq', 'bq', 'Wk', 'bk', 'Wv', 'bv', 'Wo', 'bo')}
    del _L0_xattn_all

    def _L0_ffn_setup():
        import jax, jax.numpy as jnp
        import numpy as np
        B, N, D = (4, 256, 128)
        SPARSITY = 0.01
        key = jax.random.key(seed)
        k1, k2, k3 = jax.random.split(key, 3)
        x = jax.random.normal(k1, (B, N, D), dtype=jnp.float32)
        spatial = jax.random.normal(k2, (D, D), dtype=jnp.float32) * 0.02
        freq = jnp.fft.fft(spatial, axis=-1)
        k = int(D * SPARSITY)
        mag = jnp.abs(freq)
        kth = jax.lax.top_k(mag, k)[0][:, -1:]
        w_sparse = jnp.where(mag >= kth, freq, 0.0 + 0j)
        bias = jax.random.normal(k3, (D,), dtype=jnp.float32) * 0.01
        return {'x': x, 'w_freq_real': jnp.real(w_sparse).astype(jnp.float32), 'w_freq_imag': jnp.imag(w_sparse).astype(jnp.float32), 'bias': bias}
    _L0_ffn_all = _L0_ffn_setup()
    _L0_ffn_in = {k: v for k, v in _L0_ffn_all.items() if k in ('w_freq_real', 'w_freq_imag', 'bias')}
    del _L0_ffn_all

    def _L1_attn_setup():
        import jax, jax.numpy as jnp
        import numpy as np
        import math
        DIM = 128
        N_HEADS = 16
        HEAD_DIM = DIM // N_HEADS

        def rope(x):
            S = x.shape[-2]
            D = x.shape[-1]
            pos = jnp.arange(S, dtype=x.dtype)[:, None]
            dim = jnp.arange(D // 2, dtype=x.dtype)[None, :]
            theta = pos / jnp.exp(2.0 * dim / D * math.log(10000.0))
            sin = jnp.sin(theta)[None, None]
            cos = jnp.cos(theta)[None, None]
            x1 = x[..., ::2]
            x2 = x[..., 1::2]
            out1 = x1 * cos - x2 * sin
            out2 = x1 * sin + x2 * cos
            return jnp.stack([out1, out2], axis=-1).reshape(x.shape)
        key = jax.random.key(seed)
        ks = jax.random.split(key, 9)
        B, S = (2, 256)
        s = 1.0 / math.sqrt(DIM)
        inp = {'x': jax.random.normal(ks[0], (B, S, DIM), dtype=jnp.float32), 'wq': jax.random.normal(ks[1], (DIM, DIM), dtype=jnp.float32) * s, 'bq': jnp.zeros((DIM,), dtype=jnp.float32), 'wk': jax.random.normal(ks[2], (DIM, DIM), dtype=jnp.float32) * s, 'bk': jnp.zeros((DIM,), dtype=jnp.float32), 'wv': jax.random.normal(ks[3], (DIM, DIM), dtype=jnp.float32) * s, 'bv': jnp.zeros((DIM,), dtype=jnp.float32), 'wo': jax.random.normal(ks[4], (DIM, DIM), dtype=jnp.float32) * s, 'bo': jnp.zeros((DIM,), dtype=jnp.float32)}
        return inp
    _L1_attn_all = _L1_attn_setup()
    _L1_attn_in = {k: v for k, v in _L1_attn_all.items() if k in ('wq', 'bq', 'wk', 'bk', 'wv', 'bv', 'wo', 'bo')}
    del _L1_attn_all

    def _L1_xattn_setup():
        import jax, jax.numpy as jnp
        import numpy as np
        DIM = 128
        HEADS = 16
        DIM_HEAD = 64
        INNER = HEADS * DIM_HEAD
        EPS = 1e-05

        def _layernorm(t, w, b):
            mu = jnp.mean(t, axis=-1, keepdims=True)
            var = jnp.mean(jnp.square(t - mu), axis=-1, keepdims=True)
            return (t - mu) * jax.lax.rsqrt(var + EPS) * w + b
        key = jax.random.key(seed)
        ks = jax.random.split(key, 8)
        b, n, l = (8, 512, 64)
        x = jax.random.normal(ks[0], (b, n, DIM), dtype=jnp.float32)
        latents = jax.random.normal(ks[1], (b, l, DIM), dtype=jnp.float32)
        ln1_w = jnp.ones((DIM,), jnp.float32)
        ln1_b = jnp.zeros((DIM,), jnp.float32)
        ln2_w = jnp.ones((DIM,), jnp.float32)
        ln2_b = jnp.zeros((DIM,), jnp.float32)
        Wq = jax.random.normal(ks[2], (DIM, INNER), dtype=jnp.float32) / np.sqrt(DIM)
        Wkv = jax.random.normal(ks[3], (DIM, 2 * INNER), dtype=jnp.float32) / np.sqrt(DIM)
        Wo = jax.random.normal(ks[4], (INNER, DIM), dtype=jnp.float32) / np.sqrt(INNER)
        return {'x': x, 'latents': latents, 'ln1_w': ln1_w, 'ln1_b': ln1_b, 'ln2_w': ln2_w, 'ln2_b': ln2_b, 'Wq': Wq, 'Wkv': Wkv, 'Wo': Wo}
    _L1_xattn_all = _L1_xattn_setup()
    _L1_xattn_in = {k: v for k, v in _L1_xattn_all.items() if k in ('ln1_w', 'ln1_b', 'ln2_w', 'ln2_b', 'Wq', 'Wkv', 'Wo')}
    del _L1_xattn_all

    def _L1_ffn_setup():
        import jax, jax.numpy as jnp
        import numpy as np
        B, S, D = (2, 256, 128)
        E, G, K = (32, 8, 4)
        H, SH = (256, 256)
        CAP_FACTOR = 1.25

        def _l2norm(v):
            n = jnp.linalg.norm(v, axis=-1, keepdims=True)
            return v / jnp.maximum(n, 1e-12)
        key = jax.random.key(seed)
        ks = jax.random.split(key, 10)
        x = jax.random.normal(ks[0], (B, S, D), jnp.float32)
        group_centroids = jax.random.normal(ks[1], (G, D), jnp.float32) * 0.02
        expert_centroids = jax.random.normal(ks[2], (E, D), jnp.float32) * 0.02
        bias = jnp.zeros((E,), jnp.float32)
        sd_in = 1.0 / np.sqrt(D).astype(np.float32)
        sd_h = 1.0 / np.sqrt(H).astype(np.float32)
        wg = jax.random.normal(ks[3], (E, D, H), jnp.float32) * sd_in
        wu = jax.random.normal(ks[4], (E, D, H), jnp.float32) * sd_in
        wd = jax.random.normal(ks[5], (E, H, D), jnp.float32) * sd_h
        sg = jax.random.normal(ks[6], (D, SH), jnp.float32) * sd_in
        su = jax.random.normal(ks[7], (D, SH), jnp.float32) * sd_in
        sd_w = jax.random.normal(ks[8], (SH, D), jnp.float32) * sd_h
        return dict(x=x, group_centroids=group_centroids, expert_centroids=expert_centroids, bias=bias, wg=wg, wu=wu, wd=wd, sg=sg, su=su, sd=sd_w)
    _L1_ffn_all = _L1_ffn_setup()
    _L1_ffn_in = {k: v for k, v in _L1_ffn_all.items() if k in ('group_centroids', 'expert_centroids', 'bias', 'wg', 'wu', 'wd', 'sg', 'su', 'sd')}
    del _L1_ffn_all
    return {'x': x, 'ctx_1024': ctx_1024, 'mask_Bx1xSxS2_bf1': mask_Bx1xSxS2_bf1, 'L0_attn_norm1_w': _L0_attn_in['norm1_w'], 'L0_attn_norm2_w': _L0_attn_in['norm2_w'], 'L0_attn_g_wq': _L0_attn_in['g_wq'], 'L0_attn_g_kv_down': _L0_attn_in['g_kv_down'], 'L0_attn_g_k_up': _L0_attn_in['g_k_up'], 'L0_attn_g_v_up': _L0_attn_in['g_v_up'], 'L0_attn_g_wo': _L0_attn_in['g_wo'], 'L0_attn_l_wq': _L0_attn_in['l_wq'], 'L0_attn_l_wk': _L0_attn_in['l_wk'], 'L0_attn_l_wv': _L0_attn_in['l_wv'], 'L0_attn_l_wo': _L0_attn_in['l_wo'], 'L0_xattn_Wq': _L0_xattn_in['Wq'], 'L0_xattn_bq': _L0_xattn_in['bq'], 'L0_xattn_Wk': _L0_xattn_in['Wk'], 'L0_xattn_bk': _L0_xattn_in['bk'], 'L0_xattn_Wv': _L0_xattn_in['Wv'], 'L0_xattn_bv': _L0_xattn_in['bv'], 'L0_xattn_Wo': _L0_xattn_in['Wo'], 'L0_xattn_bo': _L0_xattn_in['bo'], 'L0_ffn_w_freq_real': _L0_ffn_in['w_freq_real'], 'L0_ffn_w_freq_imag': _L0_ffn_in['w_freq_imag'], 'L0_ffn_bias': _L0_ffn_in['bias'], 'L1_attn_wq': _L1_attn_in['wq'], 'L1_attn_bq': _L1_attn_in['bq'], 'L1_attn_wk': _L1_attn_in['wk'], 'L1_attn_bk': _L1_attn_in['bk'], 'L1_attn_wv': _L1_attn_in['wv'], 'L1_attn_bv': _L1_attn_in['bv'], 'L1_attn_wo': _L1_attn_in['wo'], 'L1_attn_bo': _L1_attn_in['bo'], 'L1_xattn_ln1_w': _L1_xattn_in['ln1_w'], 'L1_xattn_ln1_b': _L1_xattn_in['ln1_b'], 'L1_xattn_ln2_w': _L1_xattn_in['ln2_w'], 'L1_xattn_ln2_b': _L1_xattn_in['ln2_b'], 'L1_xattn_Wq': _L1_xattn_in['Wq'], 'L1_xattn_Wkv': _L1_xattn_in['Wkv'], 'L1_xattn_Wo': _L1_xattn_in['Wo'], 'L1_ffn_group_centroids': _L1_ffn_in['group_centroids'], 'L1_ffn_expert_centroids': _L1_ffn_in['expert_centroids'], 'L1_ffn_bias': _L1_ffn_in['bias'], 'L1_ffn_wg': _L1_ffn_in['wg'], 'L1_ffn_wu': _L1_ffn_in['wu'], 'L1_ffn_wd': _L1_ffn_in['wd'], 'L1_ffn_sg': _L1_ffn_in['sg'], 'L1_ffn_su': _L1_ffn_in['su'], 'L1_ffn_sd': _L1_ffn_in['sd']}

def reference(x, ctx_1024, mask_Bx1xSxS2_bf1, L0_attn_norm1_w, L0_attn_norm2_w, L0_attn_g_wq, L0_attn_g_kv_down, L0_attn_g_k_up, L0_attn_g_v_up, L0_attn_g_wo, L0_attn_l_wq, L0_attn_l_wk, L0_attn_l_wv, L0_attn_l_wo, L0_xattn_Wq, L0_xattn_bq, L0_xattn_Wk, L0_xattn_bk, L0_xattn_Wv, L0_xattn_bv, L0_xattn_Wo, L0_xattn_bo, L0_ffn_w_freq_real, L0_ffn_w_freq_imag, L0_ffn_bias, L1_attn_wq, L1_attn_bq, L1_attn_wk, L1_attn_bk, L1_attn_wv, L1_attn_bv, L1_attn_wo, L1_attn_bo, L1_xattn_ln1_w, L1_xattn_ln1_b, L1_xattn_ln2_w, L1_xattn_ln2_b, L1_xattn_Wq, L1_xattn_Wkv, L1_xattn_Wo, L1_ffn_group_centroids, L1_ffn_expert_centroids, L1_ffn_bias, L1_ffn_wg, L1_ffn_wu, L1_ffn_wd, L1_ffn_sg, L1_ffn_su, L1_ffn_sd):
    import jax
    import jax.numpy as jnp

    def _L0_attn_ref(hidden, norm1_w, norm2_w, g_wq, g_kv_down, g_k_up, g_v_up, g_wo, l_wq, l_wk, l_wv, l_wo):
        import jax, jax.numpy as jnp
        import numpy as np
        D = 128
        H = 16
        KVH = 4
        HD = D // H
        LAT = 32
        WIN = 32
        B, S = (1, 256)
        BASE_G, BASE_L = (1000000.0, 10000.0)
        EPS = 1e-06

        def rmsnorm(x, w):
            return x * jax.lax.rsqrt(jnp.mean(x * x, axis=-1, keepdims=True) + EPS) * w

        def qk_norm(x):
            return x * jax.lax.rsqrt(jnp.mean(x * x, axis=-1, keepdims=True) + EPS)

        def rope(x, base):
            s, hd = (x.shape[-2], x.shape[-1])
            inv_freq = 1.0 / base ** (jnp.arange(0, hd, 2, dtype=jnp.float32) / hd)
            freqs = jnp.arange(s, dtype=jnp.float32)[:, None] * inv_freq[None, :]
            cos, sin = (jnp.cos(freqs), jnp.sin(freqs))
            xe, xo = (x[..., ::2], x[..., 1::2])
            out = jnp.stack([xe * cos - xo * sin, xe * sin + xo * cos], axis=-1)
            return out.reshape(x.shape)

        def split_heads(x, n_heads):
            b, s, _ = x.shape
            return x.reshape(b, s, n_heads, HD).transpose(0, 2, 1, 3)

        def repeat_kv(x):
            return jnp.repeat(x, H // KVH, axis=1)

        def sdpa(q, k, v, mask):
            scores = jnp.einsum('bhqd,bhkd->bhqk', q, k) / np.sqrt(HD).astype(np.float32)
            scores = jnp.where(mask, scores, jnp.float32(-1e+30))
            probs = jax.nn.softmax(scores, axis=-1)
            return jnp.einsum('bhqk,bhkd->bhqd', probs, v)

        def merge_heads(x):
            b, h, s, hd = x.shape
            return x.transpose(0, 2, 1, 3).reshape(b, s, h * hd)

        def global_latent_attn(x, wq, w_kv_down, w_k_up, w_v_up, wo):
            q = split_heads(x @ wq, H)
            latent = x @ w_kv_down
            k = split_heads(latent @ w_k_up, KVH)
            v = split_heads(latent @ w_v_up, KVH)
            q, k = (rope(q, BASE_G), rope(k, BASE_G))
            q, k = (qk_norm(q), qk_norm(k))
            k, v = (repeat_kv(k), repeat_kv(v))
            i = jnp.arange(x.shape[1])
            causal = i[:, None] >= i[None, :]
            return merge_heads(sdpa(q, k, v, causal)) @ wo

        def local_gqa_attn(x, wq, wk, wv, wo):
            q = split_heads(x @ wq, H)
            k = split_heads(x @ wk, KVH)
            v = split_heads(x @ wv, KVH)
            q, k = (rope(q, BASE_L), rope(k, BASE_L))
            q, k = (qk_norm(q), qk_norm(k))
            k, v = (repeat_kv(k), repeat_kv(v))
            i = jnp.arange(x.shape[1])
            diff = i[:, None] - i[None, :]
            mask = (diff >= 0) & (diff < WIN)
            return merge_heads(sdpa(q, k, v, mask)) @ wo
        x = hidden
        x = x + global_latent_attn(rmsnorm(x, norm1_w), g_wq, g_kv_down, g_k_up, g_v_up, g_wo)
        x = x + local_gqa_attn(rmsnorm(x, norm2_w), l_wq, l_wk, l_wv, l_wo)
        return x

    def _L0_xattn_ref(q, k, v, mask, Wq, bq, Wk, bk, Wv, bv, Wo, bo):
        import jax, jax.numpy as jnp
        import numpy as np
        D_MODEL = 128
        NUM_HEADS = 16
        D_K = D_MODEL // NUM_HEADS
        B, S = (2, 256)
        b = q.shape[0]

        def proj(x, W, bias):
            y = jnp.einsum('bsd,ed->bse', x, W) + bias
            return y.reshape(b, -1, NUM_HEADS, D_K).transpose(0, 2, 1, 3)
        qh = proj(q, Wq, bq)
        kh = proj(k, Wk, bk)
        vh = proj(v, Wv, bv)
        scores = jnp.einsum('bhqd,bhkd->bhqk', qh, kh) / np.sqrt(D_K)
        scores = jnp.where(mask, scores, jnp.float32(-1000000000.0))
        attn = jax.nn.softmax(scores, axis=-1)
        out = jnp.einsum('bhqk,bhkd->bhqd', attn, vh)
        out = out.transpose(0, 2, 1, 3).reshape(b, -1, D_MODEL)
        return jnp.einsum('bsd,ed->bse', out, Wo) + bo

    def _L0_ffn_ref(x, w_freq_real, w_freq_imag, bias):
        import jax, jax.numpy as jnp
        import numpy as np
        B, N, D = (4, 256, 128)
        SPARSITY = 0.01
        w = jax.lax.complex(w_freq_real, w_freq_imag)
        x_freq = jnp.fft.fft(x, axis=-1)
        y_freq = jnp.einsum('bnd,do->bno', x_freq, w)
        y = jnp.real(jnp.fft.ifft(y_freq, axis=-1))
        return y + bias

    def _L1_attn_ref(x, wq, bq, wk, bk, wv, bv, wo, bo):
        import jax, jax.numpy as jnp
        import numpy as np
        import math
        DIM = 128
        N_HEADS = 16
        HEAD_DIM = DIM // N_HEADS

        def rope(x):
            S = x.shape[-2]
            D = x.shape[-1]
            pos = jnp.arange(S, dtype=x.dtype)[:, None]
            dim = jnp.arange(D // 2, dtype=x.dtype)[None, :]
            theta = pos / jnp.exp(2.0 * dim / D * math.log(10000.0))
            sin = jnp.sin(theta)[None, None]
            cos = jnp.cos(theta)[None, None]
            x1 = x[..., ::2]
            x2 = x[..., 1::2]
            out1 = x1 * cos - x2 * sin
            out2 = x1 * sin + x2 * cos
            return jnp.stack([out1, out2], axis=-1).reshape(x.shape)
        B, S, _ = x.shape

        def proj(w, b):
            y = jnp.einsum('bsd,ed->bse', x, w) + b
            return y.reshape(B, S, N_HEADS, HEAD_DIM).transpose(0, 2, 1, 3)
        q = rope(proj(wq, bq))
        k = rope(proj(wk, bk))
        v = proj(wv, bv)
        score = jnp.einsum('bhqd,bhkd->bhqk', q, k) / math.sqrt(HEAD_DIM)
        causal = jnp.tril(jnp.ones((S, S), dtype=bool))
        score = jnp.where(causal[None, None], score, -jnp.inf)
        attn = jax.nn.softmax(score, axis=-1)
        out = jnp.einsum('bhqk,bhkd->bhqd', attn, v)
        out = out.transpose(0, 2, 1, 3).reshape(B, S, DIM)
        return jnp.einsum('bsd,ed->bse', out, wo) + bo

    def _L1_xattn_ref(x, latents, ln1_w, ln1_b, ln2_w, ln2_b, Wq, Wkv, Wo):
        import jax, jax.numpy as jnp
        import numpy as np
        DIM = 128
        HEADS = 16
        DIM_HEAD = 64
        INNER = HEADS * DIM_HEAD
        EPS = 1e-05

        def _layernorm(t, w, b):
            mu = jnp.mean(t, axis=-1, keepdims=True)
            var = jnp.mean(jnp.square(t - mu), axis=-1, keepdims=True)
            return (t - mu) * jax.lax.rsqrt(var + EPS) * w + b
        xn = _layernorm(x, ln1_w, ln1_b)
        latn = _layernorm(latents, ln2_w, ln2_b)
        b, l, _ = latn.shape
        q = latn @ Wq
        kv_input = jnp.concatenate([xn, latn], axis=1)
        kv = kv_input @ Wkv
        k, v = jnp.split(kv, 2, axis=-1)

        def heads(t):
            return t.reshape(t.shape[0], t.shape[1], HEADS, DIM_HEAD).transpose(0, 2, 1, 3)
        q, k, v = (heads(q), heads(k), heads(v))
        scale = 1.0 / np.sqrt(np.sqrt(DIM_HEAD))
        weight = jnp.einsum('bhld,bhnd->bhln', q * scale, k * scale)
        weight = jax.nn.softmax(weight.astype(jnp.float32), axis=-1).astype(weight.dtype)
        out = jnp.einsum('bhln,bhnd->bhld', weight, v)
        out = out.transpose(0, 2, 1, 3).reshape(b, l, INNER)
        return out @ Wo

    def _L1_ffn_ref(x, group_centroids, expert_centroids, bias, wg, wu, wd, sg, su, sd):
        import jax, jax.numpy as jnp
        import numpy as np
        B, S, D = (2, 256, 128)
        E, G, K = (32, 8, 4)
        H, SH = (256, 256)
        CAP_FACTOR = 1.25

        def _l2norm(v):
            n = jnp.linalg.norm(v, axis=-1, keepdims=True)
            return v / jnp.maximum(n, 1e-12)
        b, s, d = x.shape
        xf = x.reshape(-1, d)
        N = xf.shape[0]
        shared = jax.nn.silu(xf @ sg) * (xf @ su) @ sd
        xn = _l2norm(xf)
        group_scores = xn @ _l2norm(group_centroids).T
        n_top_groups = max(1, G // 2)
        _, top_group_idx = jax.lax.top_k(group_scores, n_top_groups)
        expert_scores = xn @ _l2norm(expert_centroids).T + bias
        expert_to_group = jnp.arange(E) // (E // G)
        sel = jnp.zeros((N, G), xf.dtype).at[jnp.arange(N)[:, None], top_group_idx].set(1.0)
        group_mask = sel[:, expert_to_group]
        masked = expert_scores * group_mask + (1.0 - group_mask) * -1000000000.0
        top_scores, top_idx = jax.lax.top_k(masked, K)
        gates = jax.nn.softmax(top_scores, axis=-1)
        capacity = max(1, int(N / E * K * CAP_FACTOR))
        flat_e = top_idx.reshape(-1)
        flat_g = gates.reshape(-1)
        tok = jnp.repeat(jnp.arange(N), K)
        onehot = jax.nn.one_hot(flat_e, E, dtype=jnp.int32)
        pos = jnp.cumsum(onehot, axis=0)[jnp.arange(N * K), flat_e] - 1
        keep = pos < capacity
        e_s = jnp.where(keep, flat_e, E)
        p_s = jnp.where(keep, pos, 0)
        buf = jnp.zeros((E + 1, capacity, d), xf.dtype).at[e_s, p_s].set(xf[tok])[:E]
        h = jax.nn.silu(jnp.einsum('ecd,edh->ech', buf, wg)) * jnp.einsum('ecd,edh->ech', buf, wu)
        out_e = jnp.einsum('ech,ehd->ecd', h, wd)
        gathered = out_e[flat_e, jnp.minimum(pos, capacity - 1)]
        contrib = gathered * (flat_g * keep.astype(xf.dtype))[:, None]
        routed = jnp.zeros_like(xf).at[tok].add(contrib)
        return (shared + routed).reshape(b, s, d)
    x = _layernorm(x + _L0_attn_ref(x, L0_attn_norm1_w, L0_attn_norm2_w, L0_attn_g_wq, L0_attn_g_kv_down, L0_attn_g_k_up, L0_attn_g_v_up, L0_attn_g_wo, L0_attn_l_wq, L0_attn_l_wk, L0_attn_l_wv, L0_attn_l_wo), axis=-1)
    x = _layernorm(x + _L0_xattn_ref(x, ctx_1024, ctx_1024, mask_Bx1xSxS2_bf1, L0_xattn_Wq, L0_xattn_bq, L0_xattn_Wk, L0_xattn_bk, L0_xattn_Wv, L0_xattn_bv, L0_xattn_Wo, L0_xattn_bo), axis=-1)
    x = _layernorm(x + _L0_ffn_ref(x, L0_ffn_w_freq_real, L0_ffn_w_freq_imag, L0_ffn_bias), axis=-1)
    x = _layernorm(x + _L1_attn_ref(x, L1_attn_wq, L1_attn_bq, L1_attn_wk, L1_attn_bk, L1_attn_wv, L1_attn_bv, L1_attn_wo, L1_attn_bo), axis=-1)
    x = _layernorm(x + _L1_xattn_ref(ctx_1024, x, L1_xattn_ln1_w, L1_xattn_ln1_b, L1_xattn_ln2_w, L1_xattn_ln2_b, L1_xattn_Wq, L1_xattn_Wkv, L1_xattn_Wo), axis=-1)
    x = _layernorm(x + _L1_ffn_ref(x, L1_ffn_group_centroids, L1_ffn_expert_centroids, L1_ffn_bias, L1_ffn_wg, L1_ffn_wu, L1_ffn_wd, L1_ffn_sg, L1_ffn_su, L1_ffn_sd), axis=-1)
    return x

_drawn_inputs = setup_inputs


def setup_inputs(seed=0):
    import zlib

    import numpy as np

    out = dict(_drawn_inputs(seed))
    spreads = {'L0_attn_norm1_w': (1.0, 0.6),
     'L0_attn_norm2_w': (1.0, 0.6),
     'L0_xattn_bq': (0.0, 0.1),
     'L0_xattn_bk': (0.0, 0.8),
     'L0_xattn_bv': (0.0, 0.1),
     'L0_xattn_bo': (0.0, 0.1),
     'L1_attn_bq': (0.0, 0.1),
     'L1_attn_bk': (0.0, 0.1),
     'L1_attn_bv': (0.0, 0.1),
     'L1_attn_bo': (0.0, 0.1),
     'L1_xattn_ln1_w': (1.0, 0.2),
     'L1_xattn_ln1_b': (0.0, 0.1),
     'L1_xattn_ln2_w': (1.0, 0.2),
     'L1_xattn_ln2_b': (0.0, 0.1),
     'L1_ffn_bias': (0.0, 0.1)}
    factors = {'L0_attn_g_wq': 8.0,
     'L0_attn_g_kv_down': 8.0,
     'L0_attn_g_k_up': 8.0,
     'L0_attn_g_v_up': 8.0,
     'L0_attn_g_wo': 7.123,
     'L0_attn_l_wq': 2.688,
     'L0_attn_l_wk': 2.704}
    for name, (base, spread) in spreads.items():
        noise = np.random.default_rng([zlib.crc32(name.encode()), seed]).standard_normal(out[name].shape)
        drawn = base * np.exp(spread * noise) if base else spread * noise
        out[name] = jnp.asarray(drawn.astype(out[name].dtype))
    for name, factor in factors.items():
        out[name] = (out[name] * factor).astype(out[name].dtype)
    return out
```

```python
from contextlib import ExitStack, contextmanager

import numpy as np

import concourse.bass as bass
from concourse import mybir

ALU = mybir.AluOpType
ACT = mybir.ActivationFunctionType
AX_X = mybir.AxisListType.X
F32 = mybir.dt.float32
BF16 = mybir.dt.bfloat16
I32 = mybir.dt.int32
U32 = mybir.dt.uint32
U8 = mybir.dt.uint8

B, S, D = 8, 256, 128
P = 128
TILES = S // P
C = 64
H, HD = 16, 8
KVH = 4
WIN = 32
PART = 64
ROWS, ROWS_MAX = 6 * HD, 6 * HD + 3
NEG = -1e30
SCALE = 1.0 / float(np.sqrt(HD))


class Counts:

    def __init__(self, name, engine, per):
        self.name, self.engine, self.per = name, engine, per
        self.seen, self.base, self.at, self.loops = {}, {}, None, 0

    def after(self, sem, events=1):
        self.moved(sem, events)
        value = self.seen[sem.name]
        if self.at is not None:
            value = value + self.at * self.per.get((self.name, self.loops, sem.name), 0)
        return value

    def moved(self, sem, events=1):
        self.seen[sem.name] = self.seen.get(sem.name, 0) + events

    def mark(self, *sems):
        for sem in sems:
            self.base[sem.name] = self.seen.get(sem.name, 0)

    def owed(self, sem, events):
        return self.base[sem.name] + events > self.seen.get(sem.name, 0)

    def until(self, sem, events):
        return self.after(sem, self.base[sem.name] + events - self.seen.get(sem.name, 0))

    @contextmanager
    def loop(self, count):
        self.loops += 1
        before = dict(self.seen)
        with self.engine.Fori(0, count) as i:
            self.at = i
            yield i
        self.at = None
        for name, value in self.seen.items():
            n = value - before.get(name, 0)
            self.per[(self.name, self.loops, name)] = n
            self.seen[name] = value + n * (count - 1)


def place(u, side):
    return 2 * u + side


def held_heads(kv_heads):
    if kv_heads == H:
        return list(range(H))
    return [(u // 4) * 8 + side * 4 + u % 4 for u in range(8) for side in range(2)]


MERGED = [place(2 * g + uu, side) for g in range(4) for side in range(2) for uu in range(2)]


class Narrow:

    def __init__(self, name, kv_heads, *, rms=False, rope=False, qk_norm=False, cross=False, bias=False,
                 top=False, mask="causal", norm=True):
        self.name, self.kvh = name, kv_heads
        self.rms, self.rope, self.qk_norm, self.cross = rms, rope, qk_norm, cross
        self.bias, self.top, self.mask, self.norm = bias, top, mask, norm
        self.kn = kv_heads * HD
        self.key_tiles = 1 if cross else TILES
        self.keys = C if cross else P
        self.flat = TILES * D + self.key_tiles * self.kn
        self.ktiles = kv_heads // 2
        spans = {"causal": [(0, 0, S), (1, P, S)], "window": [(0, 0, P + WIN), (1, P, S)], "given": [(0, 0, S)]}[mask]
        self.steps = [(g, kt, q0, q1) for g in range(4) for kt, q0, q1 in spans]
        self.last_kt = spans[-1][0]
        self.top_steps = []
        if top:
            for t in range(TILES):
                n = C if cross else P * (t + 1)
                m = 512 // n
                self.top_steps += [(t, side, u, m, n) for u in range(0, 8, m) for side in range(2)]

    def value_head(self, u, side):
        return place(u, side) if self.kvh == H else 2 * (u // 4) + side

    def key_tile(self, u):
        return u if self.kvh == H else u // 4


class Mixing:

    name, rms, cross = "f", False, False


WH, WD = 16, 64
CHUNKS = WH * WD // P
WKEYS = S + C
KEY_TILES = [(0, P), (P, P), (S, C)]


class Wide:

    name, rms, cross = "w", False, True
    products = ([("q", c) for c in range(0, CHUNKS, 2)] + [("k", c) for c in range(CHUNKS)]
                + [("v", n) for n in range(2 * len(KEY_TILES))])


E, G, K = 32, 8, 4
HID = 256
N = B * S
NT = N // P
CAP = int(N / E * K * 1.25)
SLOT_P, SLOT_J = 80, CAP // 80
RING = 4
BEYOND = float(2 * E * CAP)
GROUP = 4

NARROW = [
    Narrow("g", KVH, rms=True, rope=True, qk_norm=True, norm=False),
    Narrow("l", KVH, rms=True, rope=True, qk_norm=True, mask="window"),
    Narrow("x", H, cross=True, bias=True, top=True, mask="given"),
    Narrow("a", H, rope=True, bias=True, top=True),
]
MIXING, WIDE = Mixing(), Wide()
LAYERS = NARROW[:3] + [MIXING, NARROW[3], WIDE]


def schedule(layer):
    if layer is MIXING:
        return [("core", "mix", 0), ("pre", "norm", 0), ("core", "mixed", 0), ("pre", "turn_x", 0)]
    if layer is WIDE:
        out = [("pre", "norm", 0), ("pre", "turn_x", 0)]
        n = len(layer.products)
        for h in range(WH + 3):
            if h < WH:
                out.append(("core", "wide_scores", h))
            if 1 <= h <= WH:
                out.append(("core", "wide_turn", h - 1))
            if h >= 3 and h % 2:
                out.append(("core", "wide_values", (h - 3) // 2))
            out += [("pre", "wide_project", k) for k in range(n * h // (WH + 3), n * (h + 1) // (WH + 3))]
        return out + [("core", "wide_output", 0)]
    n = len(layer.steps)
    per = n // 4
    scores = [("core", "scores", k) for k in range(n)]
    values = [("core", "values", g) for g in range(4)]
    out = []
    pre = [[("pre", "norm", 0), ("pre", "turn_x", 0)], [("pre", "project", 0)], [("pre", "cut", 0)], []]
    if layer.top:
        pre = [[("pre", "norm", 0), ("pre", "turn_x", 0), ("pre", "project", 0), ("pre", "cut", 0)],
               [("pre", "turn_q", 0), ("pre", "turn_k", 0)],
               [("pre", "top", k) for k in range(len(layer.top_steps) // 2)],
               [("pre", "top", k) for k in range(len(layer.top_steps) // 2, len(layer.top_steps))]]
    for g in range(4):
        out += scores[per * g:per * g + per]
        out += pre[g]
        if g:
            out.append(values[g - 1])
    out.append(values[3])
    out.append(("core", "merge", 0))
    if layer.top:
        out += [("pre", "shift", 0), ("pre", "turn_q", 1)]
    else:
        out += [("pre", "turn_q", 0), ("pre", "turn_k", 0)]
    out += [("core", "output", 0), ("pre", "release", 0)]
    return out


def run_layer(layer, counts, pieces):
    order = schedule(layer)

    def batch(core, pre):
        for phase, name, k in order:
            b = core if phase == "core" else pre
            if b is not None and name in pieces:
                pieces[name](layer, b[0], b[1], k)

    batch(None, (0, 0))
    with counts.loop(B // 2 - 1) as i:
        batch((i * 2, 0), (i * 2 + 1, 1))
        batch((i * 2 + 1, 1), (i * 2 + 2, 0))
    batch((B - 2, 0), (B - 1, 1))
    batch((B - 1, 1), None)


ZEROED = 5


def build_program(nc, t, per, stop=None):
    layers = LAYERS[:stop] if stop else LAYERS
    experts = not stop
    ctx = ExitStack()
    with ctx:
        def sb(name, shape, dt=F32):
            return ctx.enter_context(nc.sbuf_tensor("s_" + name, shape, dt))

        def ps(name, shape, dt=F32):
            return ctx.enter_context(nc.psum_tensor("p_" + name, shape, dt))

        def sem(name):
            return ctx.enter_context(nc.semaphore(name))

        x0 = sb("x0", [P, B * TILES * D])
        xb = sb("xb", [P, B * TILES * D])
        ctx_all = sb("ctx_all", [C, B * D])
        weights = {L.name: sb(f"w_{L.name}", [P, D + 2 * L.kn]) for L in NARROW}
        wo = {L.name: sb(f"wo_{L.name}", [P, D]) for L in NARROW}
        norm_w = {L.name: sb(f"nw_{L.name}", [P, 1]) for L in NARROW if L.rms}
        cos = {L.name: sb(f"cos_{L.name}", [P, L.flat]) for L in NARROW if L.rope}
        sin = {L.name: sb(f"sin_{L.name}", [P, L.flat]) for L in NARROW if L.rope}
        bias_in = {L.name: sb(f"bi_{L.name}", [P, 3 * D]) for L in NARROW if L.bias}
        bias_out = {L.name: sb(f"bo_{L.name}", [P, D]) for L in NARROW if L.bias}
        down_t = sb("down_t", [32, P])
        ups = sb("ups", [32, 2 * KVH * HD])
        given8 = sb("given8", [P, B * TILES * C], U8)
        given = sb("given", [P, B * TILES * C], BF16)
        given_t = sb("given_t", [P, B * S], BF16)
        eye = sb("eye", [P, P])
        eye_b = sb("eye_b", [P, P], BF16)
        causal_q = sb("causal_q", [P, P], BF16)
        causal_k = sb("causal_k", [P, P], BF16)
        window_k = sb("window_k", [P, P + WIN], BF16)

        xs = [sb(f"xs{n}", [P, S]) for n in range(2)]
        xc = sb("xc", [C, D])
        xt = sb("xt", [P, S + C])
        flat_max = 4 * D
        qk = sb("qk", [P, flat_max])
        qk2 = sb("qk2", [P, flat_max])
        qk3 = sb("qk3", [P, flat_max])
        cuts = [sb(f"cut{n}", [P, flat_max], BF16) for n in range(3)]
        stack_words = sb("stack_words", [P, TILES * H * PART])
        stacks = stack_words[:, :].bitcast(BF16)
        q_stack, k_stack = (stacks[:, n * TILES * H * PART:(n + 1) * TILES * H * PART] for n in range(2))
        turned_words = sb("turned_words", [P, 16 * S])
        turned_b = turned_words[:, :].bitcast(BF16)
        qt = [turned_b[:, n * 8 * S:(n + 1) * 8 * S] for n in range(2)]
        kt_ = [turned_b[:, (2 + n) * 8 * S:(3 + n) * 8 * S] for n in range(2)]
        vals_all = sb("vals_all", [P, 2 * TILES * H * 32])
        vals = [vals_all[:, n * TILES * H * 32:(n + 1) * TILES * H * 32] for n in range(2)]
        PROBS = 4
        probs_all = sb("probs_all", [P, PROBS * 4 * S])
        probs = [probs_all[:, n * 4 * S:(n + 1) * 4 * S] for n in range(PROBS)]
        ot = sb("ot", [P, 4 * S])
        rden = sb("rden", [P, 16])
        on = sb("on", [P, TILES * D])
        ont = sb("ont", [P, TILES * D])
        y = sb("y", [P, TILES * D])
        sq = sb("sq", [P, TILES * D])
        ss = sb("ss", [P, 2])
        rs = sb("rs", [P, 2])
        nss = sb("nss", [P, 40])
        nrs = sb("nrs", [P, 40])
        stats = sb("stats", [P, 2 * 6])
        mv = sb("mv", [P, 4])
        lrs = sb("lrs", [P, 2])
        half = sb("half", [P, 40])
        tops = sb("tops", [P, TILES * H])
        top2 = sb("top2", [P, TILES * H])

        fourier = sb("fourier", [P, 5 * D])
        freq_w = sb("freq_w", [P, 2 * D])
        freq_a = sb("freq_a", [P, 2 * D])
        mix_w = sb("mix_w", [P, D])
        bias_mix = sb("bias_mix", [P, D])

        wide_q = sb("wide_q", [P, WH * WD])
        wide_kv = sb("wide_kv", [P, 2 * WH * WD])
        wide_o = sb("wide_o", [P, CHUNKS * D])
        ln_wb = sb("ln_wb", [P, 4])
        wq_t = [probs_all[:, n * CHUNKS * S:(n + 1) * CHUNKS * S] for n in range(2)]
        wk_t = [sb(f"wk_t{n}", [P, CHUNKS * WKEYS]) for n in range(2)]
        wv = [sb(f"wv{n}", [P, len(KEY_TILES) * WH * WD]) for n in range(2)]
        WPROBS = 3
        wprobs = [stack_words[:, n * TILES * WKEYS:(n + 1) * TILES * WKEYS] for n in range(WPROBS)]
        WTURNED = 4
        wturned = [turned_words[:, n * 3 * S:(n + 1) * 3 * S] for n in range(WTURNED)]
        wout_t = vals_all
        wtop = sb("wtop", [P, 2 * WPROBS])
        wden = sb("wden", [P, 2 * WPROBS])
        wrden = sb("wrden", [P, 2 * WPROBS])
        wstats = sb("wstats", [P, 3 * 6])
        wmv = sb("wmv", [P, 3 * 2])
        wrs = sb("wrs", [P, 3])

        centroids = sb("centroids", [G + E, D])
        cent_t = sb("cent_t", [P, G + E])
        cent_s = sb("cent_s", [G + E, 4])
        cent_sq = sb("cent_sq", [G + E, D])
        choice_bias = sb("choice_bias", [P, E])
        before = sb("before", [P, G * G])
        iota_e = sb("iota_e", [P, E])
        iota_i = sb("iota_i", [P, E], I32)
        earlier = sb("earlier", [P, P], BF16)
        ones_b = sb("ones_b", [P, P], BF16)
        zeros = sb("zeros", [P, 8 * D])
        shared_w = sb("shared_w", [P, 2 * HID + 2 * D])
        half_up = sb("half_up", [P, NT])
        slot_in = sb("slot_in", [P, NT * K], U32)
        slot_out = sb("slot_out", [P, NT * K], U32)
        gate = sb("gate", [P, NT * K])
        small = sb("small", [P, 5 * NT])
        lstats = sb("lstats", [P, GROUP * 6])
        lmv = sb("lmv", [P, GROUP * 2])
        glrs = sb("glrs", [P, GROUP])

        class View:

            def __init__(self, buf):
                self.buf, self.at = buf, 0

            def take(self, n):
                self.at += n
                return self.buf[:, self.at - n:self.at]

        spare = View(probs_all)
        xt_all, acc = spare.take(N), spare.take(N)
        spare = View(x0)
        g_score, e_score, top8, idx8 = spare.take(NT * G), spare.take(NT * E), spare.take(NT * 8), spare.take(NT * 8)
        masked, rank, idx_f, pos = spare.take(NT * E), spare.take(NT * G), spare.take(NT * K), spare.take(NT * K)
        gates, keep, tmp_k = spare.take(NT * K), spare.take(NT * K), spare.take(NT * K)
        spare = View(turned_words)
        cmp_gt, cmp_eq, sh_hid = spare.take(NT * G * G), spare.take(NT * G * G), spare.take(1024)
        onehot, picked = vals_all[:, 0:NT * K * E], stack_words[:, 0:NT * K * E]
        spare = View(qk)
        totals = spare.take(NT * E)
        ahead, ahead2 = qk2[:, :], qk3[:, :]
        chosen = cuts[0][:, 0:NT * E]
        ew = [wv[0][:, n * 768:(n + 1) * 768] for n in range(RING)]
        ex_rows = [wk_t[1][0:SLOT_P, n * 512:(n + 1) * 512] for n in range(RING)]
        ex_t = [turned_words[:, 3072 + n * CAP:3072 + (n + 1) * CAP] for n in range(2)]
        ex_g = [wk_t[0][:, n * 2 * CAP:(n + 1) * 2 * CAP] for n in range(2)]
        ex_h = [wk_t[0][:, (2 + n) * 2 * CAP:(3 + n) * 2 * CAP] for n in range(2)]
        ex_out = [wv[1][0:SLOT_P, n * 512:(n + 1) * 512] for n in range(RING)]
        sh_gate = wv[1][:, 2048:3072]
        gathered = [vals_all[:, :], stack_words[:, :]]

        score_ps = [ps(f"score_ps{n}", [P, 2, 512]) for n in range(2)]
        out_ps = ps("out_ps", [P, 512])
        post_ps = ps("post_ps", [P, 512])
        sums_ps = (out_ps, post_ps)
        pre_ps = ps("pre_ps", [P, 512])
        turn_ps = ps("turn_ps", [P, 512])

        loaded = {n: sem(f"loaded_{n}") for n in ("x", "ctx", "mask", "early", "g", "l", "x_", "f", "a", "w")}
        consts = sem("consts")
        waited = sem("waited")
        zeroed = sem("zeroed")
        setup_ps = sem("setup_ps")
        setup_sb = sem("setup_sb")
        v_step = sem("v_step")
        g_step = sem("g_step")
        x_rows = sem("x_rows")
        x_turned = sem("x_turned")
        xt_ready = sem("xt_ready")
        projected = sem("projected")
        pre_read = sem("pre_read")
        stacked = sem("stacked")
        turned = sem("turned")
        operands = sem("operands")
        turn_read = sem("turn_read")
        top_a, top_b = sem("top_a"), sem("top_b")
        shifted = sem("shifted")
        scored = sem("scored")
        probs_ready = sem("probs_ready")
        probs_free = sem("probs_free")
        ot_ready = sem("ot_ready")
        rows_back = sem("rows_back")
        merged = sem("merged")
        merged_turned = sem("merged_turned")
        ont_ready = sem("ont_ready")
        out_projected = sem("out_projected")
        post_read = sem("post_read")
        pow_asked = sem("pow_asked")
        pow_done = sem("pow_done")
        wide_scored = sem("wide_scored")
        topped = sem("topped")
        exped = sem("exped")
        scaled = sem("scaled")
        probs_turned = sem("probs_turned")
        turned_a = sem("turned_a")
        turned_c = sem("turned_c")
        pair_summed = sem("pair_summed")
        pair_out = sem("pair_out")
        wide_made = sem("wide_made")
        wide_a = sem("wide_a")
        wide_v = sem("wide_v")
        exp_loaded = sem("exp_loaded")
        slots_zeroed = sem("slots_zeroed")
        scattered = sem("scattered")
        weights_in = [sem(f"weights_in{n}") for n in range(RING)]
        results_out = [sem(f"results_out{n}") for n in range(RING)]
        gathered_in = [sem(f"gathered_in{n}") for n in range(2)]
        r_ps = sem("r_ps")
        r_sb = sem("r_sb")
        exps_asked = sem("exps_asked")
        exps_made = sem("exps_made")
        slots_known = sem("slots_known")
        sh_made = sem("sh_made")
        sh_silu = sem("sh_silu")
        sh_gated = sem("sh_gated")
        sh_summed = sem("sh_summed")
        rows_turned = sem("rows_turned")
        rows_copied = sem("rows_copied")
        gate_made = sem("gate_made")
        up_made = sem("up_made")
        silued = sem("silued")
        gated = sem("gated")
        downed = sem("downed")
        out_rows = sem("out_rows")
        combined = sem("combined")
        written = sem("written")
        stored = sem("stored")

        block = ctx.enter_context(nc.Block())

        def rows_of(buf, b):
            return buf[:, bass.ts(b, TILES * D)]

        def wide_copy(L, par, k):
            what, c = L.products[k]
            if what == "q":
                return wq_t[par][:, c * S:(c + 2) * S], turn_ps[:, :], 1.0 / float(np.sqrt(WD))
            if what == "k":
                return wk_t[par][:, c * WKEYS:(c + 1) * WKEYS], turn_ps[:, 0:WKEYS], 1.0
            m = KEY_TILES[c // 2][1]
            at = (c // 2) * WH * WD + (c % 2) * 512
            return wv[par][0:m, at:at + 512], turn_ps[0:m, :], 1.0

        @block.sync
        def _(eng):
            eng.dma_start(x0[:, :].rearrange("p (n d) -> p n d", d=D),
                          t["x"].rearrange("b (t p) d -> p (b t) d", p=P)).then_inc(loaded["x"], 16)
            eng.dma_start(down_t[:, :], t["down_t"]).then_inc(loaded["early"], 16)
            eng.dma_start(ups[:, :], t["ups"]).then_inc(loaded["early"], 16)
            for L in NARROW[:2]:
                s = loaded[L.name]
                w = weights[L.name]
                if L.name == "g":
                    eng.dma_start(w[:, 0:D], t["w_g"]).then_inc(s, 16)
                else:
                    eng.dma_start(w[:, :], t["w_l"]).then_inc(s, 16)
                eng.dma_start(wo[L.name][:, :], t[f"wo_{L.name}"]).then_inc(s, 16)
                eng.dma_start(norm_w[L.name][:, :], t[f"nw_{L.name}"]).then_inc(s, 16)
                eng.dma_start(cos[L.name][:, :], t[f"cos_{L.name}"]).then_inc(s, 16)
                eng.dma_start(sin[L.name][:, :], t[f"sin_{L.name}"]).then_inc(s, 16)
            eng.dma_start(ctx_all[:, :].rearrange("p (b d) -> p b d", d=D),
                          t["ctx"].rearrange("b p d -> p b d")).then_inc(loaded["ctx"], 16)
            eng.dma_start(given8[:, :].rearrange("p (n c) -> p n c", c=C),
                          t["mask"].rearrange("b (t p) c -> p (b t) c", p=P)).then_inc(loaded["mask"], 16)
            for L, s in ((NARROW[2], loaded["x_"]), (NARROW[3], loaded["a"])):
                eng.dma_start(weights[L.name][:, :], t[f"w_{L.name}"]).then_inc(s, 16)
                eng.dma_start(wo[L.name][:, :], t[f"wo_{L.name}"]).then_inc(s, 16)
                eng.dma_start(bias_in[L.name][:, :], t[f"bi_{L.name}"]).then_inc(s, 16)
                eng.dma_start(bias_out[L.name][:, :], t[f"bo_{L.name}"]).then_inc(s, 16)
                if L.rope:
                    eng.dma_start(cos[L.name][:, :], t[f"cos_{L.name}"]).then_inc(s, 16)
                    eng.dma_start(sin[L.name][:, :], t[f"sin_{L.name}"]).then_inc(s, 16)
            for n, m in enumerate(("Fr", "Fi", "nFi", "Gr", "nGi")):
                eng.dma_start(fourier[:, n * D:(n + 1) * D], t[m]).then_inc(loaded["f"], 16)
            eng.dma_start(freq_w[:, 0:D], t["freq_r"]).then_inc(loaded["f"], 16)
            eng.dma_start(freq_w[:, D:2 * D], t["freq_i"]).then_inc(loaded["f"], 16)
            eng.dma_start(bias_mix[:, :], t["bias_mix"]).then_inc(loaded["f"], 16)
            eng.dma_start(wide_q[:, :], t["wide_q"]).then_inc(loaded["w"], 16)
            eng.dma_start(wide_kv[:, :], t["wide_kv"]).then_inc(loaded["w"], 16)
            eng.dma_start(wide_o[:, :].rearrange("p (c d) -> p c d", d=D),
                          t["wide_o"].rearrange("(c p) d -> p c d", p=P)).then_inc(loaded["w"], 16)
            eng.dma_start(ln_wb[:, :], t["ln_wb"]).then_inc(loaded["w"], 16)
            if not experts:
                eng.wait_ge(stored, 1)
                eng.dma_start(t["out"].rearrange("b (t p) d -> p (b t) d", p=P),
                              xb[:, :].rearrange("p (n d) -> p n d", d=D)).then_inc(stored, 16)
                eng.wait_ge(stored, 17)
                return
            eng.dma_start(centroids[0:G, :], t["group_c"]).then_inc(exp_loaded, 16)
            eng.dma_start(centroids[G:G + E, :], t["expert_c"]).then_inc(exp_loaded, 16)
            eng.dma_start(choice_bias[:, :], t["choice_bias"]).then_inc(exp_loaded, 16)
            eng.dma_start(shared_w[:, 0:HID], t["sg"]).then_inc(exp_loaded, 16)
            eng.dma_start(shared_w[:, HID:2 * HID], t["su"]).then_inc(exp_loaded, 16)
            eng.dma_start(shared_w[:, 2 * HID:].rearrange("p (c d) -> p c d", c=2),
                          t["sd"].rearrange("(p c) d -> p c d", c=2)).then_inc(exp_loaded, 16)
            eng.wait_ge(zeroed, ZEROED + 1)
            slot_blocks = t["slots"].rearrange("(p n) d -> p (n d)", p=P)
            for n in range(E * CAP // P // 8):
                eng.dma_start(slot_blocks[:, n * 8 * D:(n + 1) * 8 * D], zeros[:, :]).then_inc(slots_zeroed, 16)

            counts = Counts("sync", eng, per)

            def load_weights(e, n):
                w = ew[n]
                eng.dma_start(w[:, 0:HID], t["wg"][bass.ts(e, P), :]).then_inc(weights_in[n], 16)
                eng.dma_start(w[:, HID:2 * HID], t["wu"][bass.ts(e, P), :]).then_inc(weights_in[n], 16)
                eng.dma_start(w[:, 2 * HID:], t["wd"][bass.ts(e, P), :]).then_inc(weights_in[n], 16)

            def load_rows(e, n):
                eng.dma_start(ex_rows[n], t["slots"].rearrange("(p j) d -> p (j d)", j=SLOT_J)[bass.ts(e, SLOT_P), :])\
                   .then_inc(weights_in[n], 16)

            def store(e, n):
                eng.wait_ge(out_rows, counts.after(out_rows))
                eng.dma_start(t["results"].rearrange("(p j) d -> p (j d)", j=SLOT_J)[bass.ts(e, SLOT_P), :], ex_out[n])\
                   .then_inc(results_out[n], 16)

            eng.wait_ge(r_sb, 1)
            for n in range(RING):
                load_weights(n, n)
            for one in (slots_zeroed, scattered):
                eng.wait_ge(one, 16 * (E * CAP // P // 8 if one is slots_zeroed else NT * K))
            for n in range(RING):
                load_rows(n, n)
            with counts.loop((E - RING) // RING) as i:
                for n in range(RING):
                    eng.wait_ge(downed, counts.after(downed))
                    load_weights(i * RING + (RING + n), n)
                    load_rows(i * RING + (RING + n), n)
                    store(i * RING + n, n)
            for n in range(RING):
                store(E - RING + n, n)
            for q in range(NT // GROUP):
                eng.wait_ge(written, q + 1)
                rows = slice(q * GROUP * D, (q + 1) * GROUP * D)
                eng.dma_start(t["out"].rearrange("b (t p) d -> p (b t) d", p=P)[:, q * GROUP:(q + 1) * GROUP, :],
                              xb[:, rows].rearrange("p (n d) -> p n d", d=D)).then_inc(stored, 16)
            eng.wait_ge(stored, 16 * (NT // GROUP))

        @block.gpsimd
        def _(eng):
            counts = Counts("gpsimd", eng, per)
            eng.memset(half[:, :], -0.5).then_inc(consts, 1)
            eng.memset(eye[:, :], 0.0).then_inc(g_step, 1)
            eng.memset(causal_q[:, :], 0.0).then_inc(g_step, 1)
            eng.memset(causal_k[:, :], 0.0).then_inc(g_step, 1)
            eng.memset(window_k[:, :], 0.0).then_inc(g_step, 1)
            eng.memset(given_t[:, :], 0.0).then_inc(zeroed, 1)
            eng.wait_ge(g_step, counts.after(g_step, 4))
            eng.affine_select(out=eye[:, :], in_=eye[:, :], compare_op=ALU.not_equal, fill=1.0, base=0,
                              pattern=[[-1, P]], channel_multiplier=1).then_inc(g_step, 1)
            eng.affine_select(out=causal_q[:, :], in_=causal_q[:, :], compare_op=ALU.is_ge, fill=NEG, base=0,
                              pattern=[[-1, P]], channel_multiplier=1).then_inc(consts, 1)
            eng.affine_select(out=causal_k[:, :], in_=causal_k[:, :], compare_op=ALU.is_ge, fill=NEG, base=0,
                              pattern=[[1, P]], channel_multiplier=-1).then_inc(consts, 1)
            eng.affine_select(out=window_k[:, :], in_=window_k[:, :], compare_op=ALU.is_ge, fill=NEG, base=0,
                              pattern=[[1, P + WIN]], channel_multiplier=-1).then_inc(g_step, 1)
            eng.wait_ge(g_step, counts.after(g_step, 2))
            eng.affine_select(out=window_k[:, :], in_=window_k[:, :], compare_op=ALU.is_ge, fill=NEG, base=WIN - 1,
                              pattern=[[-1, P + WIN]], channel_multiplier=1).then_inc(consts, 1)
            eng.tensor_copy(eye_b[:, :], eye[:, :]).then_inc(consts, 1)
            eng.memset(zeros[:, :], 0.0).then_inc(zeroed, 1)
            for buf in (before, earlier, ones_b):
                eng.memset(buf[:, :], 1.0).then_inc(g_step, 1)
            eng.memset(half_up[:, :], 0.5).then_inc(g_step, 1)
            eng.iota(iota_i[:, :], pattern=[[1, E]], base=0, channel_multiplier=0).then_inc(g_step, 1)
            eng.wait_ge(g_step, counts.after(g_step, 5))
            eng.affine_select(out=before[:, :].rearrange("p (i j) -> p i j", j=G), in_=before[:, :].rearrange("p (i j) -> p i j", j=G),
                              compare_op=ALU.is_gt, fill=0.0, base=0, pattern=[[1, G], [-1, G]], channel_multiplier=0)\
               .then_inc(consts, 1)
            eng.affine_select(out=earlier[:, :], in_=earlier[:, :], compare_op=ALU.is_gt, fill=0.0, base=0,
                              pattern=[[1, P]], channel_multiplier=-1).then_inc(consts, 1)
            eng.tensor_copy(iota_e[:, :], iota_i[:, :]).then_inc(consts, 1)

            def power(dst, src, scale, eps, n):
                eng.wait_ge(pow_asked, counts.after(pow_asked))
                eng.sem_inc(waited, 1)
                eng.tensor_scalar(dst, src, scale, eps, ALU.mult, ALU.add).then_inc(g_step, 1)
                eng.wait_ge(g_step, counts.after(g_step))
                eng.tensor_tensor(dst, dst, half[:, 0:n], ALU.pow).then_inc(pow_done, 1)

            def norm(L, b, par, k):
                if L is WIDE:
                    power(wrs[:, :], wmv[:, 1:6:2], 1.0, 1e-5, 3)
                elif L.rms:
                    power(rs[:, :], ss[:, :], 1.0 / D, 1e-6, 2)

            def cut(L, b, par, k):
                if L.qk_norm:
                    power(nrs[:, :], nss[:, :], 1.0 / HD, 1e-6, 40)

            def output(L, b, par, k):
                if L in (MIXING, WIDE) or L.norm:
                    power(lrs[:, :], mv[:, 1:4:2], 1.0, 1e-5, 2)

            for L in layers:
                run_layer(L, counts, dict(norm=norm, cut=cut, output=output, mixed=output, wide_output=output))
            if not experts:
                return

            eng.wait_ge(pow_asked, counts.after(pow_asked))
            eng.tensor_tensor(cent_s[:, 1:2], cent_s[:, 0:1], half_up[0:G + E, 0:1], ALU.pow).then_inc(pow_done, 1)
            eng.wait_ge(pow_asked, counts.after(pow_asked))
            eng.tensor_tensor(small[:, NT:2 * NT], small[:, 0:NT], half_up[:, :], ALU.pow).then_inc(pow_done, 1)

            eng.wait_ge(slots_known, 1)
            eng.wait_ge(slots_zeroed, 16 * (E * CAP // P // 8))
            for tile in range(NT):
                for k in range(K):
                    eng.indirect_dma_start(t["slots"][:, :], bass.IndirectOffsetOnAxis(slot_in[:, tile * K + k:tile * K + k + 1], 0),
                                           xb[:, tile * D:(tile + 1) * D], None,
                                           bounds_check=E * CAP - 1, oob_is_err=False).then_inc(scattered, 16)
            for n in range(RING):
                eng.wait_ge(results_out[n], 16 * (E // RING))

            def gather(q):
                if q >= 2:
                    eng.wait_ge(combined, q - 1)
                for m in range(GROUP * K):
                    at = q * GROUP * K + m
                    eng.indirect_dma_start(gathered[q % 2][:, m * D:(m + 1) * D], None, t["results"][:, :],
                                           bass.IndirectOffsetOnAxis(slot_out[:, at:at + 1], 0),
                                           bounds_check=E * CAP - 1, oob_is_err=False).then_inc(gathered_in[q % 2], 16)

            gather(0)
            gather(1)
            for q in range(NT // GROUP):
                power(glrs[:, :], lmv[:, 1:2 * GROUP:2], 1.0, 1e-5, GROUP)
                if q + 2 < NT // GROUP:
                    gather(q + 2)

        @block.tensor
        def _(eng):
            counts = Counts("tensor", eng, per)
            eng.wait_ge(consts, 8)
            eng.wait_ge(loaded["early"], 32)
            eng.matmul(pre_ps[:, 0:2 * KVH * HD], down_t[:, :], ups[:, :], start=True, stop=True).then_inc(setup_ps, 1)
            eng.wait_ge(setup_sb, counts.after(setup_sb, 2))
            given_ps = turn_ps[:, :].bitcast(BF16)
            for half_ in range(2):
                if half_:
                    eng.wait_ge(setup_sb, counts.after(setup_sb))
                for n in range(8):
                    tile = half_ * 8 + n
                    last = eng.transpose(given_ps[0:C, n * P:(n + 1) * P], given[:, tile * C:(tile + 1) * C], eye_b[:, :])
                last.then_inc(setup_ps, 1)
            eng.wait_ge(zeroed, ZEROED + 1)

            def turn_x(L, b, par, k):
                if L is not WIDE or (isinstance(b, int) and b == 0):
                    eng.wait_ge(pre_read, counts.after(pre_read))
                eng.wait_ge(x_rows, counts.after(x_rows))
                for n in range(TILES):
                    last = eng.transpose(pre_ps[:, n * P:(n + 1) * P], xs[par][:, n * D:(n + 1) * D], eye[:, :])
                if L.cross:
                    last = eng.transpose(pre_ps[:, S:S + C], xc[:, :], eye[0:C, 0:C])
                last.then_inc(x_turned, 1)

            def project(L, b, par, k):
                w = weights[L.name]
                eng.wait_ge(xt_ready, counts.after(xt_ready))
                if L.cross:
                    for n in range(TILES):
                        eng.matmul(pre_ps[:, n * D:(n + 1) * D], xt[:, n * P:(n + 1) * P], w[:, 0:D], start=True, stop=True)
                    eng.matmul(pre_ps[0:C, 2 * D:4 * D], xt[:, S:S + C], w[:, D:3 * D], start=True, stop=True)\
                       .then_inc(projected, 1)
                elif L.kvh == H:
                    for n in range(TILES):
                        last = eng.matmul(pre_ps[:, n * 2 * D:(n + 1) * 2 * D], xt[:, n * P:(n + 1) * P], w[:, 0:2 * D],
                                          start=True, stop=True)
                    last.then_inc(projected, 1)
                    eng.wait_ge(pre_read, counts.after(pre_read))
                    for n in range(TILES):
                        last = eng.matmul(pre_ps[:, n * D:(n + 1) * D], xt[:, n * P:(n + 1) * P], w[:, 2 * D:3 * D],
                                          start=True, stop=True)
                    last.then_inc(projected, 1)
                else:
                    width = D + 2 * L.kn
                    for n in range(TILES):
                        last = eng.matmul(pre_ps[:, n * width:(n + 1) * width], xt[:, n * P:(n + 1) * P], w[:, :],
                                          start=True, stop=True)
                    last.then_inc(projected, 1)

            turn_b = turn_ps[:, :].bitcast(BF16)

            def turn_q(L, b, par, k):
                if k:
                    eng.wait_ge(shifted, counts.after(shifted))
                else:
                    eng.wait_ge(stacked, counts.after(stacked))
                for half_ in range(2):
                    if half_:
                        eng.wait_ge(operands, counts.after(operands))
                    elif k:
                        eng.wait_ge(turn_read, counts.after(turn_read))
                    for u in range(4 * half_, 4 * half_ + 4):
                        for n in range(TILES):
                            at = (n * H + place(u, 0)) * PART
                            rows = q_stack[:, at:at + P]
                            last = eng.transpose(turn_b[:, ((u % 4) * TILES + n) * P:((u % 4) * TILES + n + 1) * P],
                                                 rows, eye_b[:, :])
                    last.then_inc(turned, 1)

            def turn_k(L, b, par, k):
                n_k = L.keys
                per_bank = 8 if L.cross else 4
                for first in range(0, L.ktiles, per_bank):
                    eng.wait_ge(operands, counts.after(operands))
                    if L.cross:
                        eng.sem_inc(waited, 1)
                    for u in range(first, min(first + per_bank, L.ktiles)):
                        for n in range(L.key_tiles):
                            rows = (n * L.kvh + 2 * u) * PART
                            at = ((u - first) * L.key_tiles + n) * n_k
                            last = eng.transpose(turn_b[:, at:at + n_k],
                                                 k_stack[0:n_k, rows:rows + P],
                                                 eye_b[0:n_k, 0:n_k])
                    last.then_inc(turned, 1)

            def keys_of(L, par, u, side, rows, first, n):
                width = L.keys * L.key_tiles
                at = L.key_tile(u) * width + first
                return kt_[par][PART * side:PART * side + rows, at:at + n]

            def queries_of(par, u, side, rows, first, n):
                return qt[par][PART * side:PART * side + rows, u * S + first:u * S + first + n]

            def top(L, b, par, k):
                q, side, u0, m, n = L.top_steps[k]
                bank, full, free = ((pre_ps, top_a, pre_read), (turn_ps, top_b, turn_read))[k % 2]
                if k == 0:
                    eng.wait_ge(operands, counts.after(operands))
                if k != 1:
                    eng.wait_ge(free, counts.after(free))
                if L.cross:
                    eng.matmul(bank[:, 0:m * n].rearrange("p (m n) -> p m n", m=m), eye_b[:, :],
                               given[:, bass.ds(b * (TILES * C) + q * C, C)].unsqueeze(1).broadcast_to([P, m, C]),
                               start=True, stop=False, skip_group_check=True)
                else:
                    eng.matmul(bank[:, 0:m * n].rearrange("p (m n) -> p m n", m=m)[:, :, n - P:n], eye_b[:, :],
                               causal_q[:, :].unsqueeze(1).broadcast_to([P, m, P]),
                               start=True, stop=False, skip_group_check=True)
                for j in range(m):
                    last = eng.matmul(bank[:, j * n:(j + 1) * n], queries_of(par, u0 + j, side, ROWS, q * P, P),
                                      keys_of(L, par, u0 + j, side, ROWS, 0, n),
                                      start=False, stop=True, skip_group_check=True)
                last.then_inc(full, 1)

            def scores(L, b, par, k):
                g, kt, q0, q1 = L.steps[k]
                bank = score_ps[k % 2]
                rows = ROWS_MAX if L.top else ROWS
                if k == 0:
                    eng.wait_ge(operands, counts.after(operands))
                    counts.mark(probs_ready, ot_ready)
                if counts.owed(probs_ready, k - 1):
                    eng.wait_ge(probs_ready, counts.until(probs_ready, k - 1))
                n_k = L.keys
                for side in range(2):
                    if L.mask == "given":
                        width = S
                        mask = given_t[:, bass.ts(b, S)]
                    else:
                        width = q1 - q0 if L.mask == "window" else P
                        mask = (window_k if L.mask == "window" else causal_k)[:, 0:width]
                    eng.matmul(bank[0:n_k, side, :].rearrange("p (u q) -> p u q", u=2)[:, :, q0:q0 + width],
                               eye_b[:, 0:n_k], mask.unsqueeze(1).broadcast_to([P, 2, width]),
                               start=True, stop=False, skip_group_check=True)
                for side in range(2):
                    for uu in range(2):
                        u = 2 * g + uu
                        last = eng.matmul(bank[0:n_k, side, uu * S + q0:uu * S + q1],
                                          keys_of(L, par, u, side, rows, kt * P, n_k),
                                          queries_of(par, u, side, rows, q0, q1 - q0),
                                          start=False, stop=True, skip_group_check=True)
                last.then_inc(scored, 1)

            def values(L, b, par, k):
                if counts.owed(ot_ready, k - 1):
                    eng.wait_ge(ot_ready, counts.until(ot_ready, k - 1))
                if k == 1:
                    eng.wait_ge(post_read, counts.after(post_read))
                steps = [n for n, step in enumerate(L.steps) if step[0] == k]
                v = vals[par][0:L.keys, :].rearrange("p (t h c) -> p t h c", t=TILES, c=32)
                for n in steps:
                    g, kt, q0, q1 = L.steps[n]
                    if counts.owed(probs_ready, n + 1):
                        eng.wait_ge(probs_ready, counts.until(probs_ready, n + 1))
                        if L.cross:
                            eng.sem_inc(waited, 1)
                    for side in range(2):
                        for uu in range(2):
                            j = 2 * side + uu
                            h = L.value_head(2 * g + uu, side)
                            last = eng.matmul(sums_ps[k % 2][32 * j:32 * j + 32, q0:q1], v[:, kt, h, :],
                                              probs[n % PROBS][0:L.keys, j * S + q0:j * S + q1],
                                              start=(n == steps[0]), stop=(n == steps[-1]), skip_group_check=True)
                    last.then_inc(probs_free, 1)

            def merge(L, b, par, k):
                if counts.owed(ot_ready, 4):
                    eng.wait_ge(ot_ready, counts.until(ot_ready, 4))
                for pair in range(2):
                    if pair:
                        eng.wait_ge(merged, counts.after(merged))
                    for n in range(TILES):
                        for g in range(2):
                            at = (2 * n + g) * P
                            last = eng.transpose(post_ps[:, at:at + P],
                                                 ot[:, (2 * pair + g) * S + n * P:(2 * pair + g) * S + (n + 1) * P],
                                                 eye[:, :])
                    last.then_inc(rows_back, 1)

            def output(L, b, par, k):
                eng.wait_ge(merged, counts.after(merged))
                for n in range(TILES):
                    last = eng.transpose(post_ps[:, n * P:(n + 1) * P], on[:, n * D:(n + 1) * D], eye[:, :])
                last.then_inc(merged_turned, 1)
                eng.wait_ge(ont_ready, counts.after(ont_ready))
                for n in range(TILES):
                    last = eng.matmul(post_ps[:, n * D:(n + 1) * D], ont[:, n * P:(n + 1) * P], wo[L.name][:, :],
                                      start=True, stop=True)
                last.then_inc(out_projected, 1)

            def mixing_matrix():
                fr, fi, nfi, gr, ngi = (fourier[:, n * D:(n + 1) * D] for n in range(5))
                wr, wi = freq_w[:, 0:D], freq_w[:, D:2 * D]
                for n, (a, b_) in enumerate(((fr, nfi), (fi, fr))):
                    eng.matmul(out_ps[:, n * D:(n + 1) * D], wr, a, start=True, stop=False)
                    last = eng.matmul(out_ps[:, n * D:(n + 1) * D], wi, b_, start=False, stop=True)
                last.then_inc(setup_ps, 1)
                eng.wait_ge(setup_sb, counts.after(setup_sb))
                eng.matmul(out_ps[:, 0:D], freq_a[:, 0:D], gr, start=True, stop=False)
                eng.matmul(out_ps[:, 0:D], freq_a[:, D:2 * D], ngi, start=False, stop=True).then_inc(setup_ps, 1)
                eng.wait_ge(setup_sb, counts.after(setup_sb))

            def mix(L, b, par, k):
                eng.wait_ge(xt_ready, counts.after(xt_ready))
                for n in range(TILES):
                    last = eng.matmul(pre_ps[:, n * D:(n + 1) * D], xt[:, n * P:(n + 1) * P], mix_w[:, :], start=True, stop=True)
                last.then_inc(projected, 1)

            def wide_project(L, b, par, k):
                if k == 0:
                    eng.wait_ge(xt_ready, counts.after(xt_ready))
                if k % 2:
                    eng.wait_ge(wide_v, counts.after(wide_v))
                elif k:
                    eng.wait_ge(wide_a, counts.after(wide_a))
                what, c = L.products[k]
                if what == "q":
                    for n in range(2):
                        last = eng.matmul(turn_ps[:, n * S:(n + 1) * S], wide_q[:, (c + n) * P:(c + n + 1) * P], xt[:, 0:S],
                                          start=True, stop=True)
                elif what == "k":
                    last = eng.matmul(turn_ps[:, 0:WKEYS], wide_kv[:, c * P:(c + 1) * P], xt[:, :], start=True, stop=True)
                else:
                    first, n = KEY_TILES[c // 2]
                    at = WH * WD + (c % 2) * 512
                    last = eng.matmul(turn_ps[0:n, :], xt[:, first:first + n], wide_kv[:, at:at + 512], start=True, stop=True)
                last.then_inc(wide_made, 1)

            def wide_scores(L, b, par, k):
                c, rows = k // 2, slice(WD * (k % 2), WD * (k % 2) + WD)
                if k == 0:
                    eng.wait_ge(wide_a, counts.after(wide_a))
                    counts.mark(exped, turned_a, turned_c, pair_out)
                if counts.owed(exped, k - 1):
                    eng.wait_ge(exped, counts.until(exped, k - 1))
                for n in range(TILES):
                    last = eng.matmul(score_ps[k % 2][:, n, 0:WKEYS], wq_t[par][rows, c * S + n * P:c * S + (n + 1) * P],
                                      wk_t[par][rows, c * WKEYS:(c + 1) * WKEYS], start=True, stop=True)
                last.then_inc(wide_scored, 1)

            def wide_turn(L, b, par, k):
                eng.wait_ge(scaled, counts.after(scaled))
                if counts.owed(turned_a, k):
                    eng.wait_ge(turned_a, counts.until(turned_a, k))
                if k:
                    if counts.owed(turned_c, k):
                        eng.wait_ge(turned_c, counts.until(turned_c, k))
                else:
                    eng.wait_ge(post_read, counts.after(post_read))
                src = wprobs[k % WPROBS]
                for n, (first, m) in enumerate(KEY_TILES):
                    for q in range(TILES):
                        bank, at = (out_ps, n * S) if n < 2 else (post_ps, 0)
                        last = eng.transpose(bank[0:m, at + q * P:at + (q + 1) * P],
                                             src[:, q * WKEYS + first:q * WKEYS + first + m], eye[:, :])
                last.then_inc(probs_turned, 1)

            def wide_values(L, b, par, k):
                if counts.owed(turned_a, 2 * k + 2):
                    eng.wait_ge(turned_a, counts.until(turned_a, 2 * k + 2))
                if counts.owed(turned_c, 2 * k + 2):
                    eng.wait_ge(turned_c, counts.until(turned_c, 2 * k + 2))
                if counts.owed(pair_out, k):
                    eng.wait_ge(pair_out, counts.until(pair_out, k))
                for n, (first, m) in enumerate(KEY_TILES):
                    for side in range(2):
                        h = 2 * k + side
                        last = eng.matmul(pre_ps[WD * side:WD * side + WD, 0:S],
                                          wv[par][0:m, n * WH * WD + h * WD:n * WH * WD + (h + 1) * WD],
                                          wturned[h % WTURNED][0:m, n * S:(n + 1) * S],
                                          start=(n == 0), stop=(n == len(KEY_TILES) - 1), skip_group_check=True)
                last.then_inc(pair_summed, 1)

            def wide_output(L, b, par, k):
                if counts.owed(pair_out, CHUNKS):
                    eng.wait_ge(pair_out, counts.until(pair_out, CHUNKS))
                for n in range(TILES):
                    for c in range(CHUNKS):
                        last = eng.matmul(post_ps[:, n * D:(n + 1) * D], wout_t[:, c * S + n * P:c * S + (n + 1) * P],
                                          wide_o[:, c * D:(c + 1) * D], start=(c == 0), stop=(c == CHUNKS - 1))
                last.then_inc(out_projected, 1)

            for L in layers:
                eng.wait_ge(loaded["x_" if L.name == "x" else L.name], loads_of(L))
                if L is MIXING:
                    mixing_matrix()
                run_layer(L, counts, dict(turn_x=turn_x, project=project, turn_q=turn_q, turn_k=turn_k, top=top,
                                          scores=scores, values=values, merge=merge, output=output, mix=mix,
                                          wide_project=wide_project, wide_scores=wide_scores, wide_turn=wide_turn,
                                          wide_values=wide_values, wide_output=wide_output))
            if not experts:
                return

            eng.wait_ge(exp_loaded, 16 * 6)
            eng.wait_ge(r_sb, counts.after(r_sb))
            eng.transpose(out_ps[:, 0:G + E], centroids[:, :], eye[0:G + E, 0:G + E]).then_inc(r_ps, 1)
            for q in range(NT // 4):
                bank = (pre_ps, turn_ps)[q % 2]
                if q >= 2:
                    eng.wait_ge(r_sb, counts.after(r_sb))
                for m in range(4):
                    tile = 4 * q + m
                    last = eng.transpose(bank[:, m * P:(m + 1) * P], xb[:, tile * D:(tile + 1) * D], eye[:, :])
                last.then_inc(r_ps, 1)
            eng.wait_ge(r_sb, counts.after(r_sb, 2))
            for tile in range(NT):
                last = eng.matmul(score_ps[0][:, tile // 8, (tile % 8) * (G + E):(tile % 8 + 1) * (G + E)],
                                  xt_all[:, tile * P:(tile + 1) * P], cent_t[:, :], start=True, stop=True)
            last.then_inc(r_ps, 1)

            def shared(q):
                for part in range(2):
                    for c in range(2):
                        last = eng.matmul(score_ps[part][:, c, :], shared_w[:, part * HID + c:(part + 1) * HID:2],
                                          xt_all[:, q * 512:(q + 1) * 512], start=True, stop=True)
                    last.then_inc(sh_made, 1)
                eng.wait_ge(sh_gated, counts.after(sh_gated))
                bank = (pre_ps, turn_ps)[q % 2]
                for m in range(4):
                    for c in range(2):
                        last = eng.matmul(bank[:, m * P:(m + 1) * P], sh_hid[:, c * 512 + m * P:c * 512 + (m + 1) * P],
                                          shared_w[:, 2 * HID + c * D:2 * HID + (c + 1) * D], start=(c == 0), stop=(c == 1))
                last.then_inc(sh_made, 1)

            eng.wait_ge(r_sb, counts.after(r_sb, 2))
            eng.matmul(out_ps[:, :], earlier[:, :], chosen, start=True, stop=True)
            eng.matmul(post_ps[:, :], ones_b[:, :], chosen, start=True, stop=True).then_inc(r_ps, 1)
            for q in range(NT // 4):
                if q >= 2:
                    eng.wait_ge(sh_summed, counts.after(sh_summed))
                shared(q)
            eng.wait_ge(sh_summed, counts.after(sh_summed, 2))

            def turn_rows(n):
                eng.wait_ge(weights_in[n], turn_rows.arrived)
                for j in range(SLOT_J):
                    last = eng.transpose(turn_ps[:, j * SLOT_P:(j + 1) * SLOT_P], ex_rows[n][:, j * P:(j + 1) * P],
                                         eye[0:SLOT_P, 0:SLOT_P])
                last.then_inc(rows_turned, 1)

            def up(bank, part, n, full):
                w = ew[n][:, part * HID:(part + 1) * HID]
                for c in range(2):
                    last = eng.matmul(bank[:, c, 0:CAP], w[:, c::2], ex_t[n % 2], start=True, stop=True)
                last.then_inc(full, 1)

            def down(n):
                if copied[0]:
                    eng.wait_ge(out_rows, counts.after(out_rows))
                copied[0] = True
                for j in range(SLOT_J):
                    for c in range(2):
                        last = eng.matmul(pre_ps[0:SLOT_P, j * D:(j + 1) * D],
                                          ex_h[n % 2][:, c * CAP + j * SLOT_P:c * CAP + (j + 1) * SLOT_P],
                                          ew[n][:, 2 * HID + c * D:2 * HID + (c + 1) * D], start=(c == 0), stop=(c == 1))
                last.then_inc(downed, 1)

            def step(n, round_, first=False, last=False):
                eng.wait_ge(rows_copied, counts.after(rows_copied))
                if not first:
                    eng.wait_ge(silued, counts.after(silued))
                up(score_ps[0], 0, n, gate_made)
                if not first:
                    eng.wait_ge(gated, counts.after(gated))
                up(score_ps[1], 1, n, up_made)
                if not first:
                    down((n - 1) % RING)
                if not last:
                    turn_rows.arrived = round_(n + 1)
                    turn_rows((n + 1) % RING)

            copied = [False]
            turn_rows.arrived = 64
            turn_rows(0)
            once = lambda m: 64 * (1 + m // RING)
            step(0, once, first=True)
            for n in range(1, RING):
                step(n, once)
            with counts.loop(E // RING - 2) as i:
                for n in range(RING):
                    step(n, lambda m: i * 64 + 64 * (2 + m // RING))
            for n in range(RING):
                step(n, lambda m: 64 * (E // RING), last=(n == RING - 1))
            eng.wait_ge(gated, counts.after(gated))
            down(RING - 1)

        @block.scalar
        def _(eng):
            counts = Counts("scalar", eng, per)

            def turn_x(L, b, par, k):
                eng.wait_ge(x_turned, counts.after(x_turned))
                n = S + C if L.cross else S
                if L is WIDE:
                    eng.activation(xt[:, 0:S], pre_ps[:, 0:S], ACT.Identity, scale=ln_wb[:, 0:1], bias=ln_wb[:, 1:2])
                    ins = eng.activation(xt[:, S:n], pre_ps[:, S:n], ACT.Identity, scale=ln_wb[:, 2:3], bias=ln_wb[:, 3:4])
                elif L.rms:
                    ins = eng.activation(xt[:, 0:n], pre_ps[:, 0:n], ACT.Copy, scale=norm_w[L.name][:, 0:1])
                else:
                    ins = eng.activation(xt[:, 0:n], pre_ps[:, 0:n], ACT.Copy)
                ins.then_inc(xt_ready, 1)

            def copy_turned(dst, n):
                eng.wait_ge(turned, counts.after(turned))
                ins = eng.activation(dst, turn_ps[:, :].bitcast(BF16)[:, 0:n], ACT.Copy)
                ins.then_inc(operands, 1)

            def turn_q(L, b, par, k):
                for half_ in range(2):
                    copy_turned(qt[par][:, half_ * 4 * S:(half_ + 1) * 4 * S], 4 * S)

            def turn_k(L, b, par, k):
                n = L.ktiles * L.keys * L.key_tiles
                for first in range(0, n, 4 * S):
                    m = min(n - first, 4 * S)
                    copy_turned(kt_[par][:, first:first + m], m)

            def scores(L, b, par, k):
                g, kt, q0, q1 = L.steps[k]
                eng.wait_ge(scored, counts.after(scored))
                eng.wait_ge(probs_free, counts.after(probs_free))
                src = score_ps[k % 2][0:L.keys, :, :].rearrange("p s (u q) -> p (s u) q", u=2)[:, :, q0:q1]
                dst = probs[k % PROBS][0:L.keys, :].rearrange("p (j q) -> p j q", q=S)[:, :, q0:q1]
                eng.activation(dst, src, ACT.Exp, scale=SCALE).then_inc(probs_ready, 1)

            def output(L, b, par, k):
                eng.wait_ge(merged_turned, counts.after(merged_turned))
                eng.activation(ont[:, :], post_ps[:, 0:TILES * D], ACT.Copy).then_inc(ont_ready, 1)

            def wide_project(L, b, par, k):
                if k % 2:
                    eng.wait_ge(wide_made, counts.after(wide_made, 2))
                    dst, src, scale = wide_copy(L, par, k)
                    eng.activation(dst, src, ACT.Copy, scale=scale).then_inc(wide_a, 1)

            def wide_scores(L, b, par, k):
                eng.wait_ge(topped, counts.after(topped))
                dst = wprobs[k % WPROBS]
                for n in range(TILES):
                    at = 2 * (k % WPROBS) + n
                    last = eng.activation(dst[:, n * WKEYS:(n + 1) * WKEYS], score_ps[k % 2][:, n, 0:WKEYS], ACT.Exp,
                                          bias=wtop[:, at:at + 1], accum_out=wden[:, at:at + 1])
                last.then_inc(exped, 1)

            def wide_turn(L, b, par, k):
                eng.wait_ge(probs_turned, counts.after(probs_turned))
                eng.activation(wturned[k % WTURNED][:, 0:2 * S], out_ps[:, :], ACT.Copy).then_inc(turned_a, 1)

            def wide_values(L, b, par, k):
                eng.wait_ge(pair_summed, counts.after(pair_summed))
                eng.activation(wout_t[:, k * S:(k + 1) * S], pre_ps[:, 0:S], ACT.Copy).then_inc(pair_out, 1)

            for n, L in enumerate(layers):
                if L.rms or L is WIDE:
                    eng.wait_ge(loaded[L.name], loads_of(L))
                run_layer(L, counts, dict(turn_x=turn_x, turn_q=turn_q, turn_k=turn_k, scores=scores, output=output,
                                          wide_project=wide_project, wide_scores=wide_scores, wide_turn=wide_turn,
                                          wide_values=wide_values))
            if not experts:
                return

            eng.wait_ge(exps_asked, 1)
            eng.activation(gates, gates, ACT.Exp).then_inc(exps_made, 1)
            for q in range(NT // 4):
                eng.wait_ge(sh_made, counts.after(sh_made))
                if q:
                    eng.wait_ge(sh_gated, q)
                eng.activation(sh_gate.rearrange("p (c n) -> p c n", c=2), score_ps[0][:, :, :], ACT.Silu).then_inc(sh_silu, 1)
                eng.wait_ge(sh_made, counts.after(sh_made, 2))

            def activate(m):
                eng.wait_ge(gate_made, counts.after(gate_made))
                eng.activation(ex_g[m % 2].rearrange("p (c n) -> p c n", c=2), score_ps[0][:, :, 0:CAP], ACT.Silu)\
                   .then_inc(silued, 1)

            def copy_out(n, value):
                eng.wait_ge(downed, counts.after(downed))
                if value is not None:
                    eng.wait_ge(results_out[n], value)
                eng.activation(ex_out[n], pre_ps[0:SLOT_P, :], ACT.Copy).then_inc(out_rows, 1)

            activate(0)
            for n in range(1, RING):
                activate(n)
                copy_out(n - 1, None)
            activate(0)
            copy_out(RING - 1, None)
            for n in range(1, RING):
                activate(n)
                copy_out(n - 1, 16)
            with counts.loop(E // RING - 2) as i:
                for n in range(RING):
                    activate(n)
                    copy_out((n - 1) % RING, i * 16 + (32 if n else 16))
            copy_out(RING - 1, 16 * (E // RING - 1))

        @block.vector
        def _(eng):
            counts = Counts("vector", eng, per)

            for buf in (stack_words, vals_all, qk, wmv):
                eng.memset(buf[:, :], 0.0).then_inc(v_step, 1)
                eng.wait_ge(v_step, counts.after(v_step))
            eng.memset(k_stack[:, :].rearrange("p (n s) -> p n s", s=PART)[:, :, ROWS:ROWS_MAX], 1.0).then_inc(zeroed, 1)
            for n in range(2):
                eng.memset(vals[n][:, :].rearrange("p (n c) -> p n c", c=32)[:, :, HD:HD + 1], 1.0).then_inc(zeroed, 1)
            eng.wait_ge(setup_ps, counts.after(setup_ps))
            eng.tensor_copy(weights["g"][:, D:D + 2 * KVH * HD], pre_ps[:, 0:2 * KVH * HD]).then_inc(setup_sb, 1)
            eng.wait_ge(loaded["mask"], 16)
            eng.tensor_scalar(given[:, :], given8[:, :], -NEG, NEG, ALU.mult, ALU.add).then_inc(setup_sb, 1)
            eng.wait_ge(zeroed, 4)
            for half_ in range(2):
                eng.wait_ge(setup_ps, counts.after(setup_ps))
                ins = eng.tensor_copy(given_t[0:C, half_ * 8 * P:(half_ + 1) * 8 * P], turn_ps[:, :].bitcast(BF16)[0:C, :])
                ins.then_inc(setup_sb if half_ == 0 else zeroed, 1)

            def norm(L, b, par, k):
                src = rows_of(x0 if L.name == "g" else xb, b)
                if L is WIDE:
                    tiles = [(src[:, 0:D], xs[par][:, 0:D], P), (src[:, D:2 * D], xs[par][:, D:2 * D], P),
                             (ctx_all[:, bass.ts(b, D)], xc[:, :], C)]
                    for n, (a, _, m) in enumerate(tiles):
                        eng.bn_stats(wstats[0:m, 6 * n:6 * n + 6], a).then_inc(v_step, 1)
                        counts.moved(v_step)
                    eng.wait_ge(v_step, counts.after(v_step, 0))
                    eng.sem_inc(waited, 1)
                    for n, (_, _, m) in enumerate(tiles):
                        eng.bn_aggr(wmv[0:m, 2 * n:2 * n + 2], wstats[0:m, 6 * n:6 * n + 6]).then_inc(v_step if n < 2 else pow_asked, 1)
                        counts.moved(v_step if n < 2 else pow_asked)
                    eng.wait_ge(v_step, counts.after(v_step, 0))
                    eng.wait_ge(pow_done, counts.after(pow_done))
                    for n, (a, dst, m) in enumerate(tiles):
                        eng.tensor_scalar(dst, a, wmv[0:m, 2 * n:2 * n + 1], wrs[0:m, n:n + 1],
                                          ALU.subtract, ALU.mult).then_inc(v_step if n < 2 else x_rows, 1)
                        counts.moved(v_step if n < 2 else x_rows)
                    eng.wait_ge(v_step, counts.after(v_step, 0))
                    return
                if L.cross:
                    eng.tensor_copy(xc[:, :], ctx_all[:, bass.ts(b, D)]).then_inc(v_step, 1)
                    eng.wait_ge(v_step, counts.after(v_step))
                if not L.rms:
                    eng.tensor_copy(xs[par][:, :], src).then_inc(x_rows, 1)
                    return
                eng.tensor_tensor(sq[:, :], src, src, ALU.mult).then_inc(v_step, 1)
                eng.wait_ge(v_step, counts.after(v_step))
                eng.tensor_reduce(ss[:, :], sq[:, :].rearrange("p (t d) -> p t d", d=D), AX_X, ALU.add).then_inc(pow_asked, 1)
                eng.wait_ge(pow_done, counts.after(pow_done))
                eng.tensor_tensor(xs[par][:, :].rearrange("p (t d) -> p t d", d=D), src.rearrange("p (t d) -> p t d", d=D),
                                  rs[:, :].unsqueeze(2).broadcast_to([P, TILES, D]), ALU.mult).then_inc(x_rows, 1)

            def project(L, b, par, k):
                eng.wait_ge(projected, counts.after(projected))
                v = vals[par][0:L.keys, :].rearrange("p (t h c) -> p t h c", t=TILES, c=32)
                q_dst = qk[:, 0:TILES * D].rearrange("p (t d) -> p t d", d=D)
                k_dst = qk[:, TILES * D:L.flat].rearrange("p (t d) -> p t d", d=L.kn)
                if L.cross:
                    bi = bias_in[L.name]
                    eng.tensor_tensor(q_dst, pre_ps[:, 0:TILES * D].rearrange("p (t d) -> p t d", d=D),
                                      bi[:, 0:D].unsqueeze(1).broadcast_to([P, TILES, D]), ALU.add)
                    eng.tensor_tensor(qk[0:C, TILES * D:L.flat], pre_ps[0:C, 2 * D:3 * D], bi[0:C, D:2 * D], ALU.add)
                    ins = eng.tensor_tensor(v[:, 0, :, 0:HD], pre_ps[0:C, 3 * D:4 * D].rearrange("p (h c) -> p h c", c=HD),
                                            bi[0:C, 2 * D:3 * D].rearrange("p (h c) -> p h c", c=HD), ALU.add)
                elif L.kvh == H:
                    bi = bias_in[L.name]
                    src = pre_ps[:, :].rearrange("p (t d) -> p t d", d=2 * D)
                    eng.tensor_tensor(q_dst, src[:, :, 0:D], bi[:, 0:D].unsqueeze(1).broadcast_to([P, TILES, D]), ALU.add)
                    eng.tensor_tensor(k_dst, src[:, :, D:2 * D],
                                      bi[:, D:2 * D].unsqueeze(1).broadcast_to([P, TILES, D]), ALU.add).then_inc(pre_read, 1)
                    counts.moved(pre_read)
                    eng.wait_ge(projected, counts.after(projected))
                    for n in range(TILES):
                        ins = eng.tensor_tensor(v[:, n, :, 0:HD],
                                                pre_ps[:, n * D:(n + 1) * D].rearrange("p (h c) -> p h c", c=HD),
                                                bi[:, 2 * D:3 * D].rearrange("p (h c) -> p h c", c=HD), ALU.add)
                else:
                    src = pre_ps[:, 0:TILES * (D + 2 * L.kn)].rearrange("p (t d) -> p t d", t=TILES)
                    eng.tensor_copy(q_dst, src[:, :, 0:D])
                    eng.tensor_copy(k_dst, src[:, :, D:D + L.kn])
                    ins = eng.tensor_copy(v[:, :, 0:L.kvh, 0:HD],
                                          src[:, :, D + L.kn:].rearrange("p t (h c) -> p t h c", c=HD))
                ins.then_inc(pre_read, 1)
                counts.moved(pre_read)
                eng.wait_ge(pre_read, counts.after(pre_read, 0))

            def cut(L, b, par, k):
                n = L.flat
                src = qk[:, 0:n]
                if L.rope:
                    pairs = src.rearrange("p (n two) -> p n two", two=2)
                    eng.tensor_tensor(qk2[:, 0:n], src, cos[L.name][:, :], ALU.mult).then_inc(v_step, 1)
                    counts.moved(v_step)
                    eng.tensor_tensor(qk3[:, 0:n].rearrange("p (n two) -> p n two", two=2), pairs[:, :, ::-1],
                                      sin[L.name][:, :].rearrange("p (n two) -> p n two", two=2), ALU.mult).then_inc(v_step, 1)
                    eng.wait_ge(v_step, counts.after(v_step))
                    eng.tensor_tensor(src, qk2[:, 0:n], qk3[:, 0:n], ALU.add).then_inc(v_step, 1)
                    eng.wait_ge(v_step, counts.after(v_step))
                if L.qk_norm:
                    m = n // HD
                    eng.tensor_tensor(qk2[:, 0:n], src, src, ALU.mult).then_inc(v_step, 1)
                    eng.wait_ge(v_step, counts.after(v_step))
                    eng.tensor_reduce(nss[:, 0:m], qk2[:, 0:n].rearrange("p (n c) -> p n c", c=HD), AX_X, ALU.add)\
                       .then_inc(pow_asked, 1)
                    eng.wait_ge(pow_done, counts.after(pow_done))
                    eng.tensor_tensor(src.rearrange("p (n c) -> p n c", c=HD), src.rearrange("p (n c) -> p n c", c=HD),
                                      nrs[:, 0:m].unsqueeze(2).broadcast_to([P, m, HD]), ALU.mult).then_inc(v_step, 1)
                    eng.wait_ge(v_step, counts.after(v_step))
                eng.tensor_copy(cuts[0][:, 0:n], src).then_inc(v_step, 1)
                eng.wait_ge(v_step, counts.after(v_step))
                eng.tensor_tensor(qk2[:, 0:n], src, cuts[0][:, 0:n], ALU.subtract).then_inc(v_step, 1)
                eng.wait_ge(v_step, counts.after(v_step))
                eng.tensor_copy(cuts[1][:, 0:n], qk2[:, 0:n]).then_inc(v_step, 1)
                eng.wait_ge(v_step, counts.after(v_step))
                eng.tensor_tensor(cuts[2][:, 0:n], qk2[:, 0:n], cuts[1][:, 0:n], ALU.subtract).then_inc(v_step, 1)
                eng.wait_ge(v_step, counts.after(v_step))
                q_slots = (slice(0, 3), slice(3, 6, 2), slice(4, 5))
                k_slots = (slice(2, 5), slice(0, 6, 5), slice(1, 2))
                for stack, slots, first, m in ((q_stack, q_slots, 0, TILES * H),
                                               (k_stack, k_slots, TILES * D, L.key_tiles * L.kvh)):
                    dst = stack[:, 0:m * PART].rearrange("p (n s c) -> p n s c", s=PART // HD, c=HD)
                    for part in range(3):
                        out = dst[:, :, slots[part], :]
                        ins = eng.tensor_copy(out, cuts[part][:, first:first + m * HD].rearrange("p (n c) -> p n c", c=HD)
                                              .unsqueeze(2).broadcast_to([P, m, out.shape[2], HD]))
                ins.then_inc(stacked, 1)
                counts.moved(stacked)
                eng.wait_ge(stacked, counts.after(stacked, 0))

            def top(L, b, par, k):
                q, side, u0, m, n = L.top_steps[k]
                bank, full, read = ((pre_ps, top_a, pre_read), (turn_ps, top_b, turn_read))[k % 2]
                eng.wait_ge(full, counts.after(full))
                dst = tops[:, q * H:(q + 1) * H].rearrange("p (u s) -> p u s", s=2)[:, u0:u0 + m, side]
                src = bank[:, 0:m * n].rearrange("p (m n) -> p m n", n=n)
                eng.tensor_reduce(dst, src, AX_X, ALU.max).then_inc(read, 1)
                counts.moved(read)

            def shift(L, b, par, k):
                eng.wait_ge(pre_read, counts.after(pre_read, 0))
                eng.wait_ge(turn_read, counts.after(turn_read, 0))
                slot = q_stack[:, :].rearrange("p (n s) -> p n s", s=PART)
                one = [slot[:, :, ROWS + n] for n in range(3)]
                eng.tensor_scalar(tops[:, :], tops[:, :], -1.0, None, ALU.mult).then_inc(v_step, 1)
                eng.wait_ge(v_step, counts.after(v_step))
                eng.tensor_copy(one[0], tops[:, :]).then_inc(v_step, 1)
                eng.wait_ge(v_step, counts.after(v_step))
                eng.tensor_tensor(top2[:, :], tops[:, :], one[0], ALU.subtract).then_inc(v_step, 1)
                eng.wait_ge(v_step, counts.after(v_step))
                eng.tensor_copy(one[1], top2[:, :]).then_inc(v_step, 1)
                eng.wait_ge(v_step, counts.after(v_step))
                ins = eng.tensor_tensor(one[2], top2[:, :], one[1], ALU.subtract)
                ins.then_inc(shifted, 1)
                counts.moved(shifted)
                eng.wait_ge(shifted, counts.after(shifted, 0))

            def values(L, b, par, k):
                eng.wait_ge(probs_free, counts.after(probs_free, len(L.steps) // 4))
                eng.tensor_copy(ot[:, k * S:(k + 1) * S], sums_ps[k % 2][:, 0:S]).then_inc(ot_ready, 1)

            def merge(L, b, par, k):
                for pair in range(2):
                    eng.wait_ge(rows_back, counts.after(rows_back))
                    src = post_ps[:, :].rearrange("p (n c) -> p n c", c=32)
                    eng.reciprocal(rden[:, :].unsqueeze(2), src[:, :, HD:HD + 1]).then_inc(v_step, 1)
                    eng.wait_ge(v_step, counts.after(v_step))
                    dst = on[:, :].rearrange("p (t g n c) -> p t g n c", t=TILES, g=2, c=HD)[:, :, pair, :, :]
                    ins = eng.tensor_tensor(dst, src[:, :, 0:HD].rearrange("p (t n) c -> p t n c", t=TILES),
                                            rden[:, :].rearrange("p (t n) -> p t n", t=TILES).unsqueeze(3)
                                            .broadcast_to([P, TILES, 8, HD]), ALU.mult)
                    ins.then_inc(merged, 1)
                    counts.moved(merged)
                    eng.wait_ge(merged, counts.after(merged, 0))

            def layer_norm(dst, src, last):
                for n in range(TILES):
                    eng.bn_stats(stats[:, 6 * n:6 * n + 6], src[:, n * D:(n + 1) * D]).then_inc(v_step, 1)
                    counts.moved(v_step)
                eng.wait_ge(v_step, counts.after(v_step, 0))
                eng.sem_inc(waited, 1)
                for n in range(TILES):
                    eng.bn_aggr(mv[:, 2 * n:2 * n + 2], stats[:, 6 * n:6 * n + 6]).then_inc(pow_asked if n else v_step, 1)
                    counts.moved(pow_asked if n else v_step)
                eng.wait_ge(v_step, counts.after(v_step, 0))
                eng.wait_ge(pow_done, counts.after(pow_done))
                for n in range(TILES):
                    ins = eng.tensor_scalar(dst[:, n * D:(n + 1) * D], src[:, n * D:(n + 1) * D], mv[:, 2 * n:2 * n + 1],
                                            lrs[:, n:n + 1], ALU.subtract, ALU.mult)
                    ins.then_inc(v_step, 1)
                    counts.moved(v_step)
                eng.wait_ge(v_step, counts.after(v_step, 0))

            def output(L, b, par, k):
                eng.wait_ge(out_projected, counts.after(out_projected))
                src = rows_of(x0 if L.name == "g" else xb, b)
                acc = post_ps[:, 0:TILES * D]
                if L.name == "g":
                    eng.tensor_tensor(rows_of(xb, b), acc, src, ALU.add).then_inc(post_read, 1)
                    counts.moved(post_read)
                    eng.wait_ge(post_read, counts.after(post_read, 0))
                    return
                eng.tensor_tensor(y[:, :], acc, src, ALU.add).then_inc(post_read, 1)
                counts.moved(post_read)
                eng.wait_ge(post_read, counts.after(post_read, 0))
                if L.name == "l":
                    eng.tensor_tensor(y[:, :], y[:, :], rows_of(x0, b), ALU.add).then_inc(v_step, 1)
                    eng.wait_ge(v_step, counts.after(v_step))
                else:
                    eng.tensor_tensor(y[:, :].rearrange("p (t d) -> p t d", d=D), y[:, :].rearrange("p (t d) -> p t d", d=D),
                                      bias_out[L.name][:, :].unsqueeze(1).broadcast_to([P, TILES, D]), ALU.add).then_inc(v_step, 1)
                    eng.wait_ge(v_step, counts.after(v_step))
                layer_norm(rows_of(xb, b), y[:, :], None)

            def mixed(L, b, par, k):
                eng.wait_ge(projected, counts.after(projected))
                eng.tensor_tensor(y[:, :], pre_ps[:, 0:TILES * D], rows_of(xb, b), ALU.add).then_inc(pre_read, 1)
                counts.moved(pre_read)
                eng.wait_ge(pre_read, counts.after(pre_read, 0))
                eng.tensor_tensor(y[:, :].rearrange("p (t d) -> p t d", d=D), y[:, :].rearrange("p (t d) -> p t d", d=D),
                                  bias_mix[:, :].unsqueeze(1).broadcast_to([P, TILES, D]), ALU.add).then_inc(v_step, 1)
                eng.wait_ge(v_step, counts.after(v_step))
                layer_norm(rows_of(xb, b), y[:, :], None)

            def wide_project(L, b, par, k):
                if k % 2 == 0:
                    eng.wait_ge(wide_made, counts.after(wide_made, 2 if k else 1))
                    dst, src, scale = wide_copy(L, par, k)
                    eng.tensor_scalar(dst, src, scale, None, ALU.mult).then_inc(wide_v, 1)
                    if k == len(L.products) - 2:
                        eng.wait_ge(wide_made, counts.after(wide_made))

            def wide_scores(L, b, par, k):
                eng.wait_ge(wide_scored, counts.after(wide_scored))
                at = 2 * (k % WPROBS)
                eng.tensor_reduce(wtop[:, at:at + 2], score_ps[k % 2][:, :, 0:WKEYS], AX_X, ALU.max, negate=True)\
                   .then_inc(topped, 1)

            def wide_turn(L, b, par, k):
                eng.wait_ge(exped, counts.after(exped))
                at = 2 * (k % WPROBS)
                eng.reciprocal(wrden[:, at:at + 2], wden[:, at:at + 2]).then_inc(v_step, 1)
                eng.wait_ge(v_step, counts.after(v_step))
                for n in range(TILES):
                    src = wprobs[k % WPROBS][:, n * WKEYS:(n + 1) * WKEYS]
                    last = eng.tensor_scalar(src, src, wrden[:, at + n:at + n + 1], None, ALU.mult)
                last.then_inc(scaled, 1)
                eng.wait_ge(probs_turned, counts.after(probs_turned))
                eng.tensor_copy(wturned[k % WTURNED][0:C, 2 * S:3 * S], post_ps[0:C, 0:S]).then_inc(turned_c, 1)

            def wide_output(L, b, par, k):
                eng.wait_ge(out_projected, counts.after(out_projected))
                eng.tensor_tensor(y[:, :], post_ps[:, 0:TILES * D], rows_of(xb, b), ALU.add).then_inc(post_read, 1)
                counts.moved(post_read)
                eng.wait_ge(post_read, counts.after(post_read, 0))
                layer_norm(rows_of(xb, b), y[:, :], None)

            def release(L, b, par, k):
                eng.wait_ge(operands, counts.after(operands, 2 + max(1, L.ktiles * L.keys * L.key_tiles // (4 * S)) + 2 * L.top))

            eng.sem_inc(probs_free, PROBS)
            counts.moved(probs_free, PROBS)
            for first in (pre_read, post_read):
                eng.sem_inc(first, 1)
                counts.moved(first)
            eng.wait_ge(loaded["x"], 16)
            eng.wait_ge(loaded["ctx"], 16)
            for n, L in enumerate(layers):
                eng.wait_ge(loaded["x_" if L.name == "x" else L.name], loads_of(L))
                if L is MIXING:
                    eng.wait_ge(setup_ps, counts.after(setup_ps))
                    eng.tensor_copy(freq_a[:, :], out_ps[:, 0:2 * D]).then_inc(setup_sb, 1)
                    eng.wait_ge(setup_ps, counts.after(setup_ps))
                    eng.tensor_copy(mix_w[:, :], out_ps[:, 0:D]).then_inc(setup_sb, 1)
                run_layer(L, counts, dict(norm=norm, project=project, cut=cut, top=top, shift=shift, values=values,
                                          merge=merge, output=output, release=release, mixed=mixed,
                                          wide_project=wide_project, wide_scores=wide_scores, wide_turn=wide_turn,
                                          wide_output=wide_output))
            if not experts:
                eng.tensor_copy(rden[:, 0:1], rden[:, 0:1]).then_inc(stored, 1)
                return

            eng.wait_ge(exp_loaded, 16 * 6)
            eng.tensor_tensor(cent_sq[:, :], centroids[:, :], centroids[:, :], ALU.mult).then_inc(v_step, 1)
            eng.wait_ge(v_step, counts.after(v_step))
            eng.tensor_reduce(cent_s[:, 0:1], cent_sq[:, :], AX_X, ALU.add).then_inc(pow_asked, 1)
            counts.moved(pow_asked)
            eng.wait_ge(pow_done, counts.after(pow_done))
            eng.tensor_scalar(cent_s[:, 2:3], cent_s[:, 1:2], 1e-12, None, ALU.max).then_inc(v_step, 1)
            eng.wait_ge(v_step, counts.after(v_step))
            eng.reciprocal(cent_s[:, 3:4], cent_s[:, 2:3]).then_inc(v_step, 1)
            eng.wait_ge(v_step, counts.after(v_step))
            eng.tensor_scalar(centroids[:, :], centroids[:, :], cent_s[:, 3:4], None, ALU.mult).then_inc(r_sb, 1)
            counts.moved(r_sb)
            tokens = xb[:, :].rearrange("p (t d) -> p t d", d=D)
            eng.tensor_tensor(acc, xb[:, :], xb[:, :], ALU.mult).then_inc(v_step, 1)
            eng.wait_ge(v_step, counts.after(v_step))
            eng.tensor_reduce(small[:, 0:NT], acc.rearrange("p (t d) -> p t d", d=D), AX_X, ALU.add).then_inc(pow_asked, 1)
            counts.moved(pow_asked)
            eng.wait_ge(r_ps, counts.after(r_ps))
            eng.tensor_copy(cent_t[:, :], out_ps[:, 0:G + E]).then_inc(v_step, 1)
            eng.wait_ge(v_step, counts.after(v_step))
            for q in range(NT // 4):
                eng.wait_ge(r_ps, counts.after(r_ps))
                eng.tensor_copy(xt_all[:, q * 512:(q + 1) * 512], (pre_ps, turn_ps)[q % 2][:, :]).then_inc(r_sb, 1)
                counts.moved(r_sb)
            eng.wait_ge(pow_done, counts.after(pow_done))
            eng.tensor_scalar(small[:, 2 * NT:3 * NT], small[:, NT:2 * NT], 1e-12, None, ALU.max).then_inc(v_step, 1)
            eng.wait_ge(v_step, counts.after(v_step))
            eng.reciprocal(small[:, 3 * NT:4 * NT], small[:, 2 * NT:3 * NT]).then_inc(v_step, 1)
            eng.wait_ge(v_step, counts.after(v_step))
            inverse = small[:, 3 * NT:4 * NT]
            eng.wait_ge(r_ps, counts.after(r_ps))
            for half_ in range(2):
                src = score_ps[0][:, half_, 0:8 * (G + E)].rearrange("p (t n) -> p t n", n=G + E)
                inv = inverse[:, half_ * 8:half_ * 8 + 8].unsqueeze(2)
                eng.tensor_tensor(g_score[:, half_ * 8 * G:(half_ + 1) * 8 * G].rearrange("p (t n) -> p t n", n=G),
                                  src[:, :, 0:G], inv.broadcast_to([P, 8, G]), ALU.mult)
                last = eng.tensor_tensor(e_score[:, half_ * 8 * E:(half_ + 1) * 8 * E].rearrange("p (t n) -> p t n", n=E),
                                         src[:, :, G:], inv.broadcast_to([P, 8, E]), ALU.mult)
            last.then_inc(r_sb, 1)
            counts.moved(r_sb)
            eng.wait_ge(r_sb, counts.after(r_sb, 0))
            by_tile = e_score.rearrange("p (t n) -> p t n", n=E)
            eng.tensor_tensor(by_tile, by_tile, choice_bias[:, :].unsqueeze(1).broadcast_to([P, NT, E]), ALU.add).then_inc(v_step, 1)
            counts.moved(v_step)
            other = g_score.rearrange("p (t j) -> p t j", j=G).unsqueeze(2).broadcast_to([P, NT, G, G])
            own = g_score.rearrange("p (t i) -> p t i", i=G).unsqueeze(3).broadcast_to([P, NT, G, G])
            gt4, eq4 = (m.rearrange("p (t i j) -> p t i j", i=G, j=G) for m in (cmp_gt, cmp_eq))
            eng.tensor_tensor(gt4, other, own, ALU.is_gt).then_inc(v_step, 1)
            counts.moved(v_step)
            eng.tensor_tensor(eq4, other, own, ALU.is_equal).then_inc(v_step, 1)
            eng.wait_ge(v_step, counts.after(v_step))
            eng.tensor_tensor(cmp_eq.rearrange("p (t n) -> p t n", n=G * G), cmp_eq.rearrange("p (t n) -> p t n", n=G * G),
                              before[:, :].unsqueeze(1).broadcast_to([P, NT, G * G]), ALU.mult).then_inc(v_step, 1)
            eng.wait_ge(v_step, counts.after(v_step))
            eng.tensor_tensor(cmp_gt, cmp_gt, cmp_eq, ALU.add).then_inc(v_step, 1)
            eng.wait_ge(v_step, counts.after(v_step))
            eng.tensor_reduce(rank, cmp_gt.rearrange("p (n j) -> p n j", j=G), AX_X, ALU.add).then_inc(v_step, 1)
            eng.wait_ge(v_step, counts.after(v_step))
            eng.tensor_scalar(rank, rank, float(G // 2), None, ALU.is_lt).then_inc(v_step, 1)
            eng.wait_ge(v_step, counts.after(v_step))
            per_group = [P, NT * G, E // G]
            eng.tensor_tensor(e_score.rearrange("p (n m) -> p n m", m=E // G), e_score.rearrange("p (n m) -> p n m", m=E // G),
                              rank.unsqueeze(2).broadcast_to(per_group), ALU.mult).then_inc(v_step, 1)
            eng.wait_ge(v_step, counts.after(v_step))
            eng.tensor_scalar(rank, rank, 1e9, -1e9, ALU.mult, ALU.add).then_inc(v_step, 1)
            eng.wait_ge(v_step, counts.after(v_step))
            eng.tensor_tensor(masked.rearrange("p (n m) -> p n m", m=E // G), e_score.rearrange("p (n m) -> p n m", m=E // G),
                              rank.unsqueeze(2).broadcast_to(per_group), ALU.add).then_inc(v_step, 1)
            eng.wait_ge(v_step, counts.after(v_step))
            for tile in range(NT):
                last = eng.max(top8[:, tile * 8:(tile + 1) * 8], masked[:, tile * E:(tile + 1) * E])
            last.then_inc(v_step, 1)
            eng.wait_ge(v_step, counts.after(v_step))
            for tile in range(NT):
                last = eng.max_index(idx8.bitcast(U32)[:, tile * 8:(tile + 1) * 8], top8[:, tile * 8:(tile + 1) * 8],
                                     masked[:, tile * E:(tile + 1) * E])
            last.then_inc(v_step, 1)
            eng.wait_ge(v_step, counts.after(v_step))
            top4 = top8.rearrange("p (t n) -> p t n", n=8)
            by_k = gates.rearrange("p (t k) -> p t k", k=K)
            eng.tensor_tensor(by_k, top4[:, :, 0:K], top4[:, :, 0:1].broadcast_to([P, NT, K]), ALU.subtract).then_inc(exps_asked, 1)
            counts.moved(exps_asked)
            eng.tensor_copy(idx_f.rearrange("p (t k) -> p t k", k=K),
                            idx8.bitcast(U32).rearrange("p (t n) -> p t n", n=8)[:, :, 0:K]).then_inc(v_step, 1)
            eng.wait_ge(v_step, counts.after(v_step))
            eng.tensor_tensor(onehot.rearrange("p (n e) -> p n e", e=E), iota_e[:, :].unsqueeze(1).broadcast_to([P, NT * K, E]),
                              idx_f.unsqueeze(2).broadcast_to([P, NT * K, E]), ALU.is_equal).then_inc(v_step, 1)
            eng.wait_ge(v_step, counts.after(v_step))
            with nc.allow_low_precision(reason="sums of at most one are exact"):
                eng.tensor_reduce(chosen.rearrange("p (t e) -> p t e", e=E),
                                  onehot.rearrange("p (t k e) -> p t e k", k=K, e=E), AX_X, ALU.add).then_inc(r_sb, 1)
                counts.moved(r_sb)
            eng.wait_ge(exps_made, counts.after(exps_made))
            eng.tensor_reduce(small[:, 4 * NT:5 * NT], by_k, AX_X, ALU.add).then_inc(v_step, 1)
            eng.wait_ge(v_step, counts.after(v_step))
            eng.reciprocal(small[:, 4 * NT:5 * NT], small[:, 4 * NT:5 * NT]).then_inc(v_step, 1)
            eng.wait_ge(v_step, counts.after(v_step))
            eng.tensor_tensor(by_k, by_k, small[:, 4 * NT:5 * NT].unsqueeze(2).broadcast_to([P, NT, K]), ALU.mult).then_inc(v_step, 1)
            eng.wait_ge(v_step, counts.after(v_step))
            eng.wait_ge(r_ps, counts.after(r_ps))
            eng.memset(ahead[:, 0:E], 0.0).then_inc(v_step, 1)
            eng.wait_ge(v_step, counts.after(v_step))
            eng.tensor_copy(ahead[:, E:], post_ps[:, 0:(NT - 1) * E]).then_inc(v_step, 1)
            eng.wait_ge(v_step, counts.after(v_step))
            a, c = ahead, ahead2
            for shift_ in (1, 2, 4, 8):
                eng.tensor_copy(c[:, 0:shift_ * E], a[:, 0:shift_ * E]).then_inc(v_step, 1)
                counts.moved(v_step)
                eng.tensor_tensor(c[:, shift_ * E:], a[:, shift_ * E:], a[:, 0:(NT - shift_) * E], ALU.add).then_inc(v_step, 1)
                eng.wait_ge(v_step, counts.after(v_step))
                a, c = c, a
            eng.tensor_tensor(totals, a, out_ps[:, :], ALU.add).then_inc(v_step, 1)
            eng.wait_ge(v_step, counts.after(v_step))
            for tile in range(NT):
                span = slice(tile * K * E, (tile + 1) * K * E)
                last = eng.tensor_tensor(picked[:, span].rearrange("p (k e) -> p k e", k=K),
                                         onehot[:, span].rearrange("p (k e) -> p k e", k=K),
                                         totals[:, tile * E:(tile + 1) * E].unsqueeze(1).broadcast_to([P, K, E]), ALU.mult)
            last.then_inc(v_step, 1)
            eng.wait_ge(v_step, counts.after(v_step))
            eng.tensor_reduce(pos, picked.rearrange("p (n e) -> p n e", e=E), AX_X, ALU.add).then_inc(v_step, 1)
            eng.wait_ge(v_step, counts.after(v_step))
            eng.tensor_scalar(keep, pos, float(CAP), None, ALU.is_lt).then_inc(v_step, 1)
            eng.wait_ge(v_step, counts.after(v_step))
            eng.tensor_tensor(gate[:, :], gates, keep, ALU.mult).then_inc(v_step, 1)
            counts.moved(v_step)
            eng.tensor_scalar(keep, keep, -BEYOND, BEYOND, ALU.mult, ALU.add).then_inc(v_step, 1)
            eng.wait_ge(v_step, counts.after(v_step))
            eng.tensor_scalar(idx_f, idx_f, float(CAP), None, ALU.mult).then_inc(v_step, 1)
            eng.wait_ge(v_step, counts.after(v_step))
            eng.tensor_tensor(keep, keep, pos, ALU.add).then_inc(v_step, 1)
            eng.wait_ge(v_step, counts.after(v_step))
            eng.tensor_tensor(slot_in[:, :], keep, idx_f, ALU.add).then_inc(v_step, 1)
            eng.wait_ge(v_step, counts.after(v_step))
            eng.tensor_scalar(pos, pos, float(CAP - 1), None, ALU.min).then_inc(v_step, 1)
            eng.wait_ge(v_step, counts.after(v_step))
            eng.tensor_tensor(slot_out[:, :], pos, idx_f, ALU.add).then_inc(slots_known, 1)

            for q in range(NT // 4):
                eng.wait_ge(sh_made, counts.after(sh_made, 2))
                eng.wait_ge(sh_silu, q + 1)
                eng.tensor_tensor(sh_hid.rearrange("p (c n) -> p c n", c=2), sh_gate.rearrange("p (c n) -> p c n", c=2),
                                  score_ps[1][:, :, :], ALU.mult).then_inc(sh_gated, 1)
                counts.moved(sh_gated)
                eng.wait_ge(sh_made, counts.after(sh_made))
                eng.tensor_tensor(acc[:, q * 512:(q + 1) * 512], (pre_ps, turn_ps)[q % 2][:, :],
                                  xb[:, q * 512:(q + 1) * 512], ALU.add).then_inc(sh_summed, 1)
                counts.moved(sh_summed)
            eng.wait_ge(sh_summed, counts.after(sh_summed, 0))

            def copy_rows(n):
                eng.wait_ge(rows_turned, counts.after(rows_turned))
                eng.tensor_copy(ex_t[n % 2], turn_ps[:, 0:CAP]).then_inc(rows_copied, 1)

            def multiply(n):
                eng.wait_ge(silued, counts.after(silued))
                eng.wait_ge(up_made, counts.after(up_made))
                eng.tensor_tensor(ex_h[n % 2].rearrange("p (c n) -> p c n", c=2), ex_g[n % 2].rearrange("p (c n) -> p c n", c=2),
                                  score_ps[1][:, :, 0:CAP], ALU.mult).then_inc(gated, 1)

            copy_rows(0)
            with counts.loop((E - 2) // 2) as i:
                for n in range(2):
                    multiply(n)
                    copy_rows(n + 1)
            multiply(0)
            copy_rows(1)
            multiply(1)

            for q in range(NT // GROUP):
                eng.wait_ge(gathered_in[q % 2], 16 * GROUP * K * (q // 2 + 1))
                for k in range(K):
                    for m in range(GROUP):
                        tile = q * GROUP + m
                        at = acc[:, tile * D:(tile + 1) * D]
                        last = eng.scalar_tensor_tensor(out=at, in0=gathered[q % 2][:, (m * K + k) * D:(m * K + k + 1) * D],
                                                        scalar=gate[:, tile * K + k:tile * K + k + 1], in1=at,
                                                        op0=ALU.mult, op1=ALU.add)
                        if m == GROUP - 1:
                            last.then_inc(combined if k == K - 1 else v_step, 1)
                            counts.moved(combined if k == K - 1 else v_step)
                    eng.wait_ge(combined if k == K - 1 else v_step, counts.after(combined if k == K - 1 else v_step, 0))
                for m in range(GROUP):
                    tile = q * GROUP + m
                    last = eng.bn_stats(lstats[:, 6 * m:6 * m + 6], acc[:, tile * D:(tile + 1) * D])
                last.then_inc(v_step, 1)
                eng.wait_ge(v_step, counts.after(v_step))
                for m in range(GROUP):
                    last = eng.bn_aggr(lmv[:, 2 * m:2 * m + 2], lstats[:, 6 * m:6 * m + 6])
                last.then_inc(pow_asked, 1)
                counts.moved(pow_asked)
                eng.wait_ge(pow_asked, counts.after(pow_asked, 0))
                eng.wait_ge(pow_done, counts.after(pow_done))
                for m in range(GROUP):
                    tile = slice((q * GROUP + m) * D, (q * GROUP + m + 1) * D)
                    last = eng.tensor_scalar(xb[:, tile], acc[:, tile], lmv[:, 2 * m:2 * m + 1], glrs[:, m:m + 1],
                                             ALU.subtract, ALU.mult)
                last.then_inc(written, 1)


def loads_of(L):
    if L is MIXING:
        return 16 * 8
    if L is WIDE:
        return 16 * 4
    return 16 * ((2 + 2 * L.rope + 2 * L.bias) + L.rms)


def rope_tables(L, base):
    dim = np.arange(HD // 2, dtype=np.float32)
    pos = np.arange(S, dtype=np.float32)[:, None]
    if L.name == "a":
        angle = pos / np.exp(np.float32(2.0) * dim / np.float32(HD) * np.float32(np.log(10000.0)))[None, :]
    else:
        inv = np.float32(1.0) / np.float32(base) ** (np.arange(0, HD, 2, dtype=np.float32) / np.float32(HD))
        angle = pos * inv[None, :]
    angle = angle.astype(np.float32)
    c, s = np.cos(angle), np.sin(angle)
    c2 = np.repeat(c, 2, axis=1)
    s2 = np.stack([-s, s], axis=-1).reshape(S, HD)

    def lay(table):
        q = np.tile(table.reshape(TILES, P, 1, HD), (1, 1, H, 1)).transpose(1, 0, 2, 3).reshape(P, -1)
        k = np.tile(table.reshape(TILES, P, 1, HD), (1, 1, L.kvh, 1)).transpose(1, 0, 2, 3).reshape(P, -1)
        return np.ascontiguousarray(np.concatenate([q, k], axis=1).astype(np.float32))
    return lay(c2), lay(s2)


def merged_rows(w, kv_heads=H):
    return w.reshape(H, HD, D)[[held_heads(kv_heads)[n] for n in MERGED]].reshape(D, D)


def held_columns(w):
    return w.reshape(D, H, HD)[:, held_heads(KVH)].reshape(D, D)


def layout(i):
    cat = np.concatenate
    a = {"x": i["x"], "ctx": i["ctx_1024"], "mask": i["mask_Bx1xSxS2_bf1"].reshape(B, S, C).view(np.uint8),
         "down_t": i["L0_attn_g_kv_down"].T, "ups": cat([i["L0_attn_g_k_up"], i["L0_attn_g_v_up"]], axis=1),
         "w_g": held_columns(i["L0_attn_g_wq"]), "wo_g": merged_rows(i["L0_attn_g_wo"], KVH), "nw_g": i["L0_attn_norm1_w"][:, None],
         "w_l": cat([held_columns(i["L0_attn_l_wq"]), i["L0_attn_l_wk"], i["L0_attn_l_wv"]], axis=1),
         "wo_l": merged_rows(i["L0_attn_l_wo"], KVH), "nw_l": i["L0_attn_norm2_w"][:, None]}
    for name, p, (q, k, v, o) in (("x", "L0_xattn_", ("Wq", "Wk", "Wv", "Wo")), ("a", "L1_attn_", ("wq", "wk", "wv", "wo"))):
        a[f"w_{name}"] = cat([i[p + q].T, i[p + k].T, i[p + v].T], axis=1)
        a[f"wo_{name}"] = merged_rows(i[p + o].T)
        a[f"bi_{name}"] = np.tile(cat([i[p + "bq"], i[p + "bk"], i[p + "bv"]])[None], (P, 1))
        a[f"bo_{name}"] = np.tile(i[p + "bo"][None], (P, 1))
    for L, base in ((NARROW[0], 1e6), (NARROW[1], 1e4), (NARROW[3], 1e4)):
        a[f"cos_{L.name}"], a[f"sin_{L.name}"] = rope_tables(L, base)
    wave = 2.0 * np.pi * (np.outer(np.arange(D), np.arange(D)) % D) / D
    a.update(Fr=np.cos(wave).astype(np.float32), Fi=-np.sin(wave).astype(np.float32), nFi=np.sin(wave).astype(np.float32),
             Gr=(np.cos(wave) / D).astype(np.float32), nGi=-(np.sin(wave) / D).astype(np.float32),
             freq_r=i["L0_ffn_w_freq_real"], freq_i=i["L0_ffn_w_freq_imag"],
             bias_mix=np.tile(i["L0_ffn_bias"][None], (P, 1)),
             wide_q=i["L1_xattn_Wq"], wide_kv=i["L1_xattn_Wkv"], wide_o=i["L1_xattn_Wo"],
             group_c=i["L1_ffn_group_centroids"], expert_c=i["L1_ffn_expert_centroids"],
             choice_bias=np.tile(i["L1_ffn_bias"][None], (P, 1)), sg=i["L1_ffn_sg"], su=i["L1_ffn_su"], sd=i["L1_ffn_sd"],
             wg=i["L1_ffn_wg"].reshape(E * D, HID), wu=i["L1_ffn_wu"].reshape(E * D, HID),
             wd=i["L1_ffn_wd"].reshape(E * P, 2 * D),
             ln_wb=np.stack([i["L1_xattn_ln2_w"], i["L1_xattn_ln2_b"], i["L1_xattn_ln1_w"], i["L1_xattn_ln1_b"]], axis=1))
    return {n: np.ascontiguousarray(v) for n, v in a.items()}


def make_program(nc, arrays, per):
    t = {n: nc.dram_tensor(n, a.shape, mybir.dt.from_np(a.dtype), kind="ExternalInput").ap() for n, a in arrays.items()}
    t["out"] = nc.dram_tensor("out", (B, S, D), F32, kind="ExternalOutput").ap()
    t["slots"] = nc.dram_tensor("slots", (E * CAP, D), F32, kind="Internal").ap()
    t["results"] = nc.dram_tensor("results", (E * CAP, D), F32, kind="Internal").ap()
    build_program(nc, t, per)


def kernel(**inputs):
    import concourse.bacc as bacc
    from concourse.bass_utils import run_bass_kernel_spmd

    arrays = layout({n: np.asarray(a) for n, a in inputs.items()})
    per = {}
    make_program(bacc.Bacc("TRN2", target_bir_lowering=False, num_devices=1), arrays, per)
    nc = bacc.Bacc("TRN2", target_bir_lowering=False, num_devices=1)
    make_program(nc, arrays, per)
    result = run_bass_kernel_spmd(nc, [arrays], core_ids=[0])
    return result.results[0]["out"]
```

```python
from contextlib import ExitStack, contextmanager

import numpy as np

import concourse.bass as bass
from concourse import mybir

ALU = mybir.AluOpType
ACT = mybir.ActivationFunctionType
AX_X = mybir.AxisListType.X
F32 = mybir.dt.float32
BF16 = mybir.dt.bfloat16
I32 = mybir.dt.int32
U32 = mybir.dt.uint32
U8 = mybir.dt.uint8

B, S, D = 8, 256, 128
P = 128
TILES = S // P
C = 64
H, HD = 16, 8
KVH = 4
WIN = 32
PART = 64
ROWS, ROWS_MAX = 6 * HD, 6 * HD + 3
NEG = -1e30
SCALE = 1.0 / float(np.sqrt(HD))


class Counts:

    def __init__(self, name, engine, per):
        self.name, self.engine, self.per = name, engine, per
        self.seen, self.base, self.at, self.loops = {}, {}, None, 0

    def after(self, sem, events=1):
        self.moved(sem, events)
        value = self.seen[sem.name]
        if self.at is not None:
            value = value + self.at * self.per.get((self.name, self.loops, sem.name), 0)
        return value

    def moved(self, sem, events=1):
        self.seen[sem.name] = self.seen.get(sem.name, 0) + events

    def layer(self, events):
        self.events = {sem.name: n for sem, n in events}
        for name, n in self.events.items():
            self.base[name, 1] = self.seen.get(name, 0) - n

    def batch(self, par, *sems):
        for sem in sems:
            self.base[sem.name, par] = self.base[sem.name, 1 - par] + self.events[sem.name]

    def owed(self, sem, par, event):
        return self.base[sem.name, par] + event > self.seen.get(sem.name, 0)

    def until(self, sem, par, event):
        return self.after(sem, self.base[sem.name, par] + event - self.seen.get(sem.name, 0))

    @contextmanager
    def loop(self, count):
        self.loops += 1
        before, base = dict(self.seen), dict(self.base)
        with self.engine.Fori(0, count) as i:
            self.at = i
            yield i
        self.at = None
        for name, value in self.seen.items():
            n = value - before.get(name, 0)
            self.per[(self.name, self.loops, name)] = n
            self.seen[name] = value + n * (count - 1)
        for name, value in self.base.items():
            self.base[name] = value + (value - base.get(name, value)) * (count - 1)


def place(u, side):
    return 2 * u + side


def held_heads(kv_heads):
    if kv_heads == H:
        return list(range(H))
    return [(u // 4) * 8 + side * 4 + u % 4 for u in range(8) for side in range(2)]


MERGED = [place(2 * g + uu, side) for g in range(4) for side in range(2) for uu in range(2)]


class Narrow:

    def __init__(self, name, kv_heads, *, rms=False, rope=False, qk_norm=False, cross=False, bias=False,
                 top=False, mask="causal", norm=True):
        self.name, self.kvh = name, kv_heads
        self.rms, self.rope, self.qk_norm, self.cross = rms, rope, qk_norm, cross
        self.bias, self.top, self.mask, self.norm = bias, top, mask, norm
        self.kn = kv_heads * HD
        self.key_tiles = 1 if cross else TILES
        self.keys = C if cross else P
        self.flat = TILES * D + self.key_tiles * self.kn
        self.ktiles = kv_heads // 2
        self.turns = 2 + max(1, self.ktiles * self.keys * self.key_tiles // (4 * S)) + 2 * top
        spans = {"causal": [(0, 0, S), (1, P, S)], "window": [(0, 0, P + WIN), (1, P, S)], "given": [(0, 0, S)]}[mask]
        self.steps = [(g, kt, q0, q1) for g in range(4) for kt, q0, q1 in spans]
        self.last_kt = spans[-1][0]
        self.top_steps = []
        if top:
            for t in range(TILES):
                n = C if cross else P * (t + 1)
                m = 512 // n
                self.top_steps += [(t, side, u, m, n) for u in range(0, 8, m) for side in range(2)]

    def value_head(self, u, side):
        return place(u, side) if self.kvh == H else 2 * (u // 4) + side

    def key_tile(self, u):
        return u if self.kvh == H else u // 4


class Mixing:

    name, rms, cross = "f", False, False


WH, WD = 16, 64
CHUNKS = WH * WD // P
WKEYS = S + C
KEY_TILES = [(0, P), (P, P), (S, C)]


class Wide:

    name, rms, cross = "w", False, True
    products = ([("q", c) for c in range(0, CHUNKS, 2)] + [("k", c) for c in range(CHUNKS)]
                + [("v", n) for n in range(2 * len(KEY_TILES))])


E, G, K = 32, 8, 4
HID = 256
N = B * S
NT = N // P
CAP = int(N / E * K * 1.25)
SLOT_P, SLOT_J = 80, CAP // 80
RING = 4
BEYOND = float(2 * E * CAP)
GROUP = 4

NARROW = [
    Narrow("g", KVH, rms=True, rope=True, qk_norm=True, norm=False),
    Narrow("l", KVH, rms=True, rope=True, qk_norm=True, mask="window"),
    Narrow("x", H, cross=True, bias=True, top=True, mask="given"),
    Narrow("a", H, rope=True, bias=True, top=True),
]
MIXING, WIDE = Mixing(), Wide()
LAYERS = NARROW[:3] + [MIXING, NARROW[3], WIDE]


def schedule(layer):
    if layer is MIXING:
        return [("core", "mix", 0), ("pre", "norm", 0), ("pre", "normed", 0), ("core", "mixed", 0), ("core", "finished", 0), ("pre", "turn_x", 0)]
    if layer is WIDE:
        out = []
        n = len(layer.products)
        for h in range(WH):
            if h == 2:
                out.append(("pre", "wide_project", 0))
            out.append(("core", "wide_scores", h))
            if h == 1:
                out.append(("pre", "turn_x", 0))
            phase, past = ("core", h) if h >= 2 else ("late", h + WH)
            out.append((phase, "wide_turn", past - 2))
            out.append(("core", "wide_exp", h))
            out.append(("core" if h else "late", "wide_scale", (h - 1) % WH))
            phase, past = ("core", h) if h >= 4 else ("late", h + WH)
            if past % 2 == 0:
                out.append((phase, "wide_values", (past - 4) // 2))
            if h == 0:
                out.append(("pre", "norm", 0))
                out.append(("pre", "normed", 0))
            if h == 3:
                out.append(("late", "wide_output", 0))
            if h == 4:
                out.append(("late", "finished", 0))
            if h >= 3:
                out += [("pre", "wide_project", k) for k in range(1 + (n - 1) * (h - 3) // (WH - 3), 1 + (n - 1) * (h - 2) // (WH - 3))]
        return out
    per = len(layer.steps) // 4

    def scores(g):
        return [("core", "scores", k) for k in range(per * g, per * g + per)]

    if layer.top:
        tops = [("pre", "top", k) for k in range(len(layer.top_steps))]
        between = [scores(2), [("core", "values", 1)] + scores(3), [("core", "values", 2)], [("core", "values", 3)]]
        n = len(tops) // 4
        filled = sum((between[m] + tops[n * m:n * (m + 1)] for m in range(4)), [])
        return ([("far", "norm", 0), ("far", "normed", 0)] + scores(0)
                + [("pre", "project_v", 0), ("far", "turn_x", 0), ("pre", "cut", 3)] + scores(1)
                + [("pre", "turn_q", 0), ("far", "project", 0), ("pre", "turn_q", 1), ("far", "cut", 0)]
                + [("core", "values", 0), ("pre", "turn_k", 0), ("far", "cut", 1), ("far", "cut", 2)] + filled
                + [("pre", "shift", 0), ("core", "merge", 0), ("pre", "turn_q", 2), ("core", "merge", 1), ("pre", "turn_q", 3)]
                + [("core", "output", 0), ("core", "finished", 0)])
    return ([("far", "norm", 0)] + scores(0) + [("pre", "project_v", 0), ("far", "normed", 0)] + scores(1)
            + [("far", "turn_x", 0), ("core", "values", 0), ("far", "project", 0), ("far", "cut", 0)] + scores(2)
            + [("core", "values", 1), ("pre", "cut", 3), ("core", "merge", 0)] + scores(3)
            + [("pre", "turn_q", 0), ("core", "values", 2), ("pre", "turn_q", 1)]
            + [("core", "values", 3), ("pre", "turn_k", 0), ("core", "merge", 1), ("far", "cut", 1), ("core", "output", 0)]
            + [("far", "cut", 2), ("core", "finished", 0)])


def run_layer(layer, counts, pieces):
    order = schedule(layer)

    def batch(**at):
        for phase, name, k in order:
            if phase in at and name in pieces:
                b, par = at[phase]
                pieces[name](layer, b, par, k)

    if layer in (MIXING, WIDE):
        batch(pre=(0, 0))
        batch(core=(0, 0), pre=(1, 1))
        with counts.loop(B // 2 - 1) as i:
            batch(late=(i * 2, 0), core=(i * 2 + 1, 1), pre=(i * 2 + 2, 0))
            batch(late=(i * 2 + 1, 1), core=(i * 2 + 2, 0), pre=(i * 2 + 3, 1))
        batch(late=(B - 2, 0), core=(B - 1, 1))
        batch(late=(B - 1, 1))
        return
    batch(far=(0, 0))
    batch(pre=(0, 0), far=(1, 1))
    with counts.loop(B // 2 - 1) as i:
        batch(core=(i * 2, 0), pre=(i * 2 + 1, 1), far=(i * 2 + 2, 0))
        batch(core=(i * 2 + 1, 1), pre=(i * 2 + 2, 0), far=(i * 2 + 3, 1))
    batch(core=(B - 2, 0), pre=(B - 1, 1))
    batch(core=(B - 1, 1))


ZEROED = 5


def build_program(nc, t, per, stop=None):
    layers = LAYERS[:stop] if stop else LAYERS
    experts = not stop
    ctx = ExitStack()
    with ctx:
        def sb(name, shape, dt=F32):
            return ctx.enter_context(nc.sbuf_tensor("s_" + name, shape, dt))

        def ps(name, shape, dt=F32):
            return ctx.enter_context(nc.psum_tensor("p_" + name, shape, dt))

        def sem(name):
            return ctx.enter_context(nc.semaphore(name))

        x0 = sb("x0", [P, B * TILES * D])
        xb = sb("xb", [P, B * TILES * D])
        ctx_all = sb("ctx_all", [C, B * D])
        weights = {L.name: sb(f"w_{L.name}", [P, D + 2 * L.kn]) for L in NARROW}
        wo = {L.name: sb(f"wo_{L.name}", [P, D]) for L in NARROW}
        norm_w = {L.name: sb(f"nw_{L.name}", [P, 1]) for L in NARROW if L.rms}
        cos = {L.name: sb(f"cos_{L.name}", [P, L.flat]) for L in NARROW if L.rope}
        sin = {L.name: sb(f"sin_{L.name}", [P, L.flat]) for L in NARROW if L.rope}
        bias_in = {L.name: sb(f"bi_{L.name}", [P, 3 * D]) for L in NARROW if L.bias}
        bias_out = {L.name: sb(f"bo_{L.name}", [P, D]) for L in NARROW if L.bias}
        down_t = sb("down_t", [32, P])
        ups = sb("ups", [32, 2 * KVH * HD])
        given8 = sb("given8", [P, B * TILES * C], U8)
        given = sb("given", [P, B * TILES * C], BF16)
        given_t = sb("given_t", [P, B * S], BF16)
        eye = sb("eye", [P, P])
        eye_b = sb("eye_b", [P, P], BF16)
        causal_q = sb("causal_q", [P, P], BF16)
        causal_k = sb("causal_k", [P, P], BF16)
        window_k = sb("window_k", [P, P + WIN], BF16)

        xs = [sb(f"xs{n}", [P, S]) for n in range(2)]
        xc = sb("xc", [C, D])
        xt = sb("xt", [P, S + C])
        flat_max = 4 * D
        qk = sb("qk", [P, flat_max])
        qk2 = sb("qk2", [P, flat_max])
        qk3 = sb("qk3", [P, flat_max])
        cuts = [sb(f"cut{n}", [P, flat_max], BF16) for n in range(3)]
        stack_words = sb("stack_words", [P, TILES * H * PART])
        stacks = stack_words[:, :].bitcast(BF16)
        q_stack, k_stack = (stacks[:, n * TILES * H * PART:(n + 1) * TILES * H * PART] for n in range(2))
        turned_words = sb("turned_words", [P, 16 * S])
        turned_b = turned_words[:, :].bitcast(BF16)
        qt = [turned_b[:, n * 8 * S:(n + 1) * 8 * S] for n in range(2)]
        kt_ = [turned_b[:, (2 + n) * 8 * S:(3 + n) * 8 * S] for n in range(2)]
        vals_all = sb("vals_all", [P, 2 * TILES * H * 32])
        vals = [vals_all[:, n * TILES * H * 32:(n + 1) * TILES * H * 32] for n in range(2)]
        PROBS = 4
        probs_all = sb("probs_all", [P, PROBS * 4 * S])
        probs = [probs_all[:, n * 4 * S:(n + 1) * 4 * S] for n in range(PROBS)]
        ot = sb("ot", [P, 4 * S])
        rden = sb("rden", [P, 16])
        on = sb("on", [P, TILES * D])
        ont = sb("ont", [P, TILES * D])
        y = sb("y", [P, TILES * D])
        sq = sb("sq", [P, TILES * D])
        ss = sb("ss", [P, 2])
        rs = sb("rs", [P, 2])
        nss = sb("nss", [P, 40])
        nrs = sb("nrs", [P, 40])
        stats = sb("stats", [P, 2 * 6])
        mv = sb("mv", [P, 4])
        lrs = sb("lrs", [P, 2])
        half = sb("half", [P, 40])
        tops = sb("tops", [P, TILES * H])
        top2 = sb("top2", [P, TILES * H])

        fourier = sb("fourier", [P, 5 * D])
        freq_w = sb("freq_w", [P, 2 * D])
        freq_a = sb("freq_a", [P, 2 * D])
        mix_w = sb("mix_w", [P, D])
        bias_mix = sb("bias_mix", [P, D])

        wide_q = sb("wide_q", [P, WH * WD])
        wide_kv = sb("wide_kv", [P, 2 * WH * WD])
        wide_o = sb("wide_o", [P, CHUNKS * D])
        ln_wb = sb("ln_wb", [P, 4])
        wq_t = [probs_all[:, n * CHUNKS * S:(n + 1) * CHUNKS * S] for n in range(2)]
        wk_t = [sb(f"wk_t{n}", [P, CHUNKS * WKEYS]) for n in range(2)]
        wv = [sb(f"wv{n}", [P, len(KEY_TILES) * WH * WD]) for n in range(2)]
        WPROBS = 4
        wprobs = [(x0, stack_words)[n // 2][:, n % 2 * TILES * WKEYS:(n % 2 + 1) * TILES * WKEYS] for n in range(WPROBS)]
        WTURNED = 4
        wturned = [turned_words[:, n * 3 * S:(n + 1) * 3 * S] for n in range(WTURNED)]
        wout_t = vals_all
        wtop = sb("wtop", [P, 2 * WPROBS])
        wden = sb("wden", [P, 2 * WPROBS])
        wrden = sb("wrden", [P, 2 * WPROBS])
        wstats = sb("wstats", [P, 3 * 6])
        wmv = sb("wmv", [P, 3 * 2])
        wrs = sb("wrs", [P, 3])

        centroids = sb("centroids", [G + E, D])
        cent_t = sb("cent_t", [P, G + E])
        cent_s = sb("cent_s", [G + E, 4])
        cent_sq = sb("cent_sq", [G + E, D])
        choice_bias = sb("choice_bias", [P, E])
        before = sb("before", [P, G * G])
        iota_e = sb("iota_e", [P, E])
        iota_i = sb("iota_i", [P, E], I32)
        earlier = sb("earlier", [P, P], BF16)
        ones_b = sb("ones_b", [P, P], BF16)
        zeros = sb("zeros", [P, 8 * D])
        shared_w = sb("shared_w", [P, 2 * HID + 2 * D])
        half_up = sb("half_up", [P, NT])
        slot_in = sb("slot_in", [P, NT * K], U32)
        slot_out = sb("slot_out", [P, NT * K], U32)
        gate = sb("gate", [P, NT * K])
        small = sb("small", [P, 5 * NT])
        lstats = sb("lstats", [P, GROUP * 6])
        lmv = sb("lmv", [P, GROUP * 2])
        glrs = sb("glrs", [P, GROUP])

        class View:

            def __init__(self, buf):
                self.buf, self.at = buf, 0

            def take(self, n):
                self.at += n
                return self.buf[:, self.at - n:self.at]

        spare = View(probs_all)
        xt_all, acc = spare.take(N), spare.take(N)
        spare = View(x0)
        g_score, e_score, top8, idx8 = spare.take(NT * G), spare.take(NT * E), spare.take(NT * 8), spare.take(NT * 8)
        masked, rank, idx_f, pos = spare.take(NT * E), spare.take(NT * G), spare.take(NT * K), spare.take(NT * K)
        gates, keep, tmp_k = spare.take(NT * K), spare.take(NT * K), spare.take(NT * K)
        spare = View(turned_words)
        cmp_gt, cmp_eq, sh_hid = spare.take(NT * G * G), spare.take(NT * G * G), spare.take(1024)
        onehot, picked = vals_all[:, 0:NT * K * E], stack_words[:, 0:NT * K * E]
        spare = View(qk)
        totals = spare.take(NT * E)
        ahead, ahead2 = qk2[:, :], qk3[:, :]
        chosen = cuts[0][:, 0:NT * E]
        ew = [wv[0][:, n * 768:(n + 1) * 768] for n in range(RING)]
        ex_rows = [wk_t[1][0:SLOT_P, n * 512:(n + 1) * 512] for n in range(RING)]
        ex_t = [turned_words[:, 3072 + n * CAP:3072 + (n + 1) * CAP] for n in range(2)]
        ex_g = [wk_t[0][:, n * 2 * CAP:(n + 1) * 2 * CAP] for n in range(2)]
        ex_h = [wk_t[0][:, (2 + n) * 2 * CAP:(3 + n) * 2 * CAP] for n in range(2)]
        ex_out = [wv[1][0:SLOT_P, n * 512:(n + 1) * 512] for n in range(RING)]
        sh_gate = wv[1][:, 2048:3072]
        gathered = [vals_all[:, :], stack_words[:, :]]

        score_ps = [ps(f"score_ps{n}", [P, 2, 512]) for n in range(2)]
        out_ps = ps("out_ps", [P, 512])
        post_ps = ps("post_ps", [P, 512])
        sums_ps = (out_ps, post_ps)
        pre_ps = ps("pre_ps", [P, 512])
        turn_ps = ps("turn_ps", [P, 512])

        loaded = {n: sem(f"loaded_{n}") for n in ("x", "ctx", "mask", "early", "g", "l", "x_", "f", "a", "w")}
        consts = sem("consts")
        waited = sem("waited")
        zeroed = sem("zeroed")
        setup_ps = sem("setup_ps")
        setup_sb = sem("setup_sb")
        v_step = sem("v_step")
        g_step = sem("g_step")
        x_rows = sem("x_rows")
        x_turned = sem("x_turned")
        xt_ready = sem("xt_ready")
        projected = sem("projected")
        pre_read = sem("pre_read")
        stacked = sem("stacked")
        turned = sem("turned")
        operands = sem("operands")
        turn_read = sem("turn_read")
        top_a, top_b = sem("top_a"), sem("top_b")
        shifted = sem("shifted")
        scored = sem("scored")
        probs_ready = sem("probs_ready")
        probs_free = sem("probs_free")
        ot_ready = sem("ot_ready")
        rows_back = sem("rows_back")
        merged = sem("merged")
        merged_turned = sem("merged_turned")
        ont_ready = sem("ont_ready")
        out_projected = sem("out_projected")
        post_read = sem("post_read")
        pow_asked = sem("pow_asked")
        pow_done = sem("pow_done")
        wide_scored = sem("wide_scored")
        topped = sem("topped")
        exped = sem("exped")
        scaled = sem("scaled")
        probs_turned = sem("probs_turned")
        turned_a = sem("turned_a")
        turned_c = sem("turned_c")
        pair_summed = sem("pair_summed")
        pair_out = sem("pair_out")
        wide_made = sem("wide_made")
        wide_a = sem("wide_a")
        wide_v = sem("wide_v")
        exp_loaded = sem("exp_loaded")
        slots_zeroed = sem("slots_zeroed")
        scattered = sem("scattered")
        weights_in = [sem(f"weights_in{n}") for n in range(RING)]
        results_out = [sem(f"results_out{n}") for n in range(RING)]
        gathered_in = [sem(f"gathered_in{n}") for n in range(2)]
        r_ps = sem("r_ps")
        r_sb = sem("r_sb")
        exps_asked = sem("exps_asked")
        exps_made = sem("exps_made")
        slots_known = sem("slots_known")
        sh_made = sem("sh_made")
        sh_silu = sem("sh_silu")
        sh_gated = sem("sh_gated")
        sh_summed = sem("sh_summed")
        rows_turned = sem("rows_turned")
        rows_copied = sem("rows_copied")
        gate_made = sem("gate_made")
        up_made = sem("up_made")
        silued = sem("silued")
        gated = sem("gated")
        downed = sem("downed")
        out_rows = sem("out_rows")
        combined = sem("combined")
        written = sem("written")
        stored = sem("stored")

        turn_banks = [bank[:, :].bitcast(BF16) for bank in (turn_ps, pre_ps)]

        block = ctx.enter_context(nc.Block())

        def rows_of(buf, b):
            return buf[:, bass.ts(b, TILES * D)]

        def wide_copy(L, par, k):
            what, c = L.products[k]
            if what == "q":
                return wq_t[par][:, c * S:(c + 2) * S], turn_ps[:, :], 1.0 / float(np.sqrt(WD))
            if what == "k":
                return wk_t[par][:, c * WKEYS:(c + 1) * WKEYS], turn_ps[:, 0:WKEYS], 1.0
            m = KEY_TILES[c // 2][1]
            at = (c // 2) * WH * WD + (c % 2) * 512
            return wv[par][0:m, at:at + 512], turn_ps[0:m, :], 1.0

        @block.sync
        def _(eng):
            eng.dma_start(x0[:, :].rearrange("p (n d) -> p n d", d=D),
                          t["x"].rearrange("b (t p) d -> p (b t) d", p=P)).then_inc(loaded["x"], 16)
            eng.dma_start(down_t[:, :], t["down_t"]).then_inc(loaded["early"], 16)
            eng.dma_start(ups[:, :], t["ups"]).then_inc(loaded["early"], 16)
            for L in NARROW[:2]:
                s = loaded[L.name]
                w = weights[L.name]
                if L.name == "g":
                    eng.dma_start(w[:, 0:D], t["w_g"]).then_inc(s, 16)
                else:
                    eng.dma_start(w[:, :], t["w_l"]).then_inc(s, 16)
                eng.dma_start(wo[L.name][:, :], t[f"wo_{L.name}"]).then_inc(s, 16)
                eng.dma_start(norm_w[L.name][:, :], t[f"nw_{L.name}"]).then_inc(s, 16)
                eng.dma_start(cos[L.name][:, :], t[f"cos_{L.name}"]).then_inc(s, 16)
                eng.dma_start(sin[L.name][:, :], t[f"sin_{L.name}"]).then_inc(s, 16)
            eng.dma_start(ctx_all[:, :].rearrange("p (b d) -> p b d", d=D),
                          t["ctx"].rearrange("b p d -> p b d")).then_inc(loaded["ctx"], 16)
            eng.dma_start(given8[:, :].rearrange("p (n c) -> p n c", c=C),
                          t["mask"].rearrange("b (t p) c -> p (b t) c", p=P)).then_inc(loaded["mask"], 16)
            for L, s in ((NARROW[2], loaded["x_"]), (NARROW[3], loaded["a"])):
                eng.dma_start(weights[L.name][:, :], t[f"w_{L.name}"]).then_inc(s, 16)
                eng.dma_start(wo[L.name][:, :], t[f"wo_{L.name}"]).then_inc(s, 16)
                eng.dma_start(bias_in[L.name][:, :], t[f"bi_{L.name}"]).then_inc(s, 16)
                eng.dma_start(bias_out[L.name][:, :], t[f"bo_{L.name}"]).then_inc(s, 16)
                if L.rope:
                    eng.dma_start(cos[L.name][:, :], t[f"cos_{L.name}"]).then_inc(s, 16)
                    eng.dma_start(sin[L.name][:, :], t[f"sin_{L.name}"]).then_inc(s, 16)
            for n, m in enumerate(("Fr", "Fi", "nFi", "Gr", "nGi")):
                eng.dma_start(fourier[:, n * D:(n + 1) * D], t[m]).then_inc(loaded["f"], 16)
            eng.dma_start(freq_w[:, 0:D], t["freq_r"]).then_inc(loaded["f"], 16)
            eng.dma_start(freq_w[:, D:2 * D], t["freq_i"]).then_inc(loaded["f"], 16)
            eng.dma_start(bias_mix[:, :], t["bias_mix"]).then_inc(loaded["f"], 16)
            eng.dma_start(wide_q[:, :], t["wide_q"]).then_inc(loaded["w"], 16)
            eng.dma_start(wide_kv[:, :], t["wide_kv"]).then_inc(loaded["w"], 16)
            eng.dma_start(wide_o[:, :].rearrange("p (c d) -> p c d", d=D),
                          t["wide_o"].rearrange("(c p) d -> p c d", p=P)).then_inc(loaded["w"], 16)
            eng.dma_start(ln_wb[:, :], t["ln_wb"]).then_inc(loaded["w"], 16)
            if not experts:
                eng.wait_ge(stored, 1)
                eng.dma_start(t["out"].rearrange("b (t p) d -> p (b t) d", p=P),
                              xb[:, :].rearrange("p (n d) -> p n d", d=D)).then_inc(stored, 16)
                eng.wait_ge(stored, 17)
                return
            eng.dma_start(centroids[0:G, :], t["group_c"]).then_inc(exp_loaded, 16)
            eng.dma_start(centroids[G:G + E, :], t["expert_c"]).then_inc(exp_loaded, 16)
            eng.dma_start(choice_bias[:, :], t["choice_bias"]).then_inc(exp_loaded, 16)
            eng.dma_start(shared_w[:, 0:HID], t["sg"]).then_inc(exp_loaded, 16)
            eng.dma_start(shared_w[:, HID:2 * HID], t["su"]).then_inc(exp_loaded, 16)
            eng.dma_start(shared_w[:, 2 * HID:].rearrange("p (c d) -> p c d", c=2),
                          t["sd"].rearrange("(p c) d -> p c d", c=2)).then_inc(exp_loaded, 16)
            eng.wait_ge(zeroed, ZEROED + 1)
            slot_blocks = t["slots"].rearrange("(p n) d -> p (n d)", p=P)
            for n in range(E * CAP // P // 8):
                eng.dma_start(slot_blocks[:, n * 8 * D:(n + 1) * 8 * D], zeros[:, :]).then_inc(slots_zeroed, 16)

            counts = Counts("sync", eng, per)

            def load_weights(e, n):
                w = ew[n]
                eng.dma_start(w[:, 0:HID], t["wg"][bass.ts(e, P), :]).then_inc(weights_in[n], 16)
                eng.dma_start(w[:, HID:2 * HID], t["wu"][bass.ts(e, P), :]).then_inc(weights_in[n], 16)
                eng.dma_start(w[:, 2 * HID:], t["wd"][bass.ts(e, P), :]).then_inc(weights_in[n], 16)

            def load_rows(e, n):
                eng.dma_start(ex_rows[n], t["slots"].rearrange("(p j) d -> p (j d)", j=SLOT_J)[bass.ts(e, SLOT_P), :])\
                   .then_inc(weights_in[n], 16)

            def store(e, n):
                eng.wait_ge(out_rows, counts.after(out_rows))
                eng.dma_start(t["results"].rearrange("(p j) d -> p (j d)", j=SLOT_J)[bass.ts(e, SLOT_P), :], ex_out[n])\
                   .then_inc(results_out[n], 16)

            eng.wait_ge(r_sb, 1)
            for n in range(RING):
                load_weights(n, n)
            for one in (slots_zeroed, scattered):
                eng.wait_ge(one, 16 * (E * CAP // P // 8 if one is slots_zeroed else NT * K))
            for n in range(RING):
                load_rows(n, n)
            with counts.loop((E - RING) // RING) as i:
                for n in range(RING):
                    eng.wait_ge(downed, counts.after(downed))
                    load_weights(i * RING + (RING + n), n)
                    load_rows(i * RING + (RING + n), n)
                    store(i * RING + n, n)
            for n in range(RING):
                store(E - RING + n, n)
            for q in range(NT // GROUP):
                eng.wait_ge(written, q + 1)
                rows = slice(q * GROUP * D, (q + 1) * GROUP * D)
                eng.dma_start(t["out"].rearrange("b (t p) d -> p (b t) d", p=P)[:, q * GROUP:(q + 1) * GROUP, :],
                              xb[:, rows].rearrange("p (n d) -> p n d", d=D)).then_inc(stored, 16)
            eng.wait_ge(stored, 16 * (NT // GROUP))

        @block.gpsimd
        def _(eng):
            counts = Counts("gpsimd", eng, per)
            eng.memset(half[:, :], -0.5).then_inc(consts, 1)
            eng.memset(eye[:, :], 0.0).then_inc(g_step, 1)
            eng.memset(causal_q[:, :], 0.0).then_inc(g_step, 1)
            eng.memset(causal_k[:, :], 0.0).then_inc(g_step, 1)
            eng.memset(window_k[:, :], 0.0).then_inc(g_step, 1)
            eng.memset(given_t[:, :], 0.0).then_inc(zeroed, 1)
            eng.wait_ge(g_step, counts.after(g_step, 4))
            eng.affine_select(out=eye[:, :], in_=eye[:, :], compare_op=ALU.not_equal, fill=1.0, base=0,
                              pattern=[[-1, P]], channel_multiplier=1).then_inc(g_step, 1)
            eng.affine_select(out=causal_q[:, :], in_=causal_q[:, :], compare_op=ALU.is_ge, fill=NEG, base=0,
                              pattern=[[-1, P]], channel_multiplier=1).then_inc(consts, 1)
            eng.affine_select(out=causal_k[:, :], in_=causal_k[:, :], compare_op=ALU.is_ge, fill=NEG, base=0,
                              pattern=[[1, P]], channel_multiplier=-1).then_inc(consts, 1)
            eng.affine_select(out=window_k[:, :], in_=window_k[:, :], compare_op=ALU.is_ge, fill=NEG, base=0,
                              pattern=[[1, P + WIN]], channel_multiplier=-1).then_inc(g_step, 1)
            eng.wait_ge(g_step, counts.after(g_step, 2))
            eng.affine_select(out=window_k[:, :], in_=window_k[:, :], compare_op=ALU.is_ge, fill=NEG, base=WIN - 1,
                              pattern=[[-1, P + WIN]], channel_multiplier=1).then_inc(consts, 1)
            eng.tensor_copy(eye_b[:, :], eye[:, :]).then_inc(consts, 1)
            eng.memset(zeros[:, :], 0.0).then_inc(zeroed, 1)
            for buf in (before, earlier, ones_b):
                eng.memset(buf[:, :], 1.0).then_inc(g_step, 1)
            eng.memset(half_up[:, :], 0.5).then_inc(g_step, 1)
            eng.iota(iota_i[:, :], pattern=[[1, E]], base=0, channel_multiplier=0).then_inc(g_step, 1)
            eng.wait_ge(g_step, counts.after(g_step, 5))
            eng.affine_select(out=before[:, :].rearrange("p (i j) -> p i j", j=G), in_=before[:, :].rearrange("p (i j) -> p i j", j=G),
                              compare_op=ALU.is_gt, fill=0.0, base=0, pattern=[[1, G], [-1, G]], channel_multiplier=0)\
               .then_inc(consts, 1)
            eng.affine_select(out=earlier[:, :], in_=earlier[:, :], compare_op=ALU.is_gt, fill=0.0, base=0,
                              pattern=[[1, P]], channel_multiplier=-1).then_inc(consts, 1)
            eng.tensor_copy(iota_e[:, :], iota_i[:, :]).then_inc(consts, 1)

            def power(dst, src, scale, eps, n):
                eng.wait_ge(pow_asked, counts.after(pow_asked))
                eng.sem_inc(waited, 1)
                eng.tensor_scalar(dst, src, scale, eps, ALU.mult, ALU.add).then_inc(g_step, 1)
                eng.wait_ge(g_step, counts.after(g_step))
                eng.tensor_tensor(dst, dst, half[:, 0:n], ALU.pow).then_inc(pow_done, 1)

            def norm(L, b, par, k):
                if L is WIDE:
                    power(wrs[:, :], wmv[:, 1:6:2], 1.0, 1e-5, 3)
                elif L.rms:
                    power(rs[:, :], ss[:, :], 1.0 / D, 1e-6, 2)

            def cut(L, b, par, k):
                if L.qk_norm and k == 0:
                    power(nrs[:, :], nss[:, :], 1.0 / HD, 1e-6, 40)

            def output(L, b, par, k):
                if L in (MIXING, WIDE) or L.norm:
                    power(lrs[:, :], mv[:, 1:4:2], 1.0, 1e-5, 2)

            for L in layers:
                run_layer(L, counts, dict(norm=norm, cut=cut, output=output, mixed=output, wide_output=output))
            if not experts:
                return

            eng.wait_ge(pow_asked, counts.after(pow_asked))
            eng.tensor_tensor(cent_s[:, 1:2], cent_s[:, 0:1], half_up[0:G + E, 0:1], ALU.pow).then_inc(pow_done, 1)
            eng.wait_ge(pow_asked, counts.after(pow_asked))
            eng.tensor_tensor(small[:, NT:2 * NT], small[:, 0:NT], half_up[:, :], ALU.pow).then_inc(pow_done, 1)

            eng.wait_ge(slots_known, 1)
            eng.wait_ge(slots_zeroed, 16 * (E * CAP // P // 8))
            for tile in range(NT):
                for k in range(K):
                    eng.indirect_dma_start(t["slots"][:, :], bass.IndirectOffsetOnAxis(slot_in[:, tile * K + k:tile * K + k + 1], 0),
                                           xb[:, tile * D:(tile + 1) * D], None,
                                           bounds_check=E * CAP - 1, oob_is_err=False).then_inc(scattered, 16)
            for n in range(RING):
                eng.wait_ge(results_out[n], 16 * (E // RING))

            def gather(q):
                if q >= 2:
                    eng.wait_ge(combined, q - 1)
                for m in range(GROUP * K):
                    at = q * GROUP * K + m
                    eng.indirect_dma_start(gathered[q % 2][:, m * D:(m + 1) * D], None, t["results"][:, :],
                                           bass.IndirectOffsetOnAxis(slot_out[:, at:at + 1], 0),
                                           bounds_check=E * CAP - 1, oob_is_err=False).then_inc(gathered_in[q % 2], 16)

            gather(0)
            gather(1)
            for q in range(NT // GROUP):
                power(glrs[:, :], lmv[:, 1:2 * GROUP:2], 1.0, 1e-5, GROUP)
                if q + 2 < NT // GROUP:
                    gather(q + 2)

        @block.tensor
        def _(eng):
            counts = Counts("tensor", eng, per)
            eng.wait_ge(consts, 8)
            eng.wait_ge(loaded["early"], 32)
            eng.matmul(pre_ps[:, 0:2 * KVH * HD], down_t[:, :], ups[:, :], start=True, stop=True).then_inc(setup_ps, 1)
            eng.wait_ge(setup_sb, counts.after(setup_sb, 2))
            given_ps = turn_ps[:, :].bitcast(BF16)
            for half_ in range(2):
                if half_:
                    eng.wait_ge(setup_sb, counts.after(setup_sb))
                for n in range(8):
                    tile = half_ * 8 + n
                    last = eng.transpose(given_ps[0:C, n * P:(n + 1) * P], given[:, tile * C:(tile + 1) * C], eye_b[:, :])
                last.then_inc(setup_ps, 1)
            eng.wait_ge(zeroed, ZEROED + 1)

            def turn_x(L, b, par, k):
                if L is WIDE and not (isinstance(b, int) and b <= 1):
                    eng.wait_ge(pair_out, counts.until(pair_out, par, CHUNKS - 1))
                if unread_pre[0]:
                    eng.wait_ge(pre_read, counts.after(pre_read, unread_pre[0]))
                    unread_pre[0] = 0
                if L in NARROW and not (isinstance(b, int) and b <= 1) and counts.owed(operands, par, L.turns):
                    eng.wait_ge(operands, counts.until(operands, par, L.turns))
                eng.wait_ge(x_rows, counts.after(x_rows))
                for n in range(TILES):
                    last = eng.transpose(pre_ps[:, n * P:(n + 1) * P], xs[par][:, n * D:(n + 1) * D], eye[:, :])
                if L.cross:
                    last = eng.transpose(pre_ps[:, S:S + C], xc[:, :], eye[0:C, 0:C])
                last.then_inc(x_turned, 1)

            def project(L, b, par, k):
                w = weights[L.name]
                eng.wait_ge(xt_ready, counts.after(xt_ready))
                if L.cross:
                    for n in range(TILES):
                        eng.matmul(pre_ps[:, n * D:(n + 1) * D], xt[:, n * P:(n + 1) * P], w[:, 0:D], start=True, stop=True)
                    last = eng.matmul(pre_ps[0:C, 2 * D:3 * D], xt[:, S:S + C], w[:, D:2 * D], start=True, stop=True)
                else:
                    width = D + L.kn
                    for n in range(TILES):
                        last = eng.matmul(pre_ps[:, n * width:(n + 1) * width], xt[:, n * P:(n + 1) * P], w[:, 0:width],
                                          start=True, stop=True)
                last.then_inc(projected, 1)
                unread_pre[0] += 1

            def project_v(L, b, par, k):
                w = weights[L.name][:, D + L.kn:D + 2 * L.kn]
                if not (isinstance(b, int) and b == 0) and counts.owed(operands, 1 - par, L.turns - 1):
                    eng.wait_ge(operands, counts.until(operands, 1 - par, L.turns - 1))
                for n in range(L.key_tiles):
                    first = S if L.cross else n * P
                    last = eng.matmul(turn_ps[0:L.keys, n * L.kn:(n + 1) * L.kn], xt[:, first:first + L.keys], w,
                                      start=True, stop=True)
                last.then_inc(projected, 1)

            def turn_q(L, b, par, k):
                if k == 0:
                    counts.batch(par, operands)
                    eng.wait_ge(stacked, counts.after(stacked))
                elif k == 2:
                    eng.wait_ge(shifted, counts.after(shifted))
                    eng.wait_ge(turn_read, counts.after(turn_read))
                elif k == 1 and unread_pre[0]:
                    eng.wait_ge(pre_read, counts.after(pre_read, unread_pre[0]))
                    unread_pre[0] = 0
                bank = turn_banks[k % 2]
                for u in range(4 * (k % 2), 4 * (k % 2) + 4):
                    for n in range(TILES):
                        at = (n * H + place(u, 0)) * PART
                        last = eng.transpose(bank[:, ((u % 4) * TILES + n) * P:((u % 4) * TILES + n + 1) * P],
                                             q_stack[:, at:at + P], eye_b[:, :])
                last.then_inc(turned, 1)

            def turn_k(L, b, par, k):
                n_k = L.keys
                per_bank = 8 if L.cross else 4
                for n_bank, first in enumerate(range(0, L.ktiles, per_bank)):
                    eng.wait_ge(operands, counts.until(operands, par, 1 + n_bank))
                    if L.cross:
                        eng.sem_inc(waited, 1)
                    for u in range(first, min(first + per_bank, L.ktiles)):
                        for n in range(L.key_tiles):
                            rows = (n * L.kvh + 2 * u) * PART
                            at = ((u - first) * L.key_tiles + n) * n_k
                            last = eng.transpose(turn_banks[n_bank][:, at:at + n_k],
                                                 k_stack[0:n_k, rows:rows + P],
                                                 eye_b[0:n_k, 0:n_k])
                    last.then_inc(turned, 1)

            def keys_of(L, par, u, side, rows, first, n):
                width = L.keys * L.key_tiles
                at = L.key_tile(u) * width + first
                return kt_[par][PART * side:PART * side + rows, at:at + n]

            def queries_of(par, u, side, rows, first, n):
                return qt[par][PART * side:PART * side + rows, u * S + first:u * S + first + n]

            def top(L, b, par, k):
                q, side, u0, m, n = L.top_steps[k]
                bank, full = ((pre_ps, top_a), (turn_ps, top_b))[k % 2]
                if k == 0:
                    eng.wait_ge(operands, counts.until(operands, par, L.turns - 2))
                if k % 2 == 0 and unread_pre[0]:
                    eng.wait_ge(pre_read, counts.after(pre_read, unread_pre[0]))
                    unread_pre[0] = 0
                elif k % 2 and k > 1:
                    eng.wait_ge(turn_read, counts.after(turn_read))
                unread_pre[0] += 1 - k % 2
                if L.cross:
                    eng.matmul(bank[:, 0:m * n].rearrange("p (m n) -> p m n", m=m), eye_b[:, :],
                               given[:, bass.ds(b * (TILES * C) + q * C, C)].unsqueeze(1).broadcast_to([P, m, C]),
                               start=True, stop=False, skip_group_check=True)
                else:
                    eng.matmul(bank[:, 0:m * n].rearrange("p (m n) -> p m n", m=m)[:, :, n - P:n], eye_b[:, :],
                               causal_q[:, :].unsqueeze(1).broadcast_to([P, m, P]),
                               start=True, stop=False, skip_group_check=True)
                for j in range(m):
                    last = eng.matmul(bank[:, j * n:(j + 1) * n], queries_of(par, u0 + j, side, ROWS, q * P, P),
                                      keys_of(L, par, u0 + j, side, ROWS, 0, n),
                                      start=False, stop=True, skip_group_check=True)
                last.then_inc(full, 1)

            def scores(L, b, par, k):
                g, kt, q0, q1 = L.steps[k]
                bank = score_ps[k % 2]
                rows = ROWS_MAX if L.top else ROWS
                if k == 0:
                    counts.batch(par, probs_ready, ot_ready)
                ready = L.turns - (1 if L.top and g < 2 else 0)
                if counts.owed(operands, par, ready):
                    eng.wait_ge(operands, counts.until(operands, par, ready))
                if counts.owed(probs_ready, par, k - 1):
                    eng.wait_ge(probs_ready, counts.until(probs_ready, par, k - 1))
                if L.cross:
                    eng.sem_inc(waited, 1)
                n_k = L.keys
                for side in range(2):
                    if L.mask == "given":
                        width = S
                        mask = given_t[:, bass.ts(b, S)]
                    else:
                        width = q1 - q0 if L.mask == "window" else P
                        mask = (window_k if L.mask == "window" else causal_k)[:, 0:width]
                    eng.matmul(bank[0:n_k, side, :].rearrange("p (u q) -> p u q", u=2)[:, :, q0:q0 + width],
                               eye_b[:, 0:n_k], mask.unsqueeze(1).broadcast_to([P, 2, width]),
                               start=True, stop=False, skip_group_check=True)
                for side in range(2):
                    for uu in range(2):
                        u = 2 * g + uu
                        last = eng.matmul(bank[0:n_k, side, uu * S + q0:uu * S + q1],
                                          keys_of(L, par, u, side, rows, kt * P, n_k),
                                          queries_of(par, u, side, rows, q0, q1 - q0),
                                          start=False, stop=True, skip_group_check=True)
                last.then_inc(scored, 1)

            def values(L, b, par, k):
                if counts.owed(ot_ready, par, k - 1):
                    eng.wait_ge(ot_ready, counts.until(ot_ready, par, k - 1))
                if k == 1:
                    eng.wait_ge(post_read, counts.after(post_read))
                if k == 3 and not L.top:
                    eng.wait_ge(merged, counts.after(merged))
                steps = [n for n, step in enumerate(L.steps) if step[0] == k]
                v = vals[par][0:L.keys, :].rearrange("p (t h c) -> p t h c", t=TILES, c=32)
                for n in steps:
                    g, kt, q0, q1 = L.steps[n]
                    if counts.owed(probs_ready, par, n + 1):
                        eng.wait_ge(probs_ready, counts.until(probs_ready, par, n + 1))
                        if L.cross:
                            eng.sem_inc(waited, 1)
                    for side in range(2):
                        for uu in range(2):
                            j = 2 * side + uu
                            h = L.value_head(2 * g + uu, side)
                            last = eng.matmul(sums_ps[k % 2][32 * j:32 * j + 32, q0:q1], v[:, kt, h, :],
                                              probs[n % PROBS][0:L.keys, j * S + q0:j * S + q1],
                                              start=(n == steps[0]), stop=(n == steps[-1]), skip_group_check=True)
                    last.then_inc(probs_free, 1)

            def merge(L, b, par, k):
                groups = 4 if L.top else 2 * k + 2
                if counts.owed(ot_ready, par, groups):
                    eng.wait_ge(ot_ready, counts.until(ot_ready, par, groups))
                if k and L.top:
                    eng.wait_ge(merged, counts.after(merged))
                for n in range(TILES):
                    for g in range(2):
                        at = (2 * n + g) * P
                        last = eng.transpose(post_ps[:, at:at + P],
                                             ot[:, (2 * k + g) * S + n * P:(2 * k + g) * S + (n + 1) * P], eye[:, :])
                last.then_inc(rows_back, 1)

            def output(L, b, par, k):
                eng.wait_ge(merged, counts.after(merged))
                for n in range(TILES):
                    last = eng.transpose(post_ps[:, n * P:(n + 1) * P], on[:, n * D:(n + 1) * D], eye[:, :])
                last.then_inc(merged_turned, 1)
                eng.wait_ge(ont_ready, counts.after(ont_ready))
                for n in range(TILES):
                    last = eng.matmul(post_ps[:, n * D:(n + 1) * D], ont[:, n * P:(n + 1) * P], wo[L.name][:, :],
                                      start=True, stop=True)
                last.then_inc(out_projected, 1)

            def mixing_matrix():
                fr, fi, nfi, gr, ngi = (fourier[:, n * D:(n + 1) * D] for n in range(5))
                wr, wi = freq_w[:, 0:D], freq_w[:, D:2 * D]
                for n, (a, b_) in enumerate(((fr, nfi), (fi, fr))):
                    eng.matmul(out_ps[:, n * D:(n + 1) * D], wr, a, start=True, stop=False)
                    last = eng.matmul(out_ps[:, n * D:(n + 1) * D], wi, b_, start=False, stop=True)
                last.then_inc(setup_ps, 1)
                eng.wait_ge(setup_sb, counts.after(setup_sb))
                eng.matmul(out_ps[:, 0:D], freq_a[:, 0:D], gr, start=True, stop=False)
                eng.matmul(out_ps[:, 0:D], freq_a[:, D:2 * D], ngi, start=False, stop=True).then_inc(setup_ps, 1)
                eng.wait_ge(setup_sb, counts.after(setup_sb))

            def mix(L, b, par, k):
                eng.wait_ge(xt_ready, counts.after(xt_ready))
                for n in range(TILES):
                    last = eng.matmul(pre_ps[:, n * D:(n + 1) * D], xt[:, n * P:(n + 1) * P], mix_w[:, :], start=True, stop=True)
                last.then_inc(projected, 1)
                unread_pre[0] += 1

            def wide_project(L, b, par, k):
                if k == 0:
                    eng.wait_ge(xt_ready, counts.after(xt_ready))
                if k % 2:
                    eng.wait_ge(wide_v, counts.after(wide_v))
                elif k:
                    eng.wait_ge(wide_a, counts.after(wide_a))
                what, c = L.products[k]
                if what == "q":
                    for n in range(2):
                        last = eng.matmul(turn_ps[:, n * S:(n + 1) * S], wide_q[:, (c + n) * P:(c + n + 1) * P], xt[:, 0:S],
                                          start=True, stop=True)
                elif what == "k":
                    last = eng.matmul(turn_ps[:, 0:WKEYS], wide_kv[:, c * P:(c + 1) * P], xt[:, :], start=True, stop=True)
                else:
                    first, n = KEY_TILES[c // 2]
                    at = WH * WD + (c % 2) * 512
                    last = eng.matmul(turn_ps[0:n, :], xt[:, first:first + n], wide_kv[:, at:at + 512], start=True, stop=True)
                last.then_inc(wide_made, 1)

            def wide_scores(L, b, par, k):
                c, rows = k // 2, slice(WD * (k % 2), WD * (k % 2) + WD)
                if k == 0:
                    eng.wait_ge(wide_a, counts.after(wide_a))
                    counts.batch(par, exped, turned_a, turned_c, pair_out)
                if counts.owed(exped, par, k - 1):
                    eng.wait_ge(exped, counts.until(exped, par, k - 1))
                for n in range(TILES):
                    last = eng.matmul(score_ps[k % 2][:, n, 0:WKEYS], wq_t[par][rows, c * S + n * P:c * S + (n + 1) * P],
                                      wk_t[par][rows, c * WKEYS:(c + 1) * WKEYS], start=True, stop=True)
                last.then_inc(wide_scored, 1)

            def wide_turn(L, b, par, k):
                eng.wait_ge(scaled, counts.after(scaled))
                if counts.owed(turned_a, par, k):
                    eng.wait_ge(turned_a, counts.until(turned_a, par, k))
                if counts.owed(turned_c, par, k):
                    eng.wait_ge(turned_c, counts.until(turned_c, par, k))
                if unread[0]:
                    eng.wait_ge(post_read, counts.after(post_read))
                    unread[0] = False
                src = wprobs[k % WPROBS]
                for n, (first, m) in enumerate(KEY_TILES):
                    for q in range(TILES):
                        bank, at = (out_ps, n * S) if n < 2 else (post_ps, 0)
                        last = eng.transpose(bank[0:m, at + q * P:at + (q + 1) * P],
                                             src[:, q * WKEYS + first:q * WKEYS + first + m], eye[:, :])
                last.then_inc(probs_turned, 1)

            def wide_values(L, b, par, k):
                if counts.owed(turned_a, par, 2 * k + 2):
                    eng.wait_ge(turned_a, counts.until(turned_a, par, 2 * k + 2))
                if counts.owed(turned_c, par, 2 * k + 2):
                    eng.wait_ge(turned_c, counts.until(turned_c, par, 2 * k + 2))
                if counts.owed(pair_out, par, k):
                    eng.wait_ge(pair_out, counts.until(pair_out, par, k))
                for n, (first, m) in enumerate(KEY_TILES):
                    for side in range(2):
                        h = 2 * k + side
                        last = eng.matmul(pre_ps[WD * side:WD * side + WD, 0:S],
                                          wv[par][0:m, n * WH * WD + h * WD:n * WH * WD + (h + 1) * WD],
                                          wturned[h % WTURNED][0:m, n * S:(n + 1) * S],
                                          start=(n == 0), stop=(n == len(KEY_TILES) - 1), skip_group_check=True)
                last.then_inc(pair_summed, 1)

            def wide_output(L, b, par, k):
                if counts.owed(pair_out, par, CHUNKS):
                    eng.wait_ge(pair_out, counts.until(pair_out, par, CHUNKS))
                ahead_ = WH if isinstance(b, int) and b == B - 1 else WH + 2
                if counts.owed(turned_c, par, ahead_):
                    eng.wait_ge(turned_c, counts.until(turned_c, par, ahead_))
                for n in range(TILES):
                    for c in range(CHUNKS):
                        last = eng.matmul(post_ps[:, n * D:(n + 1) * D], wout_t[:, c * S + n * P:c * S + (n + 1) * P],
                                          wide_o[:, c * D:(c + 1) * D], start=(c == 0), stop=(c == CHUNKS - 1))
                last.then_inc(out_projected, 1)
                unread[0] = True

            unread, unread_pre = [True], [0]
            for L in layers:
                eng.wait_ge(loaded["x_" if L.name == "x" else L.name], loads_of(L))
                if L is MIXING:
                    mixing_matrix()
                elif L is WIDE:
                    counts.layer([(exped, WH), (turned_a, WH), (turned_c, WH), (pair_out, CHUNKS)])
                else:
                    counts.layer([(probs_ready, len(L.steps)), (ot_ready, 4), (operands, L.turns)])
                run_layer(L, counts, dict(turn_x=turn_x, project=project, project_v=project_v, turn_q=turn_q, turn_k=turn_k, top=top,
                                          scores=scores, values=values, merge=merge, output=output, mix=mix,
                                          wide_project=wide_project, wide_scores=wide_scores, wide_turn=wide_turn,
                                          wide_values=wide_values, wide_output=wide_output))
            if not experts:
                return

            eng.wait_ge(exp_loaded, 16 * 6)
            eng.wait_ge(r_sb, counts.after(r_sb))
            eng.transpose(out_ps[:, 0:G + E], centroids[:, :], eye[0:G + E, 0:G + E]).then_inc(r_ps, 1)
            for q in range(NT // 4):
                bank = (pre_ps, turn_ps)[q % 2]
                if q >= 2:
                    eng.wait_ge(r_sb, counts.after(r_sb))
                for m in range(4):
                    tile = 4 * q + m
                    last = eng.transpose(bank[:, m * P:(m + 1) * P], xb[:, tile * D:(tile + 1) * D], eye[:, :])
                last.then_inc(r_ps, 1)
            eng.wait_ge(r_sb, counts.after(r_sb, 2))
            for tile in range(NT):
                last = eng.matmul(score_ps[0][:, tile // 8, (tile % 8) * (G + E):(tile % 8 + 1) * (G + E)],
                                  xt_all[:, tile * P:(tile + 1) * P], cent_t[:, :], start=True, stop=True)
            last.then_inc(r_ps, 1)

            def shared(q):
                for part in range(2):
                    for c in range(2):
                        last = eng.matmul(score_ps[part][:, c, :], shared_w[:, part * HID + c:(part + 1) * HID:2],
                                          xt_all[:, q * 512:(q + 1) * 512], start=True, stop=True)
                    last.then_inc(sh_made, 1)
                eng.wait_ge(sh_gated, counts.after(sh_gated))
                bank = (pre_ps, turn_ps)[q % 2]
                for m in range(4):
                    for c in range(2):
                        last = eng.matmul(bank[:, m * P:(m + 1) * P], sh_hid[:, c * 512 + m * P:c * 512 + (m + 1) * P],
                                          shared_w[:, 2 * HID + c * D:2 * HID + (c + 1) * D], start=(c == 0), stop=(c == 1))
                last.then_inc(sh_made, 1)

            eng.wait_ge(r_sb, counts.after(r_sb, 2))
            eng.matmul(out_ps[:, :], earlier[:, :], chosen, start=True, stop=True)
            eng.matmul(post_ps[:, :], ones_b[:, :], chosen, start=True, stop=True).then_inc(r_ps, 1)
            for q in range(NT // 4):
                if q >= 2:
                    eng.wait_ge(sh_summed, counts.after(sh_summed))
                shared(q)
            eng.wait_ge(sh_summed, counts.after(sh_summed, 2))

            def turn_rows(n):
                eng.wait_ge(weights_in[n], turn_rows.arrived)
                for j in range(SLOT_J):
                    last = eng.transpose(turn_ps[:, j * SLOT_P:(j + 1) * SLOT_P], ex_rows[n][:, j * P:(j + 1) * P],
                                         eye[0:SLOT_P, 0:SLOT_P])
                last.then_inc(rows_turned, 1)

            def up(bank, part, n, full):
                w = ew[n][:, part * HID:(part + 1) * HID]
                for c in range(2):
                    last = eng.matmul(bank[:, c, 0:CAP], w[:, c::2], ex_t[n % 2], start=True, stop=True)
                last.then_inc(full, 1)

            def down(n):
                if copied[0]:
                    eng.wait_ge(out_rows, counts.after(out_rows))
                copied[0] = True
                for j in range(SLOT_J):
                    for c in range(2):
                        last = eng.matmul(pre_ps[0:SLOT_P, j * D:(j + 1) * D],
                                          ex_h[n % 2][:, c * CAP + j * SLOT_P:c * CAP + (j + 1) * SLOT_P],
                                          ew[n][:, 2 * HID + c * D:2 * HID + (c + 1) * D], start=(c == 0), stop=(c == 1))
                last.then_inc(downed, 1)

            def step(n, round_, first=False, last=False):
                eng.wait_ge(rows_copied, counts.after(rows_copied))
                if not first:
                    eng.wait_ge(silued, counts.after(silued))
                up(score_ps[0], 0, n, gate_made)
                if not first:
                    eng.wait_ge(gated, counts.after(gated))
                up(score_ps[1], 1, n, up_made)
                if not first:
                    down((n - 1) % RING)
                if not last:
                    turn_rows.arrived = round_(n + 1)
                    turn_rows((n + 1) % RING)

            copied = [False]
            turn_rows.arrived = 64
            turn_rows(0)
            once = lambda m: 64 * (1 + m // RING)
            step(0, once, first=True)
            for n in range(1, RING):
                step(n, once)
            with counts.loop(E // RING - 2) as i:
                for n in range(RING):
                    step(n, lambda m: i * 64 + 64 * (2 + m // RING))
            for n in range(RING):
                step(n, lambda m: 64 * (E // RING), last=(n == RING - 1))
            eng.wait_ge(gated, counts.after(gated))
            down(RING - 1)

        @block.scalar
        def _(eng):
            counts = Counts("scalar", eng, per)

            def turn_x(L, b, par, k):
                eng.wait_ge(x_turned, counts.after(x_turned))
                n = S + C if L.cross else S
                if L is WIDE:
                    eng.activation(xt[:, 0:S], pre_ps[:, 0:S], ACT.Identity, scale=ln_wb[:, 0:1], bias=ln_wb[:, 1:2])
                    ins = eng.activation(xt[:, S:n], pre_ps[:, S:n], ACT.Identity, scale=ln_wb[:, 2:3], bias=ln_wb[:, 3:4])
                elif L.rms:
                    ins = eng.activation(xt[:, 0:n], pre_ps[:, 0:n], ACT.Copy, scale=norm_w[L.name][:, 0:1])
                else:
                    ins = eng.activation(xt[:, 0:n], pre_ps[:, 0:n], ACT.Copy)
                ins.then_inc(xt_ready, 1)

            def copy_turned(dst, n, bank):
                eng.wait_ge(turned, counts.after(turned))
                ins = eng.activation(dst, turn_banks[bank][:, 0:n], ACT.Copy)
                ins.then_inc(operands, 1)

            def turn_q(L, b, par, k):
                copy_turned(qt[par][:, (k % 2) * 4 * S:(k % 2 + 1) * 4 * S], 4 * S, k % 2)

            def turn_k(L, b, par, k):
                n = L.ktiles * L.keys * L.key_tiles
                for first in range(0, n, 4 * S):
                    m = min(n - first, 4 * S)
                    copy_turned(kt_[par][:, first:first + m], m, first // (4 * S))

            def scores(L, b, par, k):
                g, kt, q0, q1 = L.steps[k]
                eng.wait_ge(scored, counts.after(scored))
                eng.wait_ge(probs_free, counts.after(probs_free))
                src = score_ps[k % 2][0:L.keys, :, :].rearrange("p s (u q) -> p (s u) q", u=2)[:, :, q0:q1]
                dst = probs[k % PROBS][0:L.keys, :].rearrange("p (j q) -> p j q", q=S)[:, :, q0:q1]
                eng.activation(dst, src, ACT.Exp, scale=SCALE).then_inc(probs_ready, 1)

            def output(L, b, par, k):
                eng.wait_ge(merged_turned, counts.after(merged_turned))
                eng.activation(ont[:, :], post_ps[:, 0:TILES * D], ACT.Copy).then_inc(ont_ready, 1)

            def wide_project(L, b, par, k):
                if k % 2:
                    eng.wait_ge(wide_made, counts.after(wide_made, 2))
                    dst, src, scale = wide_copy(L, par, k)
                    eng.activation(dst, src, ACT.Copy, scale=scale).then_inc(wide_a, 1)

            def wide_exp(L, b, par, k):
                eng.wait_ge(topped, counts.after(topped))
                dst = wprobs[k % WPROBS]
                for n in range(TILES):
                    at = 2 * (k % WPROBS) + n
                    last = eng.activation(dst[:, n * WKEYS:(n + 1) * WKEYS], score_ps[k % 2][:, n, 0:WKEYS], ACT.Exp,
                                          bias=wtop[:, at:at + 1], accum_out=wden[:, at:at + 1])
                last.then_inc(exped, 1)

            def wide_turn(L, b, par, k):
                eng.wait_ge(probs_turned, counts.after(probs_turned))
                eng.activation(wturned[k % WTURNED][:, 0:2 * S], out_ps[:, :], ACT.Copy).then_inc(turned_a, 1)

            def wide_values(L, b, par, k):
                eng.wait_ge(pair_summed, counts.after(pair_summed))
                eng.activation(wout_t[:, k * S:(k + 1) * S], pre_ps[:, 0:S], ACT.Copy).then_inc(pair_out, 1)

            for n, L in enumerate(layers):
                if L.rms or L is WIDE:
                    eng.wait_ge(loaded[L.name], loads_of(L))
                run_layer(L, counts, dict(turn_x=turn_x, turn_q=turn_q, turn_k=turn_k, scores=scores, output=output,
                                          wide_project=wide_project, wide_exp=wide_exp, wide_turn=wide_turn,
                                          wide_values=wide_values))
            if not experts:
                return

            eng.wait_ge(exps_asked, 1)
            eng.activation(gates, gates, ACT.Exp).then_inc(exps_made, 1)
            for q in range(NT // 4):
                eng.wait_ge(sh_made, counts.after(sh_made))
                if q:
                    eng.wait_ge(sh_gated, q)
                eng.activation(sh_gate.rearrange("p (c n) -> p c n", c=2), score_ps[0][:, :, :], ACT.Silu).then_inc(sh_silu, 1)
                eng.wait_ge(sh_made, counts.after(sh_made, 2))

            def activate(m):
                eng.wait_ge(gate_made, counts.after(gate_made))
                eng.activation(ex_g[m % 2].rearrange("p (c n) -> p c n", c=2), score_ps[0][:, :, 0:CAP], ACT.Silu)\
                   .then_inc(silued, 1)

            def copy_out(n, value):
                eng.wait_ge(downed, counts.after(downed))
                if value is not None:
                    eng.wait_ge(results_out[n], value)
                eng.activation(ex_out[n], pre_ps[0:SLOT_P, :], ACT.Copy).then_inc(out_rows, 1)

            activate(0)
            for n in range(1, RING):
                activate(n)
                copy_out(n - 1, None)
            activate(0)
            copy_out(RING - 1, None)
            for n in range(1, RING):
                activate(n)
                copy_out(n - 1, 16)
            with counts.loop(E // RING - 2) as i:
                for n in range(RING):
                    activate(n)
                    copy_out((n - 1) % RING, i * 16 + (32 if n else 16))
            copy_out(RING - 1, 16 * (E // RING - 1))

        @block.vector
        def _(eng):
            counts = Counts("vector", eng, per)

            for buf in (stack_words, vals_all, qk, wmv):
                eng.memset(buf[:, :], 0.0).then_inc(v_step, 1)
                eng.wait_ge(v_step, counts.after(v_step))
            eng.memset(k_stack[:, :].rearrange("p (n s) -> p n s", s=PART)[:, :, ROWS:ROWS_MAX], 1.0).then_inc(zeroed, 1)
            for n in range(2):
                eng.memset(vals[n][:, :].rearrange("p (n c) -> p n c", c=32)[:, :, HD:HD + 1], 1.0).then_inc(zeroed, 1)
            eng.wait_ge(setup_ps, counts.after(setup_ps))
            eng.tensor_copy(weights["g"][:, D:D + 2 * KVH * HD], pre_ps[:, 0:2 * KVH * HD]).then_inc(setup_sb, 1)
            eng.wait_ge(loaded["mask"], 16)
            eng.tensor_scalar(given[:, :], given8[:, :], -NEG, NEG, ALU.mult, ALU.add).then_inc(setup_sb, 1)
            eng.wait_ge(zeroed, 4)
            for half_ in range(2):
                eng.wait_ge(setup_ps, counts.after(setup_ps))
                ins = eng.tensor_copy(given_t[0:C, half_ * 8 * P:(half_ + 1) * 8 * P], turn_ps[:, :].bitcast(BF16)[0:C, :])
                ins.then_inc(setup_sb if half_ == 0 else zeroed, 1)

            def wide_tiles(b, par):
                src = rows_of(xb, b)
                return [(src[:, 0:D], xs[par][:, 0:D], P), (src[:, D:2 * D], xs[par][:, D:2 * D], P),
                        (ctx_all[:, bass.ts(b, D)], xc[:, :], C)]

            def norm(L, b, par, k):
                src = rows_of(x0 if L.name == "g" else xb, b)
                if L is WIDE:
                    tiles = wide_tiles(b, par)
                    for n, (a, _, m) in enumerate(tiles):
                        eng.bn_stats(wstats[0:m, 6 * n:6 * n + 6], a).then_inc(v_step, 1)
                        counts.moved(v_step)
                    eng.wait_ge(v_step, counts.after(v_step, 0))
                    eng.sem_inc(waited, 1)
                    for n, (_, _, m) in enumerate(tiles):
                        eng.bn_aggr(wmv[0:m, 2 * n:2 * n + 2], wstats[0:m, 6 * n:6 * n + 6]).then_inc(v_step if n < 2 else pow_asked, 1)
                        counts.moved(v_step if n < 2 else pow_asked)
                    eng.wait_ge(v_step, counts.after(v_step, 0))
                    return
                if L.cross:
                    eng.tensor_copy(xc[:, :], ctx_all[:, bass.ts(b, D)]).then_inc(v_step, 1)
                    eng.wait_ge(v_step, counts.after(v_step))
                if L.rms:
                    eng.tensor_tensor(sq[:, :], src, src, ALU.mult).then_inc(v_step, 1)
                    eng.wait_ge(v_step, counts.after(v_step))
                    eng.tensor_reduce(ss[:, :], sq[:, :].rearrange("p (t d) -> p t d", d=D), AX_X, ALU.add).then_inc(pow_asked, 1)

            def normed(L, b, par, k):
                src = rows_of(x0 if L.name == "g" else xb, b)
                if L is WIDE:
                    eng.wait_ge(pow_done, counts.after(pow_done))
                    for n, (a, dst, m) in enumerate(wide_tiles(b, par)):
                        eng.tensor_scalar(dst, a, wmv[0:m, 2 * n:2 * n + 1], wrs[0:m, n:n + 1],
                                          ALU.subtract, ALU.mult).then_inc(v_step if n < 2 else x_rows, 1)
                        counts.moved(v_step if n < 2 else x_rows)
                    eng.wait_ge(v_step, counts.after(v_step, 0))
                    return
                if not L.rms:
                    eng.tensor_copy(xs[par][:, :], src).then_inc(x_rows, 1)
                    return
                eng.wait_ge(pow_done, counts.after(pow_done))
                eng.tensor_tensor(xs[par][:, :].rearrange("p (t d) -> p t d", d=D), src.rearrange("p (t d) -> p t d", d=D),
                                  rs[:, :].unsqueeze(2).broadcast_to([P, TILES, D]), ALU.mult).then_inc(x_rows, 1)

            def project(L, b, par, k):
                eng.wait_ge(projected, counts.after(projected))
                q_dst = qk[:, 0:TILES * D].rearrange("p (t d) -> p t d", d=D)
                k_dst = qk[:, TILES * D:L.flat].rearrange("p (t d) -> p t d", d=L.kn)
                src = pre_ps[:, 0:TILES * (D + L.kn)].rearrange("p (t d) -> p t d", t=TILES)
                if L.cross:
                    bi = bias_in[L.name]
                    eng.tensor_tensor(q_dst, pre_ps[:, 0:TILES * D].rearrange("p (t d) -> p t d", d=D),
                                      bi[:, 0:D].unsqueeze(1).broadcast_to([P, TILES, D]), ALU.add)
                    last = eng.tensor_tensor(qk[0:C, TILES * D:L.flat], pre_ps[0:C, 2 * D:3 * D], bi[0:C, D:2 * D], ALU.add)
                elif L.bias:
                    bi = bias_in[L.name]
                    eng.tensor_tensor(q_dst, src[:, :, 0:D], bi[:, 0:D].unsqueeze(1).broadcast_to([P, TILES, D]), ALU.add)
                    last = eng.tensor_tensor(k_dst, src[:, :, D:2 * D], bi[:, D:2 * D].unsqueeze(1).broadcast_to([P, TILES, D]),
                                             ALU.add)
                else:
                    eng.tensor_copy(q_dst, src[:, :, 0:D])
                    last = eng.tensor_copy(k_dst, src[:, :, D:D + L.kn])
                last.then_inc(pre_read, 1)
                counts.moved(pre_read)
                eng.wait_ge(pre_read, counts.after(pre_read, 0))

            def project_v(L, b, par, k):
                eng.wait_ge(projected, counts.after(projected))
                v = vals[par][0:L.keys, :].rearrange("p (t h c) -> p t h c", t=TILES, c=32)
                for n in range(L.key_tiles):
                    src = turn_ps[0:L.keys, n * L.kn:(n + 1) * L.kn].rearrange("p (h c) -> p h c", c=HD)
                    if L.bias:
                        last = eng.tensor_tensor(v[:, n, 0:L.kvh, 0:HD], src, bias_in[L.name][0:L.keys, 2 * D:3 * D]
                                                 .rearrange("p (h c) -> p h c", c=HD), ALU.add)
                    else:
                        last = eng.tensor_copy(v[:, n, 0:L.kvh, 0:HD], src)
                last.then_inc(v_step, 1)
                counts.moved(v_step)

            def cut(L, b, par, k):
                n, m = L.flat, L.flat // HD
                src = qk[:, 0:n]
                by_head = src.rearrange("p (n c) -> p n c", c=HD)
                if k == 0 and L.rope:
                    eng.tensor_tensor(qk2[:, 0:n], src, cos[L.name][:, :], ALU.mult).then_inc(v_step, 1)
                    counts.moved(v_step)
                    eng.tensor_tensor(qk3[:, 0:n].rearrange("p (n two) -> p n two", two=2),
                                      src.rearrange("p (n two) -> p n two", two=2)[:, :, ::-1],
                                      sin[L.name][:, :].rearrange("p (n two) -> p n two", two=2), ALU.mult).then_inc(v_step, 1)
                    eng.wait_ge(v_step, counts.after(v_step))
                    eng.tensor_tensor(src, qk2[:, 0:n], qk3[:, 0:n], ALU.add).then_inc(v_step, 1)
                    eng.wait_ge(v_step, counts.after(v_step))
                if k == 0 and L.qk_norm:
                    eng.tensor_tensor(qk2[:, 0:n], src, src, ALU.mult).then_inc(v_step, 1)
                    eng.wait_ge(v_step, counts.after(v_step))
                    eng.tensor_reduce(nss[:, 0:m], qk2[:, 0:n].rearrange("p (n c) -> p n c", c=HD), AX_X, ALU.add)\
                       .then_inc(pow_asked, 1)
                if k == 1 and L.qk_norm:
                    eng.wait_ge(pow_done, counts.after(pow_done))
                    eng.tensor_tensor(by_head, by_head, nrs[:, 0:m].unsqueeze(2).broadcast_to([P, m, HD]), ALU.mult)\
                       .then_inc(v_step, 1)
                    eng.wait_ge(v_step, counts.after(v_step))
                if k == 1:
                    eng.tensor_copy(cuts[0][:, 0:n], src).then_inc(v_step, 1)
                    eng.wait_ge(v_step, counts.after(v_step))
                    eng.tensor_tensor(qk2[:, 0:n], src, cuts[0][:, 0:n], ALU.subtract).then_inc(v_step, 1)
                    eng.wait_ge(v_step, counts.after(v_step))
                if k == 2:
                    eng.tensor_copy(cuts[1][:, 0:n], qk2[:, 0:n]).then_inc(v_step, 1)
                    eng.wait_ge(v_step, counts.after(v_step))
                    eng.tensor_tensor(cuts[2][:, 0:n], qk2[:, 0:n], cuts[1][:, 0:n], ALU.subtract).then_inc(v_step, 1)
                    eng.wait_ge(v_step, counts.after(v_step))
                if k != 3:
                    return
                if not (isinstance(b, int) and b == 0):
                    eng.wait_ge(operands, counts.after(operands, L.turns))
                q_slots = (slice(0, 3), slice(3, 6, 2), slice(4, 5))
                k_slots = (slice(2, 5), slice(0, 6, 5), slice(1, 2))
                for stack, slots, first, m in ((q_stack, q_slots, 0, TILES * H),
                                               (k_stack, k_slots, TILES * D, L.key_tiles * L.kvh)):
                    dst = stack[:, 0:m * PART].rearrange("p (n s c) -> p n s c", s=PART // HD, c=HD)
                    for part in range(3):
                        out = dst[:, :, slots[part], :]
                        last = eng.tensor_copy(out, cuts[part][:, first:first + m * HD].rearrange("p (n c) -> p n c", c=HD)
                                               .unsqueeze(2).broadcast_to([P, m, out.shape[2], HD]))
                last.then_inc(stacked, 1)
                counts.moved(stacked)
                eng.wait_ge(stacked, counts.after(stacked, 0))

            def top(L, b, par, k):
                q, side, u0, m, n = L.top_steps[k]
                bank, full, read = ((pre_ps, top_a, pre_read), (turn_ps, top_b, turn_read))[k % 2]
                eng.wait_ge(full, counts.after(full))
                dst = tops[:, q * H:(q + 1) * H].rearrange("p (u s) -> p u s", s=2)[:, u0:u0 + m, side]
                src = bank[:, 0:m * n].rearrange("p (m n) -> p m n", n=n)
                eng.tensor_reduce(dst, src, AX_X, ALU.max).then_inc(read, 1)
                counts.moved(read)

            def shift(L, b, par, k):
                eng.wait_ge(pre_read, counts.after(pre_read, 0))
                eng.wait_ge(turn_read, counts.after(turn_read, 0))
                slot = q_stack[:, :].rearrange("p (n s) -> p n s", s=PART)
                one = [slot[:, :, ROWS + n] for n in range(3)]
                eng.tensor_scalar(tops[:, :], tops[:, :], -1.0, None, ALU.mult).then_inc(v_step, 1)
                eng.wait_ge(v_step, counts.after(v_step))
                eng.tensor_copy(one[0], tops[:, :]).then_inc(v_step, 1)
                eng.wait_ge(v_step, counts.after(v_step))
                eng.tensor_tensor(top2[:, :], tops[:, :], one[0], ALU.subtract).then_inc(v_step, 1)
                eng.wait_ge(v_step, counts.after(v_step))
                eng.tensor_copy(one[1], top2[:, :]).then_inc(v_step, 1)
                eng.wait_ge(v_step, counts.after(v_step))
                ins = eng.tensor_tensor(one[2], top2[:, :], one[1], ALU.subtract)
                ins.then_inc(shifted, 1)
                counts.moved(shifted)
                eng.wait_ge(shifted, counts.after(shifted, 0))

            def values(L, b, par, k):
                eng.wait_ge(probs_free, counts.after(probs_free, len(L.steps) // 4))
                eng.tensor_copy(ot[:, k * S:(k + 1) * S], sums_ps[k % 2][:, 0:S]).then_inc(ot_ready, 1)

            def merge(L, b, par, k):
                for pair in (k,):
                    eng.wait_ge(rows_back, counts.after(rows_back))
                    src = post_ps[:, :].rearrange("p (n c) -> p n c", c=32)
                    eng.reciprocal(rden[:, :].unsqueeze(2), src[:, :, HD:HD + 1]).then_inc(v_step, 1)
                    eng.wait_ge(v_step, counts.after(v_step))
                    dst = on[:, :].rearrange("p (t g n c) -> p t g n c", t=TILES, g=2, c=HD)[:, :, pair, :, :]
                    ins = eng.tensor_tensor(dst, src[:, :, 0:HD].rearrange("p (t n) c -> p t n c", t=TILES),
                                            rden[:, :].rearrange("p (t n) -> p t n", t=TILES).unsqueeze(3)
                                            .broadcast_to([P, TILES, 8, HD]), ALU.mult)
                    ins.then_inc(merged, 1)
                    counts.moved(merged)
                    eng.wait_ge(merged, counts.after(merged, 0))

            def statistics():
                for n in range(TILES):
                    last = eng.bn_stats(stats[:, 6 * n:6 * n + 6], y[:, n * D:(n + 1) * D])
                last.then_inc(v_step, 1)
                eng.wait_ge(v_step, counts.after(v_step))
                eng.sem_inc(waited, 1)
                for n in range(TILES):
                    last = eng.bn_aggr(mv[:, 2 * n:2 * n + 2], stats[:, 6 * n:6 * n + 6])
                last.then_inc(pow_asked, 1)
                counts.moved(pow_asked)
                eng.wait_ge(pow_asked, counts.after(pow_asked, 0))

            def finished(L, b, par, k):
                if L.name == "g":
                    return
                eng.wait_ge(pow_done, counts.after(pow_done))
                dst = rows_of(xb, b)
                for n in range(TILES):
                    last = eng.tensor_scalar(dst[:, n * D:(n + 1) * D], y[:, n * D:(n + 1) * D], mv[:, 2 * n:2 * n + 1],
                                             lrs[:, n:n + 1], ALU.subtract, ALU.mult)
                last.then_inc(v_step, 1)
                eng.wait_ge(v_step, counts.after(v_step))

            def output(L, b, par, k):
                eng.wait_ge(out_projected, counts.after(out_projected))
                src = rows_of(x0 if L.name == "g" else xb, b)
                acc = post_ps[:, 0:TILES * D]
                if L.name == "g":
                    eng.tensor_tensor(rows_of(xb, b), acc, src, ALU.add).then_inc(post_read, 1)
                    counts.moved(post_read)
                    eng.wait_ge(post_read, counts.after(post_read, 0))
                    return
                eng.tensor_tensor(y[:, :], acc, src, ALU.add).then_inc(post_read, 1)
                counts.moved(post_read)
                eng.wait_ge(post_read, counts.after(post_read, 0))
                if L.name == "l":
                    eng.tensor_tensor(y[:, :], y[:, :], rows_of(x0, b), ALU.add).then_inc(v_step, 1)
                    eng.wait_ge(v_step, counts.after(v_step))
                else:
                    eng.tensor_tensor(y[:, :].rearrange("p (t d) -> p t d", d=D), y[:, :].rearrange("p (t d) -> p t d", d=D),
                                      bias_out[L.name][:, :].unsqueeze(1).broadcast_to([P, TILES, D]), ALU.add).then_inc(v_step, 1)
                    eng.wait_ge(v_step, counts.after(v_step))
                statistics()

            def mixed(L, b, par, k):
                eng.wait_ge(projected, counts.after(projected))
                eng.tensor_tensor(y[:, :], pre_ps[:, 0:TILES * D], rows_of(xb, b), ALU.add).then_inc(pre_read, 1)
                counts.moved(pre_read)
                eng.wait_ge(pre_read, counts.after(pre_read, 0))
                eng.tensor_tensor(y[:, :].rearrange("p (t d) -> p t d", d=D), y[:, :].rearrange("p (t d) -> p t d", d=D),
                                  bias_mix[:, :].unsqueeze(1).broadcast_to([P, TILES, D]), ALU.add).then_inc(v_step, 1)
                eng.wait_ge(v_step, counts.after(v_step))
                statistics()

            def wide_project(L, b, par, k):
                if k % 2 == 0:
                    eng.wait_ge(wide_made, counts.after(wide_made, 2 if k else 1))
                    dst, src, scale = wide_copy(L, par, k)
                    eng.tensor_scalar(dst, src, scale, None, ALU.mult).then_inc(wide_v, 1)
                    if k == len(L.products) - 2:
                        eng.wait_ge(wide_made, counts.after(wide_made))

            def wide_scores(L, b, par, k):
                eng.wait_ge(wide_scored, counts.after(wide_scored))
                at = 2 * (k % WPROBS)
                eng.tensor_reduce(wtop[:, at:at + 2], score_ps[k % 2][:, :, 0:WKEYS], AX_X, ALU.max, negate=True)\
                   .then_inc(topped, 1)

            def wide_scale(L, b, par, k):
                eng.wait_ge(exped, counts.after(exped))
                at = 2 * (k % WPROBS)
                eng.reciprocal(wrden[:, at:at + 2], wden[:, at:at + 2]).then_inc(v_step, 1)
                eng.wait_ge(v_step, counts.after(v_step))
                for n in range(TILES):
                    src = wprobs[k % WPROBS][:, n * WKEYS:(n + 1) * WKEYS]
                    last = eng.tensor_scalar(src, src, wrden[:, at + n:at + n + 1], None, ALU.mult)
                last.then_inc(scaled, 1)

            def wide_turn(L, b, par, k):
                eng.wait_ge(probs_turned, counts.after(probs_turned))
                eng.tensor_copy(wturned[k % WTURNED][0:C, 2 * S:3 * S], post_ps[0:C, 0:S]).then_inc(turned_c, 1)

            def wide_output(L, b, par, k):
                eng.wait_ge(out_projected, counts.after(out_projected))
                eng.tensor_tensor(y[:, :], post_ps[:, 0:TILES * D], rows_of(xb, b), ALU.add).then_inc(post_read, 1)
                counts.moved(post_read)
                eng.wait_ge(post_read, counts.after(post_read, 0))
                statistics()

            eng.sem_inc(probs_free, PROBS)
            counts.moved(probs_free, PROBS)
            eng.sem_inc(post_read, 1)
            counts.moved(post_read)
            eng.wait_ge(loaded["x"], 16)
            eng.wait_ge(loaded["ctx"], 16)
            for n, L in enumerate(layers):
                eng.wait_ge(loaded["x_" if L.name == "x" else L.name], loads_of(L))
                if L is MIXING:
                    eng.wait_ge(setup_ps, counts.after(setup_ps))
                    eng.tensor_copy(freq_a[:, :], out_ps[:, 0:2 * D]).then_inc(setup_sb, 1)
                    eng.wait_ge(setup_ps, counts.after(setup_ps))
                    eng.tensor_copy(mix_w[:, :], out_ps[:, 0:D]).then_inc(setup_sb, 1)
                run_layer(L, counts, dict(norm=norm, project=project, project_v=project_v, cut=cut, top=top, shift=shift, values=values,
                                          merge=merge, output=output, mixed=mixed,
                                          wide_project=wide_project, wide_scores=wide_scores, wide_scale=wide_scale,
                                          wide_turn=wide_turn, wide_output=wide_output, normed=normed, finished=finished))
                if L not in (MIXING, WIDE):
                    eng.wait_ge(operands, counts.after(operands, L.turns))
            if not experts:
                eng.tensor_copy(rden[:, 0:1], rden[:, 0:1]).then_inc(stored, 1)
                return

            eng.wait_ge(exp_loaded, 16 * 6)
            eng.tensor_tensor(cent_sq[:, :], centroids[:, :], centroids[:, :], ALU.mult).then_inc(v_step, 1)
            eng.wait_ge(v_step, counts.after(v_step))
            eng.tensor_reduce(cent_s[:, 0:1], cent_sq[:, :], AX_X, ALU.add).then_inc(pow_asked, 1)
            counts.moved(pow_asked)
            eng.wait_ge(pow_done, counts.after(pow_done))
            eng.tensor_scalar(cent_s[:, 2:3], cent_s[:, 1:2], 1e-12, None, ALU.max).then_inc(v_step, 1)
            eng.wait_ge(v_step, counts.after(v_step))
            eng.reciprocal(cent_s[:, 3:4], cent_s[:, 2:3]).then_inc(v_step, 1)
            eng.wait_ge(v_step, counts.after(v_step))
            eng.tensor_scalar(centroids[:, :], centroids[:, :], cent_s[:, 3:4], None, ALU.mult).then_inc(r_sb, 1)
            counts.moved(r_sb)
            tokens = xb[:, :].rearrange("p (t d) -> p t d", d=D)
            eng.tensor_tensor(acc, xb[:, :], xb[:, :], ALU.mult).then_inc(v_step, 1)
            eng.wait_ge(v_step, counts.after(v_step))
            eng.tensor_reduce(small[:, 0:NT], acc.rearrange("p (t d) -> p t d", d=D), AX_X, ALU.add).then_inc(pow_asked, 1)
            counts.moved(pow_asked)
            eng.wait_ge(r_ps, counts.after(r_ps))
            eng.tensor_copy(cent_t[:, :], out_ps[:, 0:G + E]).then_inc(v_step, 1)
            eng.wait_ge(v_step, counts.after(v_step))
            for q in range(NT // 4):
                eng.wait_ge(r_ps, counts.after(r_ps))
                eng.tensor_copy(xt_all[:, q * 512:(q + 1) * 512], (pre_ps, turn_ps)[q % 2][:, :]).then_inc(r_sb, 1)
                counts.moved(r_sb)
            eng.wait_ge(pow_done, counts.after(pow_done))
            eng.tensor_scalar(small[:, 2 * NT:3 * NT], small[:, NT:2 * NT], 1e-12, None, ALU.max).then_inc(v_step, 1)
            eng.wait_ge(v_step, counts.after(v_step))
            eng.reciprocal(small[:, 3 * NT:4 * NT], small[:, 2 * NT:3 * NT]).then_inc(v_step, 1)
            eng.wait_ge(v_step, counts.after(v_step))
            inverse = small[:, 3 * NT:4 * NT]
            eng.wait_ge(r_ps, counts.after(r_ps))
            for half_ in range(2):
                src = score_ps[0][:, half_, 0:8 * (G + E)].rearrange("p (t n) -> p t n", n=G + E)
                inv = inverse[:, half_ * 8:half_ * 8 + 8].unsqueeze(2)
                eng.tensor_tensor(g_score[:, half_ * 8 * G:(half_ + 1) * 8 * G].rearrange("p (t n) -> p t n", n=G),
                                  src[:, :, 0:G], inv.broadcast_to([P, 8, G]), ALU.mult)
                last = eng.tensor_tensor(e_score[:, half_ * 8 * E:(half_ + 1) * 8 * E].rearrange("p (t n) -> p t n", n=E),
                                         src[:, :, G:], inv.broadcast_to([P, 8, E]), ALU.mult)
            last.then_inc(r_sb, 1)
            counts.moved(r_sb)
            eng.wait_ge(r_sb, counts.after(r_sb, 0))
            by_tile = e_score.rearrange("p (t n) -> p t n", n=E)
            eng.tensor_tensor(by_tile, by_tile, choice_bias[:, :].unsqueeze(1).broadcast_to([P, NT, E]), ALU.add).then_inc(v_step, 1)
            counts.moved(v_step)
            other = g_score.rearrange("p (t j) -> p t j", j=G).unsqueeze(2).broadcast_to([P, NT, G, G])
            own = g_score.rearrange("p (t i) -> p t i", i=G).unsqueeze(3).broadcast_to([P, NT, G, G])
            gt4, eq4 = (m.rearrange("p (t i j) -> p t i j", i=G, j=G) for m in (cmp_gt, cmp_eq))
            eng.tensor_tensor(gt4, other, own, ALU.is_gt).then_inc(v_step, 1)
            counts.moved(v_step)
            eng.tensor_tensor(eq4, other, own, ALU.is_equal).then_inc(v_step, 1)
            eng.wait_ge(v_step, counts.after(v_step))
            eng.tensor_tensor(cmp_eq.rearrange("p (t n) -> p t n", n=G * G), cmp_eq.rearrange("p (t n) -> p t n", n=G * G),
                              before[:, :].unsqueeze(1).broadcast_to([P, NT, G * G]), ALU.mult).then_inc(v_step, 1)
            eng.wait_ge(v_step, counts.after(v_step))
            eng.tensor_tensor(cmp_gt, cmp_gt, cmp_eq, ALU.add).then_inc(v_step, 1)
            eng.wait_ge(v_step, counts.after(v_step))
            eng.tensor_reduce(rank, cmp_gt.rearrange("p (n j) -> p n j", j=G), AX_X, ALU.add).then_inc(v_step, 1)
            eng.wait_ge(v_step, counts.after(v_step))
            eng.tensor_scalar(rank, rank, float(G // 2), None, ALU.is_lt).then_inc(v_step, 1)
            eng.wait_ge(v_step, counts.after(v_step))
            per_group = [P, NT * G, E // G]
            eng.tensor_tensor(e_score.rearrange("p (n m) -> p n m", m=E // G), e_score.rearrange("p (n m) -> p n m", m=E // G),
                              rank.unsqueeze(2).broadcast_to(per_group), ALU.mult).then_inc(v_step, 1)
            eng.wait_ge(v_step, counts.after(v_step))
            eng.tensor_scalar(rank, rank, 1e9, -1e9, ALU.mult, ALU.add).then_inc(v_step, 1)
            eng.wait_ge(v_step, counts.after(v_step))
            eng.tensor_tensor(masked.rearrange("p (n m) -> p n m", m=E // G), e_score.rearrange("p (n m) -> p n m", m=E // G),
                              rank.unsqueeze(2).broadcast_to(per_group), ALU.add).then_inc(v_step, 1)
            eng.wait_ge(v_step, counts.after(v_step))
            for tile in range(NT):
                last = eng.max(top8[:, tile * 8:(tile + 1) * 8], masked[:, tile * E:(tile + 1) * E])
            last.then_inc(v_step, 1)
            eng.wait_ge(v_step, counts.after(v_step))
            for tile in range(NT):
                last = eng.max_index(idx8.bitcast(U32)[:, tile * 8:(tile + 1) * 8], top8[:, tile * 8:(tile + 1) * 8],
                                     masked[:, tile * E:(tile + 1) * E])
            last.then_inc(v_step, 1)
            eng.wait_ge(v_step, counts.after(v_step))
            top4 = top8.rearrange("p (t n) -> p t n", n=8)
            by_k = gates.rearrange("p (t k) -> p t k", k=K)
            eng.tensor_tensor(by_k, top4[:, :, 0:K], top4[:, :, 0:1].broadcast_to([P, NT, K]), ALU.subtract).then_inc(exps_asked, 1)
            counts.moved(exps_asked)
            eng.tensor_copy(idx_f.rearrange("p (t k) -> p t k", k=K),
                            idx8.bitcast(U32).rearrange("p (t n) -> p t n", n=8)[:, :, 0:K]).then_inc(v_step, 1)
            eng.wait_ge(v_step, counts.after(v_step))
            eng.tensor_tensor(onehot.rearrange("p (n e) -> p n e", e=E), iota_e[:, :].unsqueeze(1).broadcast_to([P, NT * K, E]),
                              idx_f.unsqueeze(2).broadcast_to([P, NT * K, E]), ALU.is_equal).then_inc(v_step, 1)
            eng.wait_ge(v_step, counts.after(v_step))
            with nc.allow_low_precision(reason="sums of at most one are exact"):
                eng.tensor_reduce(chosen.rearrange("p (t e) -> p t e", e=E),
                                  onehot.rearrange("p (t k e) -> p t e k", k=K, e=E), AX_X, ALU.add).then_inc(r_sb, 1)
                counts.moved(r_sb)
            eng.wait_ge(exps_made, counts.after(exps_made))
            eng.tensor_reduce(small[:, 4 * NT:5 * NT], by_k, AX_X, ALU.add).then_inc(v_step, 1)
            eng.wait_ge(v_step, counts.after(v_step))
            eng.reciprocal(small[:, 4 * NT:5 * NT], small[:, 4 * NT:5 * NT]).then_inc(v_step, 1)
            eng.wait_ge(v_step, counts.after(v_step))
            eng.tensor_tensor(by_k, by_k, small[:, 4 * NT:5 * NT].unsqueeze(2).broadcast_to([P, NT, K]), ALU.mult).then_inc(v_step, 1)
            eng.wait_ge(v_step, counts.after(v_step))
            eng.wait_ge(r_ps, counts.after(r_ps))
            eng.memset(ahead[:, 0:E], 0.0).then_inc(v_step, 1)
            eng.wait_ge(v_step, counts.after(v_step))
            eng.tensor_copy(ahead[:, E:], post_ps[:, 0:(NT - 1) * E]).then_inc(v_step, 1)
            eng.wait_ge(v_step, counts.after(v_step))
            a, c = ahead, ahead2
            for shift_ in (1, 2, 4, 8):
                eng.tensor_copy(c[:, 0:shift_ * E], a[:, 0:shift_ * E]).then_inc(v_step, 1)
                counts.moved(v_step)
                eng.tensor_tensor(c[:, shift_ * E:], a[:, shift_ * E:], a[:, 0:(NT - shift_) * E], ALU.add).then_inc(v_step, 1)
                eng.wait_ge(v_step, counts.after(v_step))
                a, c = c, a
            eng.tensor_tensor(totals, a, out_ps[:, :], ALU.add).then_inc(v_step, 1)
            eng.wait_ge(v_step, counts.after(v_step))
            for tile in range(NT):
                span = slice(tile * K * E, (tile + 1) * K * E)
                last = eng.tensor_tensor(picked[:, span].rearrange("p (k e) -> p k e", k=K),
                                         onehot[:, span].rearrange("p (k e) -> p k e", k=K),
                                         totals[:, tile * E:(tile + 1) * E].unsqueeze(1).broadcast_to([P, K, E]), ALU.mult)
            last.then_inc(v_step, 1)
            eng.wait_ge(v_step, counts.after(v_step))
            eng.tensor_reduce(pos, picked.rearrange("p (n e) -> p n e", e=E), AX_X, ALU.add).then_inc(v_step, 1)
            eng.wait_ge(v_step, counts.after(v_step))
            eng.tensor_scalar(keep, pos, float(CAP), None, ALU.is_lt).then_inc(v_step, 1)
            eng.wait_ge(v_step, counts.after(v_step))
            eng.tensor_tensor(gate[:, :], gates, keep, ALU.mult).then_inc(v_step, 1)
            counts.moved(v_step)
            eng.tensor_scalar(keep, keep, -BEYOND, BEYOND, ALU.mult, ALU.add).then_inc(v_step, 1)
            eng.wait_ge(v_step, counts.after(v_step))
            eng.tensor_scalar(idx_f, idx_f, float(CAP), None, ALU.mult).then_inc(v_step, 1)
            eng.wait_ge(v_step, counts.after(v_step))
            eng.tensor_tensor(keep, keep, pos, ALU.add).then_inc(v_step, 1)
            eng.wait_ge(v_step, counts.after(v_step))
            eng.tensor_tensor(slot_in[:, :], keep, idx_f, ALU.add).then_inc(v_step, 1)
            eng.wait_ge(v_step, counts.after(v_step))
            eng.tensor_scalar(pos, pos, float(CAP - 1), None, ALU.min).then_inc(v_step, 1)
            eng.wait_ge(v_step, counts.after(v_step))
            eng.tensor_tensor(slot_out[:, :], pos, idx_f, ALU.add).then_inc(slots_known, 1)

            for q in range(NT // 4):
                eng.wait_ge(sh_made, counts.after(sh_made, 2))
                eng.wait_ge(sh_silu, q + 1)
                eng.tensor_tensor(sh_hid.rearrange("p (c n) -> p c n", c=2), sh_gate.rearrange("p (c n) -> p c n", c=2),
                                  score_ps[1][:, :, :], ALU.mult).then_inc(sh_gated, 1)
                counts.moved(sh_gated)
                eng.wait_ge(sh_made, counts.after(sh_made))
                eng.tensor_tensor(acc[:, q * 512:(q + 1) * 512], (pre_ps, turn_ps)[q % 2][:, :],
                                  xb[:, q * 512:(q + 1) * 512], ALU.add).then_inc(sh_summed, 1)
                counts.moved(sh_summed)
            eng.wait_ge(sh_summed, counts.after(sh_summed, 0))

            def copy_rows(n):
                eng.wait_ge(rows_turned, counts.after(rows_turned))
                eng.tensor_copy(ex_t[n % 2], turn_ps[:, 0:CAP]).then_inc(rows_copied, 1)

            def multiply(n):
                eng.wait_ge(silued, counts.after(silued))
                eng.wait_ge(up_made, counts.after(up_made))
                eng.tensor_tensor(ex_h[n % 2].rearrange("p (c n) -> p c n", c=2), ex_g[n % 2].rearrange("p (c n) -> p c n", c=2),
                                  score_ps[1][:, :, 0:CAP], ALU.mult).then_inc(gated, 1)

            copy_rows(0)
            with counts.loop((E - 2) // 2) as i:
                for n in range(2):
                    multiply(n)
                    copy_rows(n + 1)
            multiply(0)
            copy_rows(1)
            multiply(1)

            for q in range(NT // GROUP):
                eng.wait_ge(gathered_in[q % 2], 16 * GROUP * K * (q // 2 + 1))
                for k in range(K):
                    for m in range(GROUP):
                        tile = q * GROUP + m
                        at = acc[:, tile * D:(tile + 1) * D]
                        last = eng.scalar_tensor_tensor(out=at, in0=gathered[q % 2][:, (m * K + k) * D:(m * K + k + 1) * D],
                                                        scalar=gate[:, tile * K + k:tile * K + k + 1], in1=at,
                                                        op0=ALU.mult, op1=ALU.add)
                        if m == GROUP - 1:
                            last.then_inc(combined if k == K - 1 else v_step, 1)
                            counts.moved(combined if k == K - 1 else v_step)
                    eng.wait_ge(combined if k == K - 1 else v_step, counts.after(combined if k == K - 1 else v_step, 0))
                for m in range(GROUP):
                    tile = q * GROUP + m
                    last = eng.bn_stats(lstats[:, 6 * m:6 * m + 6], acc[:, tile * D:(tile + 1) * D])
                last.then_inc(v_step, 1)
                eng.wait_ge(v_step, counts.after(v_step))
                for m in range(GROUP):
                    last = eng.bn_aggr(lmv[:, 2 * m:2 * m + 2], lstats[:, 6 * m:6 * m + 6])
                last.then_inc(pow_asked, 1)
                counts.moved(pow_asked)
                eng.wait_ge(pow_asked, counts.after(pow_asked, 0))
                eng.wait_ge(pow_done, counts.after(pow_done))
                for m in range(GROUP):
                    tile = slice((q * GROUP + m) * D, (q * GROUP + m + 1) * D)
                    last = eng.tensor_scalar(xb[:, tile], acc[:, tile], lmv[:, 2 * m:2 * m + 1], glrs[:, m:m + 1],
                                             ALU.subtract, ALU.mult)
                last.then_inc(written, 1)


def loads_of(L):
    if L is MIXING:
        return 16 * 8
    if L is WIDE:
        return 16 * 4
    return 16 * ((2 + 2 * L.rope + 2 * L.bias) + L.rms)


def rope_tables(L, base):
    dim = np.arange(HD // 2, dtype=np.float32)
    pos = np.arange(S, dtype=np.float32)[:, None]
    if L.name == "a":
        angle = pos / np.exp(np.float32(2.0) * dim / np.float32(HD) * np.float32(np.log(10000.0)))[None, :]
    else:
        inv = np.float32(1.0) / np.float32(base) ** (np.arange(0, HD, 2, dtype=np.float32) / np.float32(HD))
        angle = pos * inv[None, :]
    angle = angle.astype(np.float32)
    c, s = np.cos(angle), np.sin(angle)
    c2 = np.repeat(c, 2, axis=1)
    s2 = np.stack([-s, s], axis=-1).reshape(S, HD)

    def lay(table):
        q = np.tile(table.reshape(TILES, P, 1, HD), (1, 1, H, 1)).transpose(1, 0, 2, 3).reshape(P, -1)
        k = np.tile(table.reshape(TILES, P, 1, HD), (1, 1, L.kvh, 1)).transpose(1, 0, 2, 3).reshape(P, -1)
        return np.ascontiguousarray(np.concatenate([q, k], axis=1).astype(np.float32))
    return lay(c2), lay(s2)


def merged_rows(w, kv_heads=H):
    return w.reshape(H, HD, D)[[held_heads(kv_heads)[n] for n in MERGED]].reshape(D, D)


def held_columns(w):
    return w.reshape(D, H, HD)[:, held_heads(KVH)].reshape(D, D)


def layout(i):
    cat = np.concatenate
    a = {"x": i["x"], "ctx": i["ctx_1024"], "mask": i["mask_Bx1xSxS2_bf1"].reshape(B, S, C).view(np.uint8),
         "down_t": i["L0_attn_g_kv_down"].T, "ups": cat([i["L0_attn_g_k_up"], i["L0_attn_g_v_up"]], axis=1),
         "w_g": held_columns(i["L0_attn_g_wq"]), "wo_g": merged_rows(i["L0_attn_g_wo"], KVH), "nw_g": i["L0_attn_norm1_w"][:, None],
         "w_l": cat([held_columns(i["L0_attn_l_wq"]), i["L0_attn_l_wk"], i["L0_attn_l_wv"]], axis=1),
         "wo_l": merged_rows(i["L0_attn_l_wo"], KVH), "nw_l": i["L0_attn_norm2_w"][:, None]}
    for name, p, (q, k, v, o) in (("x", "L0_xattn_", ("Wq", "Wk", "Wv", "Wo")), ("a", "L1_attn_", ("wq", "wk", "wv", "wo"))):
        a[f"w_{name}"] = cat([i[p + q].T, i[p + k].T, i[p + v].T], axis=1)
        a[f"wo_{name}"] = merged_rows(i[p + o].T)
        a[f"bi_{name}"] = np.tile(cat([i[p + "bq"], i[p + "bk"], i[p + "bv"]])[None], (P, 1))
        a[f"bo_{name}"] = np.tile(i[p + "bo"][None], (P, 1))
    for L, base in ((NARROW[0], 1e6), (NARROW[1], 1e4), (NARROW[3], 1e4)):
        a[f"cos_{L.name}"], a[f"sin_{L.name}"] = rope_tables(L, base)
    wave = 2.0 * np.pi * (np.outer(np.arange(D), np.arange(D)) % D) / D
    a.update(Fr=np.cos(wave).astype(np.float32), Fi=-np.sin(wave).astype(np.float32), nFi=np.sin(wave).astype(np.float32),
             Gr=(np.cos(wave) / D).astype(np.float32), nGi=-(np.sin(wave) / D).astype(np.float32),
             freq_r=i["L0_ffn_w_freq_real"], freq_i=i["L0_ffn_w_freq_imag"],
             bias_mix=np.tile(i["L0_ffn_bias"][None], (P, 1)),
             wide_q=i["L1_xattn_Wq"], wide_kv=i["L1_xattn_Wkv"], wide_o=i["L1_xattn_Wo"],
             group_c=i["L1_ffn_group_centroids"], expert_c=i["L1_ffn_expert_centroids"],
             choice_bias=np.tile(i["L1_ffn_bias"][None], (P, 1)), sg=i["L1_ffn_sg"], su=i["L1_ffn_su"], sd=i["L1_ffn_sd"],
             wg=i["L1_ffn_wg"].reshape(E * D, HID), wu=i["L1_ffn_wu"].reshape(E * D, HID),
             wd=i["L1_ffn_wd"].reshape(E * P, 2 * D),
             ln_wb=np.stack([i["L1_xattn_ln2_w"], i["L1_xattn_ln2_b"], i["L1_xattn_ln1_w"], i["L1_xattn_ln1_b"]], axis=1))
    return {n: np.ascontiguousarray(v) for n, v in a.items()}


def make_program(nc, arrays, per):
    t = {n: nc.dram_tensor(n, a.shape, mybir.dt.from_np(a.dtype), kind="ExternalInput").ap() for n, a in arrays.items()}
    t["out"] = nc.dram_tensor("out", (B, S, D), F32, kind="ExternalOutput").ap()
    t["slots"] = nc.dram_tensor("slots", (E * CAP, D), F32, kind="Internal").ap()
    t["results"] = nc.dram_tensor("results", (E * CAP, D), F32, kind="Internal").ap()
    build_program(nc, t, per)


def kernel(**inputs):
    import concourse.bacc as bacc
    from concourse.bass_utils import run_bass_kernel_spmd

    arrays = layout({n: np.asarray(a) for n, a in inputs.items()})
    per = {}
    make_program(bacc.Bacc("TRN2", target_bir_lowering=False, num_devices=1), arrays, per)
    nc = bacc.Bacc("TRN2", target_bir_lowering=False, num_devices=1)
    make_program(nc, arrays, per)
    result = run_bass_kernel_spmd(nc, [arrays], core_ids=[0])
    return result.results[0]["out"]
```

```python
from contextlib import ExitStack, contextmanager

import numpy as np

import concourse.bass as bass
from concourse import mybir

ALU = mybir.AluOpType
ACT = mybir.ActivationFunctionType
AX_X = mybir.AxisListType.X
F32 = mybir.dt.float32
BF16 = mybir.dt.bfloat16
I32 = mybir.dt.int32
U32 = mybir.dt.uint32
U8 = mybir.dt.uint8

B, S, D = 8, 256, 128
P = 128
TILES = S // P
C = 64
H, HD = 16, 8
KVH = 4
WIN = 32
PART = 64
ROWS, ROWS_MAX = 6 * HD, 6 * HD + 3
NEG = -1e30
SCALE = 1.0 / float(np.sqrt(HD))


class Counts:

    def __init__(self, name, engine, per):
        self.name, self.engine, self.per = name, engine, per
        self.seen, self.base, self.at, self.loops = {}, {}, None, 0

    def after(self, sem, events=1):
        self.moved(sem, events)
        value = self.seen[sem.name]
        if self.at is not None:
            value = value + self.at * self.per.get((self.name, self.loops, sem.name), 0)
        return value

    def moved(self, sem, events=1):
        self.seen[sem.name] = self.seen.get(sem.name, 0) + events

    def layer(self, events):
        self.events = {sem.name: n for sem, n in events}
        for name, n in self.events.items():
            self.base[name, 1] = self.seen.get(name, 0) - n

    def batch(self, par, *sems):
        for sem in sems:
            self.base[sem.name, par] = self.base[sem.name, 1 - par] + self.events[sem.name]

    def owed(self, sem, par, event):
        return self.base[sem.name, par] + event > self.seen.get(sem.name, 0)

    def until(self, sem, par, event):
        return self.after(sem, self.base[sem.name, par] + event - self.seen.get(sem.name, 0))

    @contextmanager
    def loop(self, count):
        self.loops += 1
        before, base = dict(self.seen), dict(self.base)
        with self.engine.Fori(0, count) as i:
            self.at = i
            yield i
        self.at = None
        for name, value in self.seen.items():
            n = value - before.get(name, 0)
            self.per[(self.name, self.loops, name)] = n
            self.seen[name] = value + n * (count - 1)
        for name, value in self.base.items():
            self.base[name] = value + (value - base.get(name, value)) * (count - 1)


def place(u, side):
    return 2 * u + side


def held_heads(kv_heads):
    if kv_heads == H:
        return list(range(H))
    return [(u // 4) * 8 + side * 4 + u % 4 for u in range(8) for side in range(2)]


MERGED = [place(2 * g + uu, side) for g in range(4) for side in range(2) for uu in range(2)]


class Narrow:

    def __init__(self, name, kv_heads, *, rms=False, rope=False, qk_norm=False, cross=False, bias=False,
                 top=False, mask="causal", norm=True):
        self.name, self.kvh = name, kv_heads
        self.rms, self.rope, self.qk_norm, self.cross = rms, rope, qk_norm, cross
        self.bias, self.top, self.mask, self.norm = bias, top, mask, norm
        self.first = name != "l"
        self.kn = kv_heads * HD
        self.key_tiles = 1 if cross else TILES
        self.keys = C if cross else P
        self.flat = TILES * D + self.key_tiles * self.kn
        self.ktiles = kv_heads // 2
        self.turns = 2 + max(1, self.ktiles * self.keys * self.key_tiles // (4 * S)) + 2 * top
        spans = {"causal": [(0, 0, S), (1, P, S)], "window": [(0, 0, P + WIN), (1, P, S)], "given": [(0, 0, S)]}[mask]
        self.steps = [(g, kt, q0, q1) for g in range(4) for kt, q0, q1 in spans]
        self.last_kt = spans[-1][0]
        self.top_steps = []
        if top:
            for t in range(TILES):
                n = C if cross else P * (t + 1)
                m = 512 // n
                self.top_steps += [(t, side, u, m, n) for u in range(0, 8, m) for side in range(2)]

    def value_head(self, u, side):
        return place(u, side) if self.kvh == H else 2 * (u // 4) + side

    def key_tile(self, u):
        return u if self.kvh == H else u // 4


class Mixing:

    name, rms, cross = "f", False, False


WH, WD = 16, 64
CHUNKS = WH * WD // P
WKEYS = S + C
KEY_TILES = [(0, P), (P, P), (S, C)]


class Wide:

    name, rms, cross = "w", False, True
    products = ([("q", c) for c in range(0, CHUNKS, 2)] + [("k", c) for c in range(CHUNKS)]
                + [("v", n) for n in range(2 * len(KEY_TILES))])


ROUTE_STEPS = 9

E, G, K = 32, 8, 4
HID = 256
N = B * S
NT = N // P
CAP = int(N / E * K * 1.25)
SLOT_P, SLOT_J = 80, CAP // 80
RING = 4
BEYOND = float(2 * E * CAP)
GROUP = 2

NARROW = [
    Narrow("g", KVH, rms=True, rope=True, qk_norm=True, norm=False),
    Narrow("l", KVH, rms=True, rope=True, qk_norm=True, mask="window"),
    Narrow("x", H, cross=True, bias=True, top=True, mask="given"),
    Narrow("a", H, rope=True, bias=True, top=True),
]
MIXING, WIDE = Mixing(), Wide()
LAYERS = NARROW[:3] + [MIXING, NARROW[3], WIDE]


TOP_ORDER = ("far norm 0, far normed 0, core scores 0, pre project_v 0, far turn_x 0, pre cut 3, "
             "core scores 1, far project 0, pre turn_q 0, pre turn_q 1, far cut 0, far cut 1, core values 0, "
             "pre turn_k 0, core scores 2, pre top 0, core values 1, far cut 2, core scores 3, pre top 1, "
             "core values 2, pre top 2, core values 3, pre top 3, pre shift 0, core merge 0, pre turn_q 2, "
             "core merge 1, pre turn_q 3, core output 0, core finished 0")
FLAT_ORDER = ("far norm 0, core scores 0, pre project_v 0, far normed 0, core scores 1, core values 0, "
              "far turn_x 0, far project 0, far cut 0, core scores 2, core values 1, core values 2, "
              "core merge 0, pre cut 3, core scores 3, pre turn_q 0, core values 3, pre turn_q 1, "
              "pre turn_k 0, core merge 1, far cut 1, core output 0, far cut 2, core finished 0")


def schedule(layer):
    if layer is MIXING:
        return [("core", "mix", 0), ("pre", "norm", 0), ("pre", "normed", 0), ("core", "mixed", 0), ("core", "finished", 0), ("pre", "turn_x", 0)]
    if layer is WIDE:
        out = []
        n = len(layer.products)
        for h in range(WH):
            if h == 2:
                out.append(("pre", "wide_project", 0))
            out.append(("core", "wide_scores", h))
            if h >= 3:
                out += [("pre", "wide_project", k) for k in range(1 + (n - 1) * (h - 3) // (WH - 3), 1 + (n - 1) * (h - 2) // (WH - 3))]
            if h == 1:
                out.append(("pre", "turn_x", 0))
            phase, past = ("core", h) if h >= 2 else ("late", h + WH)
            out.append((phase, "wide_turn", past - 2))
            out.append(("core", "wide_exp", h))
            out.append(("core" if h else "late", "wide_scale", (h - 1) % WH))
            phase, past = ("core", h) if h >= 4 else ("late", h + WH)
            if past % 2 == 0:
                out.append((phase, "wide_values", (past - 4) // 2))
            if h == 0:
                out.append(("pre", "norm", 0))
                out.append(("pre", "normed", 0))
            if h == 3:
                out.append(("late", "wide_output", 0))
            if h == 4:
                out.append(("late", "finished", 0))
                out.append(("late", "route_rows", 0))
            if 5 <= h < 5 + ROUTE_STEPS:
                out.append(("late", "route", h - 5))
        return out
    steps, tops = len(layer.steps) // 4, len(layer.top_steps) // 4
    out = []
    for piece in (TOP_ORDER if layer.top else FLAT_ORDER).split(", "):
        phase, name, k = piece.split()
        n = {"scores": steps, "top": tops}.get(name, 1)
        out += [(phase, name, m) for m in range(n * int(k), n * int(k) + n)]
    return out


def run_layers(chain, counts, pieces):
    layer = chain[0]
    order = schedule(layer)

    def batch(following=None, **at):
        for phase, name, k in order:
            if phase in at and name in pieces:
                b, par = at[phase]
                if isinstance(b, int) and b >= B:
                    if following is not None:
                        pieces[name](following, b - B, par, k)
                else:
                    pieces[name](layer, b, par, k)

    if layer in (MIXING, WIDE):
        batch(pre=(0, 0))
        batch(core=(0, 0), pre=(1, 1))
        with counts.loop(B // 2 - 1) as i:
            batch(late=(i * 2, 0), core=(i * 2 + 1, 1), pre=(i * 2 + 2, 0))
            batch(late=(i * 2 + 1, 1), core=(i * 2 + 2, 0), pre=(i * 2 + 3, 1))
        batch(late=(B - 2, 0), core=(B - 1, 1))
        batch(late=(B - 1, 1))
        return
    batch(far=(0, 0))
    batch(pre=(0, 0), far=(1, 1))
    for layer, following in zip(chain, chain[1:] + [None]):
        with counts.loop(B // 2 - 1) as i:
            batch(core=(i * 2, 0), pre=(i * 2 + 1, 1), far=(i * 2 + 2, 0))
            batch(core=(i * 2 + 1, 1), pre=(i * 2 + 2, 0), far=(i * 2 + 3, 1))
        batch(following, core=(B - 2, 0), pre=(B - 1, 1), far=(B, 0))
        batch(following, core=(B - 1, 1), pre=(B, 0), far=(B + 1, 1))


ZEROED = 5


def build_program(nc, t, per):
    chains = [LAYERS[:2]] + [[L] for L in LAYERS[2:]]
    ctx = ExitStack()
    with ctx:
        def sb(name, shape, dt=F32):
            return ctx.enter_context(nc.sbuf_tensor("s_" + name, shape, dt))

        def ps(name, shape, dt=F32):
            return ctx.enter_context(nc.psum_tensor("p_" + name, shape, dt))

        def sem(name):
            return ctx.enter_context(nc.semaphore(name))

        x0 = sb("x0", [P, B * TILES * D])
        xb = sb("xb", [P, B * TILES * D])
        ctx_all = sb("ctx_all", [C, B * D])
        weights = {L.name: sb(f"w_{L.name}", [P, D + 2 * L.kn]) for L in NARROW}
        wo = {L.name: sb(f"wo_{L.name}", [P, D]) for L in NARROW}
        norm_w = {L.name: sb(f"nw_{L.name}", [P, 1]) for L in NARROW if L.rms}
        cos = {L.name: sb(f"cos_{L.name}", [P, L.flat]) for L in NARROW if L.rope}
        sin = {L.name: sb(f"sin_{L.name}", [P, L.flat]) for L in NARROW if L.rope}
        bias_in = {L.name: sb(f"bi_{L.name}", [P, 3 * D]) for L in NARROW if L.bias}
        bias_out = {L.name: sb(f"bo_{L.name}", [P, D]) for L in NARROW if L.bias}
        down_t = sb("down_t", [32, P])
        ups = sb("ups", [32, 2 * KVH * HD])
        given8 = sb("given8", [P, B * TILES * C], U8)
        given = sb("given", [P, B * TILES * C], BF16)
        given_t = sb("given_t", [P, B * S], BF16)
        eye = sb("eye", [P, P])
        eye_b = sb("eye_b", [P, P], BF16)
        causal_q = sb("causal_q", [P, P], BF16)
        causal_k = sb("causal_k", [P, P], BF16)
        window_k = sb("window_k", [P, P + WIN], BF16)

        xs = [sb(f"xs{n}", [P, S]) for n in range(2)]
        xc = sb("xc", [C, D])
        xt = sb("xt", [P, S + C])
        flat_max = 4 * D
        qk = sb("qk", [P, flat_max])
        qk2 = sb("qk2", [P, flat_max])
        qk3 = sb("qk3", [P, flat_max])
        cuts = [sb(f"cut{n}", [P, flat_max], BF16) for n in range(3)]
        stack_words = sb("stack_words", [P, TILES * H * PART])
        stacks = stack_words[:, :].bitcast(BF16)
        q_stack, k_stack = (stacks[:, n * TILES * H * PART:(n + 1) * TILES * H * PART] for n in range(2))
        turned_words = sb("turned_words", [P, 16 * S])
        turned_b = turned_words[:, :].bitcast(BF16)
        qt = [turned_b[:, n * 8 * S:(n + 1) * 8 * S] for n in range(2)]
        kt_ = [turned_b[:, (2 + n) * 8 * S:(3 + n) * 8 * S] for n in range(2)]
        vals_all = sb("vals_all", [P, 2 * TILES * H * 32])
        vals = [vals_all[:, n * TILES * H * 32:(n + 1) * TILES * H * 32] for n in range(2)]
        PROBS = 4
        probs_all = sb("probs_all", [P, PROBS * 4 * S])
        probs = [probs_all[:, n * 4 * S:(n + 1) * 4 * S] for n in range(PROBS)]
        ot = sb("ot", [P, 4 * S])
        rden = sb("rden", [P, 16])
        on = sb("on", [P, TILES * D])
        ont = sb("ont", [P, TILES * D])
        y = sb("y", [P, TILES * D])
        sq = sb("sq", [P, TILES * D])
        ss = sb("ss", [P, 2])
        rs = sb("rs", [P, 2])
        nss = sb("nss", [P, 40])
        nrs = sb("nrs", [P, 40])
        stats = sb("stats", [P, 2 * 6])
        mv = sb("mv", [P, 4])
        lrs = sb("lrs", [P, 2])
        half = sb("half", [P, 40])
        tops = sb("tops", [P, TILES * H])
        top2 = sb("top2", [P, TILES * H])

        fourier = sb("fourier", [P, 5 * D])
        freq_w = sb("freq_w", [P, 2 * D])
        freq_a = sb("freq_a", [P, 2 * D])
        mix_w = sb("mix_w", [P, D])
        bias_mix = sb("bias_mix", [P, D])

        wide_q = sb("wide_q", [P, WH * WD])
        wide_kv = sb("wide_kv", [P, 2 * WH * WD])
        wide_o = sb("wide_o", [P, CHUNKS * D])
        ln_wb = sb("ln_wb", [P, 4])
        wq_t = [probs_all[:, n * CHUNKS * S:(n + 1) * CHUNKS * S] for n in range(2)]
        wk_t = [sb(f"wk_t{n}", [P, CHUNKS * WKEYS]) for n in range(2)]
        wv = [sb(f"wv{n}", [P, len(KEY_TILES) * WH * WD]) for n in range(2)]
        WPROBS = 4
        wprobs = [(x0, stack_words)[n // 2][:, n % 2 * TILES * WKEYS:(n % 2 + 1) * TILES * WKEYS] for n in range(WPROBS)]
        WTURNED = 4
        wturned = [turned_words[:, n * 3 * S:(n + 1) * 3 * S] for n in range(WTURNED)]
        wout_t = vals_all
        wtop = sb("wtop", [P, 2 * WPROBS])
        wden = sb("wden", [P, 2 * WPROBS])
        wrden = sb("wrden", [P, 2 * WPROBS])
        wstats = sb("wstats", [P, 3 * 6])
        wmv = sb("wmv", [P, 3 * 2])
        wrs = sb("wrs", [P, 3])

        centroids = sb("centroids", [G + E, D])
        cent_t = sb("cent_t", [P, G + E])
        cent_s = sb("cent_s", [G + E, 4])
        cent_sq = sb("cent_sq", [G + E, D])
        choice_bias = sb("choice_bias", [P, E])
        before = sb("before", [P, G * G])
        iota_e = sb("iota_e", [P, E])
        iota_i = sb("iota_i", [P, E], I32)
        earlier = sb("earlier", [P, P], BF16)
        ones_b = sb("ones_b", [P, P], BF16)
        zeros = sb("zeros", [P, 8 * D])
        shared_w = sb("shared_w", [P, 2 * HID + 2 * D])
        half_up = sb("half_up", [P, NT])
        slot_cur = sb("slot_cur", [P, TILES * K], U32)
        slot_out = sb("slot_out", [P, NT * K], U32)
        gate = sb("gate", [P, NT * K])
        small = sb("small", [P, 5 * TILES])
        taken = sb("taken", [P, E])
        lstats = sb("lstats", [P, GROUP * 6])
        lmv = sb("lmv", [P, 2 * GROUP * 2])
        glrs = sb("glrs", [P, 2 * GROUP])

        class View:

            def __init__(self, buf):
                self.buf, self.at = buf, 0

            def take(self, n):
                self.at += n
                return self.buf[:, self.at - n:self.at]

        spare = View(probs_all)
        xt_all, acc = spare.take(N), spare.take(N)
        sh_hid = turned_words[:, 0:1024]
        TK = TILES * K
        spare = View(ot)
        rows_cur, xt_cur, row_sq = spare.take(TILES * D), spare.take(TILES * P), spare.take(TILES * D)
        spare = View(qk)
        g_score, e_score, masked, rank = spare.take(TILES * G), spare.take(TILES * E), spare.take(TILES * E), spare.take(TILES * G)
        top8, idx8, idx_f, pos = spare.take(TILES * 8), spare.take(TILES * 8), spare.take(TK), spare.take(TK)
        gates, keep, totals = spare.take(TK), spare.take(TK), spare.take(TILES * E)
        spare = View(qk2)
        cmp_gt, cmp_eq, onehot = spare.take(TILES * G * G), spare.take(TILES * G * G), spare.take(TK * E)
        picked = qk3[:, 0:TK * E]
        chosen = cuts[0][:, 0:TILES * E]
        ew = [wv[0][:, n * 768:(n + 1) * 768] for n in range(RING)]
        ex_rows = [wk_t[1][0:SLOT_P, n * 512:(n + 1) * 512] for n in range(RING)]
        ex_t = [turned_words[:, 3072 + n * CAP:3072 + (n + 1) * CAP] for n in range(2)]
        ex_g = [wk_t[0][:, n * 2 * CAP:(n + 1) * 2 * CAP] for n in range(2)]
        ex_h = [wk_t[0][:, (2 + n) * 2 * CAP:(3 + n) * 2 * CAP] for n in range(2)]
        ex_out = [wv[1][0:SLOT_P, n * 512:(n + 1) * 512] for n in range(RING)]
        sh_gate = wv[1][:, 2048:3072]
        gathered = [buf[:, n * GROUP * K * D:(n + 1) * GROUP * K * D] for buf in (vals_all, stack_words, x0, wv[1])
                    for n in range(2)]

        score_ps = [ps(f"score_ps{n}", [P, 2, 512]) for n in range(2)]
        out_ps = ps("out_ps", [P, 512])
        post_ps = ps("post_ps", [P, 512])
        sums_ps = (out_ps, post_ps)
        pre_ps = ps("pre_ps", [P, 512])
        turn_ps = ps("turn_ps", [P, 512])

        loaded = {n: sem(f"loaded_{n}") for n in ("x", "ctx", "mask", "early", "g", "l", "x_", "f", "a", "w")}
        consts = sem("consts")
        waited = sem("waited")
        zeroed = sem("zeroed")
        setup_ps = sem("setup_ps")
        setup_sb = sem("setup_sb")
        v_step = sem("v_step")
        g_step = sem("g_step")
        x_rows = sem("x_rows")
        x_turned = sem("x_turned")
        xt_ready = sem("xt_ready")
        projected = sem("projected")
        pre_read = sem("pre_read")
        stacked = sem("stacked")
        turned = sem("turned")
        operands = sem("operands")
        turn_read = sem("turn_read")
        top_a, top_b = sem("top_a"), sem("top_b")
        shifted = sem("shifted")
        scored = sem("scored")
        probs_ready = sem("probs_ready")
        probs_free = sem("probs_free")
        ot_ready = sem("ot_ready")
        rows_back = sem("rows_back")
        merged = sem("merged")
        merged_turned = sem("merged_turned")
        ont_ready = sem("ont_ready")
        out_projected = sem("out_projected")
        post_read = sem("post_read")
        pow_asked = sem("pow_asked")
        pow_done = sem("pow_done")
        wide_scored = sem("wide_scored")
        topped = sem("topped")
        exped = sem("exped")
        scaled = sem("scaled")
        probs_turned = sem("probs_turned")
        turned_a = sem("turned_a")
        turned_c = sem("turned_c")
        pair_summed = sem("pair_summed")
        pair_out = sem("pair_out")
        wide_made = sem("wide_made")
        wide_a = sem("wide_a")
        exp_loaded = sem("exp_loaded")
        slots_zeroed = sem("slots_zeroed")
        scattered = sem("scattered")
        rows_free = sem("rows_free")
        weights_in = [sem(f"weights_in{n}") for n in range(RING)]
        results_out = [sem(f"results_out{n}") for n in range(RING)]
        gathered_in = [sem(f"gathered_in{n}") for n in range(NT // GROUP)]
        batch_done = sem("batch_done")
        rows_ready = sem("rows_ready")
        route_turned = sem("route_turned")
        route_xt = sem("route_xt")
        route_scored = sem("route_scored")
        route_read = sem("route_read")
        route_chosen = sem("route_chosen")
        route_counted = sem("route_counted")
        r_ps = sem("r_ps")
        r_sb = sem("r_sb")
        exps_asked = sem("exps_asked")
        exps_made = sem("exps_made")
        slots_known = sem("slots_known")
        sh_made = sem("sh_made")
        sh_silu = sem("sh_silu")
        sh_gated = sem("sh_gated")
        sh_summed = sem("sh_summed")
        rows_turned = sem("rows_turned")
        rows_copied = sem("rows_copied")
        gate_made = sem("gate_made")
        up_made = sem("up_made")
        silued = sem("silued")
        gated = sem("gated")
        downed = sem("downed")
        out_rows = sem("out_rows")
        written = sem("written")
        stored = sem("stored")

        turn_banks = [bank[:, :].bitcast(BF16) for bank in (turn_ps, pre_ps)]

        block = ctx.enter_context(nc.Block())

        def rows_of(buf, b):
            return buf[:, bass.ts(b, TILES * D)]

        def wide_copy(L, par, k):
            what, c = L.products[k]
            if what == "q":
                return wq_t[par][:, c * S:(c + 2) * S], turn_ps[:, :], 1.0 / float(np.sqrt(WD))
            if what == "k":
                return wk_t[par][:, c * WKEYS:(c + 1) * WKEYS], turn_ps[:, 0:WKEYS], 1.0
            m = KEY_TILES[c // 2][1]
            at = (c // 2) * WH * WD + (c % 2) * 512
            return wv[par][0:m, at:at + 512], turn_ps[0:m, :], 1.0

        @block.sync
        def _(eng):
            eng.dma_start(x0[:, :].rearrange("p (n d) -> p n d", d=D),
                          t["x"].rearrange("b (t p) d -> p (b t) d", p=P)).then_inc(loaded["x"], 16)
            eng.dma_start(down_t[:, :], t["down_t"]).then_inc(loaded["early"], 16)
            eng.dma_start(ups[:, :], t["ups"]).then_inc(loaded["early"], 16)
            for L in NARROW[:2]:
                s = loaded[L.name]
                w = weights[L.name]
                if L.name == "g":
                    eng.dma_start(w[:, 0:D], t["w_g"]).then_inc(s, 16)
                else:
                    eng.dma_start(w[:, :], t["w_l"]).then_inc(s, 16)
                eng.dma_start(wo[L.name][:, :], t[f"wo_{L.name}"]).then_inc(s, 16)
                eng.dma_start(norm_w[L.name][:, :], t[f"nw_{L.name}"]).then_inc(s, 16)
                eng.dma_start(cos[L.name][:, :], t[f"cos_{L.name}"]).then_inc(s, 16)
                eng.dma_start(sin[L.name][:, :], t[f"sin_{L.name}"]).then_inc(s, 16)
            eng.dma_start(ctx_all[:, :].rearrange("p (b d) -> p b d", d=D),
                          t["ctx"].rearrange("b p d -> p b d")).then_inc(loaded["ctx"], 16)
            eng.dma_start(given8[:, :].rearrange("p (n c) -> p n c", c=C),
                          t["mask"].rearrange("b (t p) c -> p (b t) c", p=P)).then_inc(loaded["mask"], 16)
            for L, s in ((NARROW[2], loaded["x_"]), (NARROW[3], loaded["a"])):
                eng.dma_start(weights[L.name][:, :], t[f"w_{L.name}"]).then_inc(s, 16)
                eng.dma_start(wo[L.name][:, :], t[f"wo_{L.name}"]).then_inc(s, 16)
                eng.dma_start(bias_in[L.name][:, :], t[f"bi_{L.name}"]).then_inc(s, 16)
                eng.dma_start(bias_out[L.name][:, :], t[f"bo_{L.name}"]).then_inc(s, 16)
                if L.rope:
                    eng.dma_start(cos[L.name][:, :], t[f"cos_{L.name}"]).then_inc(s, 16)
                    eng.dma_start(sin[L.name][:, :], t[f"sin_{L.name}"]).then_inc(s, 16)
            for n, m in enumerate(("Fr", "Fi", "nFi", "Gr", "nGi")):
                eng.dma_start(fourier[:, n * D:(n + 1) * D], t[m]).then_inc(loaded["f"], 16)
            eng.dma_start(freq_w[:, 0:D], t["freq_r"]).then_inc(loaded["f"], 16)
            eng.dma_start(freq_w[:, D:2 * D], t["freq_i"]).then_inc(loaded["f"], 16)
            eng.dma_start(bias_mix[:, :], t["bias_mix"]).then_inc(loaded["f"], 16)
            eng.dma_start(wide_q[:, :], t["wide_q"]).then_inc(loaded["w"], 16)
            eng.dma_start(wide_kv[:, :], t["wide_kv"]).then_inc(loaded["w"], 16)
            eng.dma_start(wide_o[:, :].rearrange("p (c d) -> p c d", d=D),
                          t["wide_o"].rearrange("(c p) d -> p c d", p=P)).then_inc(loaded["w"], 16)
            eng.dma_start(ln_wb[:, :], t["ln_wb"]).then_inc(loaded["w"], 16)
            eng.dma_start(centroids[0:G, :], t["group_c"]).then_inc(exp_loaded, 16)
            eng.dma_start(centroids[G:G + E, :], t["expert_c"]).then_inc(exp_loaded, 16)
            eng.dma_start(choice_bias[:, :], t["choice_bias"]).then_inc(exp_loaded, 16)
            eng.dma_start(shared_w[:, 0:HID], t["sg"]).then_inc(exp_loaded, 16)
            eng.dma_start(shared_w[:, HID:2 * HID], t["su"]).then_inc(exp_loaded, 16)
            eng.dma_start(shared_w[:, 2 * HID:].rearrange("p (c d) -> p c d", c=2),
                          t["sd"].rearrange("(p c) d -> p c d", c=2)).then_inc(exp_loaded, 16)
            eng.wait_ge(zeroed, ZEROED + 1)
            slot_blocks = t["slots"].rearrange("(p n) d -> p (n d)", p=P)
            for n in range(E * CAP // P // 8):
                eng.dma_start(slot_blocks[:, n * 8 * D:(n + 1) * 8 * D], zeros[:, :]).then_inc(slots_zeroed, 16)

            counts = Counts("sync", eng, per)

            def load_weights(e, n):
                w = ew[n]
                eng.dma_start(w[:, 0:HID], t["wg"][bass.ts(e, P), :]).then_inc(weights_in[n], 16)
                eng.dma_start(w[:, HID:2 * HID], t["wu"][bass.ts(e, P), :]).then_inc(weights_in[n], 16)
                eng.dma_start(w[:, 2 * HID:], t["wd"][bass.ts(e, P), :]).then_inc(weights_in[n], 16)

            def load_rows(e, n):
                eng.dma_start(ex_rows[n], t["slots"].rearrange("(p j) d -> p (j d)", j=SLOT_J)[bass.ts(e, SLOT_P), :])\
                   .then_inc(weights_in[n], 16)

            def store(e, n):
                eng.wait_ge(out_rows, counts.after(out_rows))
                eng.dma_start(t["results"].rearrange("(p j) d -> p (j d)", j=SLOT_J)[bass.ts(e, SLOT_P), :], ex_out[n])\
                   .then_inc(results_out[n], 16)

            with counts.loop(B - 1):
                eng.wait_ge(scattered, counts.after(scattered, 16 * TK))
                eng.sem_inc(rows_free, 1)
            eng.wait_ge(batch_done, B)
            for n in range(RING):
                load_weights(n, n)
            eng.wait_ge(scattered, 16 * NT * K)
            for n in range(RING):
                load_rows(n, n)
            with counts.loop((E - RING) // RING) as i:
                for n in range(RING):
                    eng.wait_ge(downed, counts.after(downed))
                    load_weights(i * RING + (RING + n), n)
                    load_rows(i * RING + (RING + n), n)
                    store(i * RING + n, n)
            for n in range(RING):
                store(E - RING + n, n)
            for q in range(NT // GROUP):
                eng.wait_ge(written, q + 1)
                rows = slice(q * GROUP * D, (q + 1) * GROUP * D)
                eng.dma_start(t["out"].rearrange("b (t p) d -> p (b t) d", p=P)[:, q * GROUP:(q + 1) * GROUP, :],
                              xb[:, rows].rearrange("p (n d) -> p n d", d=D)).then_inc(stored, 16)
            eng.wait_ge(stored, 16 * (NT // GROUP))

        @block.gpsimd
        def _(eng):
            counts = Counts("gpsimd", eng, per)
            eng.memset(half[:, :], -0.5).then_inc(consts, 1)
            eng.memset(eye[:, :], 0.0).then_inc(g_step, 1)
            eng.memset(causal_q[:, :], 0.0).then_inc(g_step, 1)
            eng.memset(causal_k[:, :], 0.0).then_inc(g_step, 1)
            eng.memset(window_k[:, :], 0.0).then_inc(g_step, 1)
            eng.memset(given_t[:, :], 0.0).then_inc(zeroed, 1)
            eng.wait_ge(g_step, counts.after(g_step, 4))
            eng.affine_select(out=eye[:, :], in_=eye[:, :], compare_op=ALU.not_equal, fill=1.0, base=0,
                              pattern=[[-1, P]], channel_multiplier=1).then_inc(g_step, 1)
            eng.affine_select(out=causal_q[:, :], in_=causal_q[:, :], compare_op=ALU.is_ge, fill=NEG, base=0,
                              pattern=[[-1, P]], channel_multiplier=1).then_inc(consts, 1)
            eng.affine_select(out=causal_k[:, :], in_=causal_k[:, :], compare_op=ALU.is_ge, fill=NEG, base=0,
                              pattern=[[1, P]], channel_multiplier=-1).then_inc(consts, 1)
            eng.affine_select(out=window_k[:, :], in_=window_k[:, :], compare_op=ALU.is_ge, fill=NEG, base=0,
                              pattern=[[1, P + WIN]], channel_multiplier=-1).then_inc(g_step, 1)
            eng.wait_ge(g_step, counts.after(g_step, 2))
            eng.affine_select(out=window_k[:, :], in_=window_k[:, :], compare_op=ALU.is_ge, fill=NEG, base=WIN - 1,
                              pattern=[[-1, P + WIN]], channel_multiplier=1).then_inc(consts, 1)
            eng.tensor_copy(eye_b[:, :], eye[:, :]).then_inc(consts, 1)
            eng.memset(zeros[:, :], 0.0).then_inc(zeroed, 1)
            for buf in (before, earlier, ones_b):
                eng.memset(buf[:, :], 1.0).then_inc(g_step, 1)
            eng.memset(half_up[:, :], 0.5).then_inc(g_step, 1)
            eng.iota(iota_i[:, :], pattern=[[1, E]], base=0, channel_multiplier=0).then_inc(g_step, 1)
            eng.wait_ge(g_step, counts.after(g_step, 5))
            eng.affine_select(out=before[:, :].rearrange("p (i j) -> p i j", j=G), in_=before[:, :].rearrange("p (i j) -> p i j", j=G),
                              compare_op=ALU.is_gt, fill=0.0, base=0, pattern=[[1, G], [-1, G]], channel_multiplier=0)\
               .then_inc(consts, 1)
            eng.affine_select(out=earlier[:, :], in_=earlier[:, :], compare_op=ALU.is_gt, fill=0.0, base=0,
                              pattern=[[1, P]], channel_multiplier=-1).then_inc(consts, 1)
            eng.tensor_copy(iota_e[:, :], iota_i[:, :]).then_inc(consts, 1)

            def power(dst, src, scale, eps, n):
                eng.wait_ge(pow_asked, counts.after(pow_asked))
                eng.sem_inc(waited, 1)
                eng.tensor_scalar(dst, src, scale, eps, ALU.mult, ALU.add).then_inc(g_step, 1)
                eng.wait_ge(g_step, counts.after(g_step))
                eng.tensor_tensor(dst, dst, half[:, 0:n], ALU.pow).then_inc(pow_done, 1)

            def norm(L, b, par, k):
                if L is WIDE:
                    power(wrs[:, :], wmv[:, 1:6:2], 1.0, 1e-5, 3)
                elif L.rms:
                    power(rs[:, :], ss[:, :], 1.0 / D, 1e-6, 2)

            def cut(L, b, par, k):
                if L.qk_norm and k == 0:
                    power(nrs[:, :], nss[:, :], 1.0 / HD, 1e-6, 40)

            def route_rows(L, b, par, k):
                eng.wait_ge(batch_done, counts.after(batch_done))
                eng.sem_inc(waited, 1)
                eng.wait_ge(rows_free, counts.after(rows_free))
                eng.sem_inc(waited, 1)
                eng.tensor_copy(rows_cur, rows_of(xb, b)).then_inc(rows_ready, 1)

            def route(L, b, par, k):
                if k == 0:
                    eng.wait_ge(pow_asked, counts.after(pow_asked))
                    eng.tensor_tensor(small[:, TILES:2 * TILES], small[:, 0:TILES], half_up[:, 0:TILES], ALU.pow)\
                       .then_inc(pow_done, 1)
                if k == ROUTE_STEPS - 1:
                    eng.wait_ge(slots_known, counts.after(slots_known))
                    eng.sem_inc(waited, 1)
                    for tile in range(TILES):
                        for j in range(K):
                            at = tile * K + j
                            eng.indirect_dma_start(t["slots"][:, :], bass.IndirectOffsetOnAxis(slot_cur[:, at:at + 1], 0),
                                                   rows_cur[:, tile * D:(tile + 1) * D], None,
                                                   bounds_check=E * CAP - 1, oob_is_err=False).then_inc(scattered, 16)

            def output(L, b, par, k):
                if L in (MIXING, WIDE) or L.norm:
                    power(lrs[:, :], mv[:, 1:4:2], 1.0, 1e-5, 2)

            for chain in chains:
                L = chain[0]
                pieces = dict(norm=norm, cut=cut, output=output, mixed=output, wide_output=output)
                if L is WIDE:
                    eng.wait_ge(pow_asked, counts.after(pow_asked))
                    eng.tensor_tensor(cent_s[:, 1:2], cent_s[:, 0:1], half_up[0:G + E, 0:1], ALU.pow).then_inc(pow_done, 1)
                    eng.wait_ge(slots_zeroed, 16 * (E * CAP // P // 8))
                    eng.sem_inc(rows_free, 1)
                    pieces.update(route_rows=route_rows, route=route)
                run_layers(chain, counts, pieces)
            for n in range(RING):
                eng.wait_ge(results_out[n], 16 * (E // RING))

            def gather(q):
                for m in range(GROUP * K):
                    at = q * GROUP * K + m
                    eng.indirect_dma_start(gathered[q][:, m * D:(m + 1) * D], None, t["results"][:, :],
                                           bass.IndirectOffsetOnAxis(slot_out[:, at:at + 1], 0),
                                           bounds_check=E * CAP - 1, oob_is_err=False).then_inc(gathered_in[q], 16)

            gather(0)
            for q in range(NT // GROUP):
                if q + 1 < NT // GROUP:
                    gather(q + 1)
                at = q % 2 * GROUP
                power(glrs[:, at:at + GROUP], lmv[:, 2 * at + 1:2 * at + 2 * GROUP:2], 1.0, 1e-5, GROUP)

        @block.tensor
        def _(eng):
            counts = Counts("tensor", eng, per)
            eng.wait_ge(consts, 8)
            eng.wait_ge(loaded["early"], 32)
            eng.matmul(pre_ps[:, 0:2 * KVH * HD], down_t[:, :], ups[:, :], start=True, stop=True).then_inc(setup_ps, 1)
            eng.wait_ge(setup_sb, counts.after(setup_sb, 2))
            given_ps = turn_ps[:, :].bitcast(BF16)
            for half_ in range(2):
                if half_:
                    eng.wait_ge(setup_sb, counts.after(setup_sb))
                for n in range(8):
                    tile = half_ * 8 + n
                    last = eng.transpose(given_ps[0:C, n * P:(n + 1) * P], given[:, tile * C:(tile + 1) * C], eye_b[:, :])
                last.then_inc(setup_ps, 1)
            eng.wait_ge(zeroed, ZEROED + 1)

            def turn_x(L, b, par, k):
                if L is WIDE and not (isinstance(b, int) and b <= 1):
                    eng.wait_ge(pair_out, counts.until(pair_out, par, CHUNKS - 1))
                if unread_pre[0]:
                    eng.wait_ge(pre_read, counts.after(pre_read, unread_pre[0]))
                    unread_pre[0] = 0
                if L in NARROW and not (L.first and isinstance(b, int) and b <= 1) and counts.owed(operands, par, L.turns):
                    eng.wait_ge(operands, counts.until(operands, par, L.turns))
                eng.wait_ge(x_rows, counts.after(x_rows))
                for n in range(TILES):
                    last = eng.transpose(pre_ps[:, n * P:(n + 1) * P], xs[par][:, n * D:(n + 1) * D], eye[:, :])
                if L.cross:
                    last = eng.transpose(pre_ps[:, S:S + C], xc[:, :], eye[0:C, 0:C])
                last.then_inc(x_turned, 1)

            def project(L, b, par, k):
                w = weights[L.name]
                eng.wait_ge(xt_ready, counts.after(xt_ready))
                if L.cross:
                    for n in range(TILES):
                        eng.matmul(pre_ps[:, n * D:(n + 1) * D], xt[:, n * P:(n + 1) * P], w[:, 0:D], start=True, stop=True)
                    last = eng.matmul(pre_ps[0:C, 2 * D:3 * D], xt[:, S:S + C], w[:, D:2 * D], start=True, stop=True)
                else:
                    width = D + L.kn
                    for n in range(TILES):
                        last = eng.matmul(pre_ps[:, n * width:(n + 1) * width], xt[:, n * P:(n + 1) * P], w[:, 0:width],
                                          start=True, stop=True)
                last.then_inc(projected, 1)
                unread_pre[0] += 1

            def project_v(L, b, par, k):
                w = weights[L.name][:, D + L.kn:D + 2 * L.kn]
                if not (L.first and isinstance(b, int) and b == 0) and counts.owed(operands, 1 - par, L.turns - 1):
                    eng.wait_ge(operands, counts.until(operands, 1 - par, L.turns - 1))
                for n in range(L.key_tiles):
                    first = S if L.cross else n * P
                    last = eng.matmul(turn_ps[0:L.keys, n * L.kn:(n + 1) * L.kn], xt[:, first:first + L.keys], w,
                                      start=True, stop=True)
                last.then_inc(projected, 1)

            def turn_q(L, b, par, k):
                if k == 0:
                    counts.batch(par, operands)
                    eng.wait_ge(stacked, counts.after(stacked))
                elif k == 2:
                    eng.wait_ge(shifted, counts.after(shifted))
                    eng.wait_ge(turn_read, counts.after(turn_read))
                elif k == 1 and unread_pre[0]:
                    eng.wait_ge(pre_read, counts.after(pre_read, unread_pre[0]))
                    unread_pre[0] = 0
                bank = turn_banks[k % 2]
                for u in range(4 * (k % 2), 4 * (k % 2) + 4):
                    for n in range(TILES):
                        at = (n * H + place(u, 0)) * PART
                        last = eng.transpose(bank[:, ((u % 4) * TILES + n) * P:((u % 4) * TILES + n + 1) * P],
                                             q_stack[:, at:at + P], eye_b[:, :])
                last.then_inc(turned, 1)

            def turn_k(L, b, par, k):
                n_k = L.keys
                per_bank = 8 if L.cross else 4
                for n_bank, first in enumerate(range(0, L.ktiles, per_bank)):
                    eng.wait_ge(operands, counts.until(operands, par, 1 + n_bank))
                    if L.cross:
                        eng.sem_inc(waited, 1)
                    for u in range(first, min(first + per_bank, L.ktiles)):
                        for n in range(L.key_tiles):
                            rows = (n * L.kvh + 2 * u) * PART
                            at = ((u - first) * L.key_tiles + n) * n_k
                            last = eng.transpose(turn_banks[n_bank][:, at:at + n_k],
                                                 k_stack[0:n_k, rows:rows + P],
                                                 eye_b[0:n_k, 0:n_k])
                    last.then_inc(turned, 1)

            def keys_of(L, par, u, side, rows, first, n):
                width = L.keys * L.key_tiles
                at = L.key_tile(u) * width + first
                return kt_[par][PART * side:PART * side + rows, at:at + n]

            def queries_of(par, u, side, rows, first, n):
                return qt[par][PART * side:PART * side + rows, u * S + first:u * S + first + n]

            def top(L, b, par, k):
                q, side, u0, m, n = L.top_steps[k]
                bank, full = ((pre_ps, top_a), (turn_ps, top_b))[k % 2]
                if k == 0:
                    eng.wait_ge(operands, counts.until(operands, par, L.turns - 2))
                if k % 2 == 0 and unread_pre[0]:
                    eng.wait_ge(pre_read, counts.after(pre_read, unread_pre[0]))
                    unread_pre[0] = 0
                elif k % 2 and k > 1:
                    eng.wait_ge(turn_read, counts.after(turn_read))
                unread_pre[0] += 1 - k % 2
                if L.cross:
                    eng.matmul(bank[:, 0:m * n].rearrange("p (m n) -> p m n", m=m), eye_b[:, :],
                               given[:, bass.ds(b * (TILES * C) + q * C, C)].unsqueeze(1).broadcast_to([P, m, C]),
                               start=True, stop=False, skip_group_check=True)
                else:
                    eng.matmul(bank[:, 0:m * n].rearrange("p (m n) -> p m n", m=m)[:, :, n - P:n], eye_b[:, :],
                               causal_q[:, :].unsqueeze(1).broadcast_to([P, m, P]),
                               start=True, stop=False, skip_group_check=True)
                for j in range(m):
                    last = eng.matmul(bank[:, j * n:(j + 1) * n], queries_of(par, u0 + j, side, ROWS, q * P, P),
                                      keys_of(L, par, u0 + j, side, ROWS, 0, n),
                                      start=False, stop=True, skip_group_check=True)
                last.then_inc(full, 1)

            def scores(L, b, par, k):
                g, kt, q0, q1 = L.steps[k]
                bank = score_ps[k % 2]
                rows = ROWS_MAX if L.top else ROWS
                if k == 0:
                    counts.batch(par, probs_ready, ot_ready)
                ready = L.turns - (1 if L.top and g < 2 else 0)
                if counts.owed(operands, par, ready):
                    eng.wait_ge(operands, counts.until(operands, par, ready))
                if counts.owed(probs_ready, par, k - 1):
                    eng.wait_ge(probs_ready, counts.until(probs_ready, par, k - 1))
                if L.cross:
                    eng.sem_inc(waited, 1)
                n_k = L.keys
                for side in range(2):
                    if L.mask == "given":
                        width = S
                        mask = given_t[:, bass.ts(b, S)]
                    else:
                        width = q1 - q0 if L.mask == "window" else P
                        mask = (window_k if L.mask == "window" else causal_k)[:, 0:width]
                    eng.matmul(bank[0:n_k, side, :].rearrange("p (u q) -> p u q", u=2)[:, :, q0:q0 + width],
                               eye_b[:, 0:n_k], mask.unsqueeze(1).broadcast_to([P, 2, width]),
                               start=True, stop=False, skip_group_check=True)
                for side in range(2):
                    for uu in range(2):
                        u = 2 * g + uu
                        last = eng.matmul(bank[0:n_k, side, uu * S + q0:uu * S + q1],
                                          keys_of(L, par, u, side, rows, kt * P, n_k),
                                          queries_of(par, u, side, rows, q0, q1 - q0),
                                          start=False, stop=True, skip_group_check=True)
                last.then_inc(scored, 1)

            def values(L, b, par, k):
                if counts.owed(ot_ready, par, k - 1):
                    eng.wait_ge(ot_ready, counts.until(ot_ready, par, k - 1))
                if k == 1:
                    eng.wait_ge(post_read, counts.after(post_read))
                if k == 3 and not L.top:
                    eng.wait_ge(merged, counts.after(merged))
                steps = [n for n, step in enumerate(L.steps) if step[0] == k]
                v = vals[par][0:L.keys, :].rearrange("p (t h c) -> p t h c", t=TILES, c=32)
                for n in steps:
                    g, kt, q0, q1 = L.steps[n]
                    if counts.owed(probs_ready, par, n + 1):
                        eng.wait_ge(probs_ready, counts.until(probs_ready, par, n + 1))
                        if L.cross:
                            eng.sem_inc(waited, 1)
                    for side in range(2):
                        for uu in range(2):
                            j = 2 * side + uu
                            h = L.value_head(2 * g + uu, side)
                            last = eng.matmul(sums_ps[k % 2][32 * j:32 * j + 32, q0:q1], v[:, kt, h, :],
                                              probs[n % PROBS][0:L.keys, j * S + q0:j * S + q1],
                                              start=(n == steps[0]), stop=(n == steps[-1]), skip_group_check=True)
                    last.then_inc(probs_free, 1)

            def merge(L, b, par, k):
                groups = 4 if L.top else 2 * k + 2
                if counts.owed(ot_ready, par, groups):
                    eng.wait_ge(ot_ready, counts.until(ot_ready, par, groups))
                if k and L.top:
                    eng.wait_ge(merged, counts.after(merged))
                for n in range(TILES):
                    for g in range(2):
                        at = (2 * n + g) * P
                        last = eng.transpose(post_ps[:, at:at + P],
                                             ot[:, (2 * k + g) * S + n * P:(2 * k + g) * S + (n + 1) * P], eye[:, :])
                last.then_inc(rows_back, 1)

            def output(L, b, par, k):
                eng.wait_ge(merged, counts.after(merged))
                for n in range(TILES):
                    last = eng.transpose(post_ps[:, n * P:(n + 1) * P], on[:, n * D:(n + 1) * D], eye[:, :])
                last.then_inc(merged_turned, 1)
                eng.wait_ge(ont_ready, counts.after(ont_ready))
                for n in range(TILES):
                    last = eng.matmul(post_ps[:, n * D:(n + 1) * D], ont[:, n * P:(n + 1) * P], wo[L.name][:, :],
                                      start=True, stop=True)
                last.then_inc(out_projected, 1)

            def mixing_matrix():
                fr, fi, nfi, gr, ngi = (fourier[:, n * D:(n + 1) * D] for n in range(5))
                wr, wi = freq_w[:, 0:D], freq_w[:, D:2 * D]
                for n, (a, b_) in enumerate(((fr, nfi), (fi, fr))):
                    eng.matmul(out_ps[:, n * D:(n + 1) * D], wr, a, start=True, stop=False)
                    last = eng.matmul(out_ps[:, n * D:(n + 1) * D], wi, b_, start=False, stop=True)
                last.then_inc(setup_ps, 1)
                eng.wait_ge(setup_sb, counts.after(setup_sb))
                eng.matmul(out_ps[:, 0:D], freq_a[:, 0:D], gr, start=True, stop=False)
                eng.matmul(out_ps[:, 0:D], freq_a[:, D:2 * D], ngi, start=False, stop=True).then_inc(setup_ps, 1)
                eng.wait_ge(setup_sb, counts.after(setup_sb))

            def mix(L, b, par, k):
                eng.wait_ge(xt_ready, counts.after(xt_ready))
                for n in range(TILES):
                    last = eng.matmul(pre_ps[:, n * D:(n + 1) * D], xt[:, n * P:(n + 1) * P], mix_w[:, :], start=True, stop=True)
                last.then_inc(projected, 1)
                unread_pre[0] += 1

            def wide_project(L, b, par, k):
                if k == 0:
                    eng.wait_ge(xt_ready, counts.after(xt_ready))
                if k:
                    eng.wait_ge(wide_a, counts.after(wide_a))
                what, c = L.products[k]
                if what == "q":
                    for n in range(2):
                        last = eng.matmul(turn_ps[:, n * S:(n + 1) * S], wide_q[:, (c + n) * P:(c + n + 1) * P], xt[:, 0:S],
                                          start=True, stop=True)
                elif what == "k":
                    last = eng.matmul(turn_ps[:, 0:WKEYS], wide_kv[:, c * P:(c + 1) * P], xt[:, :], start=True, stop=True)
                else:
                    first, n = KEY_TILES[c // 2]
                    at = WH * WD + (c % 2) * 512
                    last = eng.matmul(turn_ps[0:n, :], xt[:, first:first + n], wide_kv[:, at:at + 512], start=True, stop=True)
                last.then_inc(wide_made, 1)

            def wide_scores(L, b, par, k):
                c, rows = k // 2, slice(WD * (k % 2), WD * (k % 2) + WD)
                if k == 0:
                    eng.wait_ge(wide_a, counts.after(wide_a))
                    counts.batch(par, exped, turned_a, turned_c, pair_out)
                if counts.owed(exped, par, k - 1):
                    eng.wait_ge(exped, counts.until(exped, par, k - 1))
                for n in range(TILES):
                    last = eng.matmul(score_ps[k % 2][:, n, 0:WKEYS], wq_t[par][rows, c * S + n * P:c * S + (n + 1) * P],
                                      wk_t[par][rows, c * WKEYS:(c + 1) * WKEYS], start=True, stop=True)
                last.then_inc(wide_scored, 1)

            def wide_turn(L, b, par, k):
                eng.wait_ge(scaled, counts.after(scaled))
                if counts.owed(turned_a, par, k):
                    eng.wait_ge(turned_a, counts.until(turned_a, par, k))
                if counts.owed(turned_c, par, k):
                    eng.wait_ge(turned_c, counts.until(turned_c, par, k))
                if unread[0]:
                    eng.wait_ge(post_read, counts.after(post_read))
                    unread[0] = False
                src = wprobs[k % WPROBS]
                for n, (first, m) in enumerate(KEY_TILES):
                    for q in range(TILES):
                        bank, at = (out_ps, n * S) if n < 2 else (post_ps, 0)
                        last = eng.transpose(bank[0:m, at + q * P:at + (q + 1) * P],
                                             src[:, q * WKEYS + first:q * WKEYS + first + m], eye[:, :])
                last.then_inc(probs_turned, 1)

            def pre_ps_free():
                if counts.owed(pair_out, *pairs[0]):
                    eng.wait_ge(pair_out, counts.until(pair_out, *pairs[0]))
                if route_unread[0] == "turned rows":
                    eng.wait_ge(route_xt, counts.after(route_xt))
                elif route_unread[0] == "product":
                    eng.wait_ge(route_read, counts.after(route_read))
                route_unread[0] = None

            def wide_values(L, b, par, k):
                if counts.owed(turned_a, par, 2 * k + 2):
                    eng.wait_ge(turned_a, counts.until(turned_a, par, 2 * k + 2))
                if counts.owed(turned_c, par, 2 * k + 2):
                    eng.wait_ge(turned_c, counts.until(turned_c, par, 2 * k + 2))
                if pairs[0]:
                    pre_ps_free()
                pairs[0] = (par, k + 1)
                for n, (first, m) in enumerate(KEY_TILES):
                    for side in range(2):
                        h = 2 * k + side
                        last = eng.matmul(pre_ps[WD * side:WD * side + WD, 0:S],
                                          wv[par][0:m, n * WH * WD + h * WD:n * WH * WD + (h + 1) * WD],
                                          wturned[h % WTURNED][0:m, n * S:(n + 1) * S],
                                          start=(n == 0), stop=(n == len(KEY_TILES) - 1), skip_group_check=True)
                last.then_inc(pair_summed, 1)

            def route(L, b, par, k):
                if k == 0:
                    pre_ps_free()
                    eng.wait_ge(rows_ready, counts.after(rows_ready))
                    for n in range(TILES):
                        last = eng.transpose(pre_ps[:, n * P:(n + 1) * P], rows_cur[:, n * D:(n + 1) * D], eye[:, :])
                    last.then_inc(route_turned, 1)
                    route_unread[0] = "turned rows"
                if k == 1:
                    pre_ps_free()
                    for n in range(TILES):
                        last = eng.matmul(pre_ps[:, n * (G + E):(n + 1) * (G + E)], xt_cur[:, n * P:(n + 1) * P], cent_t[:, :],
                                          start=True, stop=True)
                    last.then_inc(route_scored, 1)
                    route_unread[0] = "product"
                if k == 6:
                    pre_ps_free()
                    eng.wait_ge(route_chosen, counts.after(route_chosen))
                    eng.matmul(pre_ps[:, 0:TILES * E], earlier[:, :], chosen, start=True, stop=True)
                    eng.matmul(pre_ps[:, TILES * E:2 * TILES * E], ones_b[:, :], chosen, start=True, stop=True)\
                       .then_inc(route_counted, 1)
                    route_unread[0] = "product"

            def wide_output(L, b, par, k):
                if counts.owed(pair_out, par, CHUNKS):
                    eng.wait_ge(pair_out, counts.until(pair_out, par, CHUNKS))
                ahead_ = WH if isinstance(b, int) and b == B - 1 else WH + 2
                if counts.owed(turned_c, par, ahead_):
                    eng.wait_ge(turned_c, counts.until(turned_c, par, ahead_))
                for n in range(TILES):
                    for c in range(CHUNKS):
                        last = eng.matmul(post_ps[:, n * D:(n + 1) * D], wout_t[:, c * S + n * P:c * S + (n + 1) * P],
                                          wide_o[:, c * D:(c + 1) * D], start=(c == 0), stop=(c == CHUNKS - 1))
                last.then_inc(out_projected, 1)
                unread[0] = True

            unread, unread_pre, route_unread = [True], [0], [None]
            pairs = [None]
            for chain in chains:
                for L in chain:
                    eng.wait_ge(loaded["x_" if L.name == "x" else L.name], loads_of(L))
                if L is MIXING:
                    mixing_matrix()
                elif L is WIDE:
                    counts.layer([(exped, WH), (turned_a, WH), (turned_c, WH), (pair_out, CHUNKS)])
                else:
                    counts.layer([(probs_ready, len(L.steps)), (ot_ready, 4), (operands, L.turns)])
                pieces = dict(turn_x=turn_x, project=project, project_v=project_v, turn_q=turn_q, turn_k=turn_k, top=top,
                              scores=scores, values=values, merge=merge, output=output, mix=mix,
                              wide_project=wide_project, wide_scores=wide_scores, wide_turn=wide_turn,
                              wide_values=wide_values, wide_output=wide_output)
                if L is WIDE:
                    eng.wait_ge(exp_loaded, 16 * 6)
                    eng.wait_ge(r_sb, counts.after(r_sb))
                    eng.transpose(out_ps[:, 0:G + E], centroids[:, :], eye[0:G + E, 0:G + E]).then_inc(r_ps, 1)
                    eng.wait_ge(r_sb, counts.after(r_sb))
                    pieces.update(route=route)
                run_layers(chain, counts, pieces)
            pre_ps_free()
            for q in range(NT // 4):
                bank = (pre_ps, turn_ps)[q % 2]
                if q >= 2:
                    eng.wait_ge(r_sb, counts.after(r_sb))
                for m in range(4):
                    tile = 4 * q + m
                    last = eng.transpose(bank[:, m * P:(m + 1) * P], xb[:, tile * D:(tile + 1) * D], eye[:, :])
                last.then_inc(r_ps, 1)

            def shared(q):
                for part in range(2):
                    for c in range(2):
                        last = eng.matmul(score_ps[part][:, c, :], shared_w[:, part * HID + c:(part + 1) * HID:2],
                                          xt_all[:, q * 512:(q + 1) * 512], start=True, stop=True)
                    last.then_inc(sh_made, 1)
                eng.wait_ge(sh_gated, counts.after(sh_gated))
                bank = (pre_ps, turn_ps)[q % 2]
                for m in range(4):
                    for c in range(2):
                        last = eng.matmul(bank[:, m * P:(m + 1) * P], sh_hid[:, c * 512 + m * P:c * 512 + (m + 1) * P],
                                          shared_w[:, 2 * HID + c * D:2 * HID + (c + 1) * D], start=(c == 0), stop=(c == 1))
                last.then_inc(sh_made, 1)

            eng.wait_ge(r_sb, counts.after(r_sb, 2))

            def turn_rows(n):
                eng.wait_ge(weights_in[n], turn_rows.arrived)
                for j in range(SLOT_J):
                    last = eng.transpose(turn_ps[:, j * SLOT_P:(j + 1) * SLOT_P], ex_rows[n][:, j * P:(j + 1) * P],
                                         eye[0:SLOT_P, 0:SLOT_P])
                last.then_inc(rows_turned, 1)

            def up(bank, part, n, full):
                w = ew[n][:, part * HID:(part + 1) * HID]
                for c in range(2):
                    last = eng.matmul(bank[:, c, 0:CAP], w[:, c::2], ex_t[n % 2], start=True, stop=True)
                last.then_inc(full, 1)

            def down(n):
                if copied[0]:
                    eng.wait_ge(out_rows, counts.after(out_rows))
                copied[0] = True
                for j in range(SLOT_J):
                    for c in range(2):
                        last = eng.matmul(pre_ps[0:SLOT_P, j * D:(j + 1) * D],
                                          ex_h[n % 2][:, c * CAP + j * SLOT_P:c * CAP + (j + 1) * SLOT_P],
                                          ew[n][:, 2 * HID + c * D:2 * HID + (c + 1) * D], start=(c == 0), stop=(c == 1))
                last.then_inc(downed, 1)

            def step(n, round_, first=False, last=False):
                eng.wait_ge(rows_copied, counts.after(rows_copied))
                if not first:
                    eng.wait_ge(silued, counts.after(silued))
                up(score_ps[0], 0, n, gate_made)
                if not first:
                    eng.wait_ge(gated, counts.after(gated))
                up(score_ps[1], 1, n, up_made)
                if not last:
                    turn_rows.arrived = round_(n + 1)
                    turn_rows((n + 1) % RING)
                if not first:
                    down((n - 1) % RING)

            copied = [False]
            turn_rows.arrived = 64
            turn_rows(0)
            once = lambda m: 64 * (1 + m // RING)
            step(0, once, first=True)
            for n in range(1, RING):
                step(n, once)
            with counts.loop(E // RING - 2) as i:
                for n in range(RING):
                    step(n, lambda m: i * 64 + 64 * (2 + m // RING))
            for n in range(RING):
                step(n, lambda m: 64 * (E // RING), last=(n == RING - 1))
            eng.wait_ge(gated, counts.after(gated))
            down(RING - 1)
            eng.wait_ge(out_rows, counts.after(out_rows))
            for q in range(NT // 4):
                if q >= 2:
                    eng.wait_ge(sh_summed, counts.after(sh_summed))
                shared(q)

        @block.scalar
        def _(eng):
            counts = Counts("scalar", eng, per)

            def turn_x(L, b, par, k):
                eng.wait_ge(x_turned, counts.after(x_turned))
                n = S + C if L.cross else S
                if L is WIDE:
                    eng.activation(xt[:, 0:S], pre_ps[:, 0:S], ACT.Identity, scale=ln_wb[:, 0:1], bias=ln_wb[:, 1:2])
                    ins = eng.activation(xt[:, S:n], pre_ps[:, S:n], ACT.Identity, scale=ln_wb[:, 2:3], bias=ln_wb[:, 3:4])
                elif L.rms:
                    ins = eng.activation(xt[:, 0:n], pre_ps[:, 0:n], ACT.Copy, scale=norm_w[L.name][:, 0:1])
                else:
                    ins = eng.activation(xt[:, 0:n], pre_ps[:, 0:n], ACT.Copy)
                ins.then_inc(xt_ready, 1)

            def copy_turned(dst, n, bank):
                eng.wait_ge(turned, counts.after(turned))
                ins = eng.activation(dst, turn_banks[bank][:, 0:n], ACT.Copy)
                ins.then_inc(operands, 1)

            def turn_q(L, b, par, k):
                copy_turned(qt[par][:, (k % 2) * 4 * S:(k % 2 + 1) * 4 * S], 4 * S, k % 2)

            def turn_k(L, b, par, k):
                n = L.ktiles * L.keys * L.key_tiles
                for first in range(0, n, 4 * S):
                    m = min(n - first, 4 * S)
                    copy_turned(kt_[par][:, first:first + m], m, first // (4 * S))

            def scores(L, b, par, k):
                g, kt, q0, q1 = L.steps[k]
                eng.wait_ge(scored, counts.after(scored))
                eng.wait_ge(probs_free, counts.after(probs_free))
                src = score_ps[k % 2][0:L.keys, :, :].rearrange("p s (u q) -> p (s u) q", u=2)[:, :, q0:q1]
                dst = probs[k % PROBS][0:L.keys, :].rearrange("p (j q) -> p j q", q=S)[:, :, q0:q1]
                eng.activation(dst, src, ACT.Exp, scale=SCALE).then_inc(probs_ready, 1)

            def output(L, b, par, k):
                eng.wait_ge(merged_turned, counts.after(merged_turned))
                eng.activation(ont[:, :], post_ps[:, 0:TILES * D], ACT.Copy).then_inc(ont_ready, 1)

            def wide_project(L, b, par, k):
                eng.wait_ge(wide_made, counts.after(wide_made))
                dst, src, scale = wide_copy(L, par, k)
                eng.activation(dst, src, ACT.Copy, scale=scale).then_inc(wide_a, 1)

            def route(L, b, par, k):
                if k == 0:
                    eng.wait_ge(route_turned, counts.after(route_turned))
                    eng.activation(xt_cur, pre_ps[:, 0:TILES * P], ACT.Copy).then_inc(route_xt, 1)
                if k == 5:
                    eng.wait_ge(exps_asked, counts.after(exps_asked))
                    eng.activation(gates, gates, ACT.Exp).then_inc(exps_made, 1)

            def wide_exp(L, b, par, k):
                eng.wait_ge(topped, counts.after(topped))
                dst = wprobs[k % WPROBS]
                for n in range(TILES):
                    at = 2 * (k % WPROBS) + n
                    last = eng.activation(dst[:, n * WKEYS:(n + 1) * WKEYS], score_ps[k % 2][:, n, 0:WKEYS], ACT.Exp,
                                          bias=wtop[:, at:at + 1], accum_out=wden[:, at:at + 1])
                last.then_inc(exped, 1)

            def wide_turn(L, b, par, k):
                eng.wait_ge(probs_turned, counts.after(probs_turned))
                eng.activation(wturned[k % WTURNED][:, 0:2 * S], out_ps[:, :], ACT.Copy).then_inc(turned_a, 1)

            def wide_values(L, b, par, k):
                eng.wait_ge(pair_summed, counts.after(pair_summed))
                eng.activation(wout_t[:, k * S:(k + 1) * S], pre_ps[:, 0:S], ACT.Copy).then_inc(pair_out, 1)

            for chain in chains:
                for L in chain:
                    if L.rms or L is WIDE:
                        eng.wait_ge(loaded[L.name], loads_of(L))
                pieces = dict(turn_x=turn_x, turn_q=turn_q, turn_k=turn_k, scores=scores, output=output,
                              wide_project=wide_project, wide_exp=wide_exp, wide_turn=wide_turn, wide_values=wide_values)
                if L is WIDE:
                    pieces.update(route=route)
                run_layers(chain, counts, pieces)
            def activate(m):
                eng.wait_ge(gate_made, counts.after(gate_made))
                eng.activation(ex_g[m % 2].rearrange("p (c n) -> p c n", c=2), score_ps[0][:, :, 0:CAP], ACT.Silu)\
                   .then_inc(silued, 1)

            def copy_out(n, value):
                eng.wait_ge(downed, counts.after(downed))
                if value is not None:
                    eng.wait_ge(results_out[n], value)
                eng.activation(ex_out[n], pre_ps[0:SLOT_P, :], ACT.Copy).then_inc(out_rows, 1)

            activate(0)
            for n in range(1, RING):
                activate(n)
                copy_out(n - 1, None)
            activate(0)
            copy_out(RING - 1, None)
            for n in range(1, RING):
                activate(n)
                copy_out(n - 1, 16)
            with counts.loop(E // RING - 2) as i:
                for n in range(RING):
                    activate(n)
                    copy_out((n - 1) % RING, i * 16 + (32 if n else 16))
            copy_out(RING - 1, 16 * (E // RING - 1))
            for q in range(NT // 4):
                eng.wait_ge(sh_made, counts.after(sh_made))
                if q:
                    eng.wait_ge(sh_gated, q)
                eng.activation(sh_gate.rearrange("p (c n) -> p c n", c=2), score_ps[0][:, :, :], ACT.Silu).then_inc(sh_silu, 1)
                eng.wait_ge(sh_made, counts.after(sh_made, 2))

        @block.vector
        def _(eng):
            counts = Counts("vector", eng, per)

            for buf in (stack_words, vals_all, qk, wmv):
                eng.memset(buf[:, :], 0.0).then_inc(v_step, 1)
                eng.wait_ge(v_step, counts.after(v_step))
            eng.memset(k_stack[:, :].rearrange("p (n s) -> p n s", s=PART)[:, :, ROWS:ROWS_MAX], 1.0).then_inc(zeroed, 1)
            for n in range(2):
                eng.memset(vals[n][:, :].rearrange("p (n c) -> p n c", c=32)[:, :, HD:HD + 1], 1.0).then_inc(zeroed, 1)
            eng.wait_ge(setup_ps, counts.after(setup_ps))
            eng.tensor_copy(weights["g"][:, D:D + 2 * KVH * HD], pre_ps[:, 0:2 * KVH * HD]).then_inc(setup_sb, 1)
            eng.wait_ge(loaded["mask"], 16)
            eng.tensor_scalar(given[:, :], given8[:, :], -NEG, NEG, ALU.mult, ALU.add).then_inc(setup_sb, 1)
            eng.wait_ge(zeroed, 4)
            for half_ in range(2):
                eng.wait_ge(setup_ps, counts.after(setup_ps))
                ins = eng.tensor_copy(given_t[0:C, half_ * 8 * P:(half_ + 1) * 8 * P], turn_ps[:, :].bitcast(BF16)[0:C, :])
                ins.then_inc(setup_sb if half_ == 0 else zeroed, 1)

            def wide_tiles(b, par):
                src = rows_of(xb, b)
                return [(src[:, 0:D], xs[par][:, 0:D], P), (src[:, D:2 * D], xs[par][:, D:2 * D], P),
                        (ctx_all[:, bass.ts(b, D)], xc[:, :], C)]

            def norm(L, b, par, k):
                src = rows_of(x0 if L.name == "g" else xb, b)
                if L is WIDE:
                    tiles = wide_tiles(b, par)
                    for n, (a, _, m) in enumerate(tiles):
                        eng.bn_stats(wstats[0:m, 6 * n:6 * n + 6], a).then_inc(v_step, 1)
                        counts.moved(v_step)
                    eng.wait_ge(v_step, counts.after(v_step, 0))
                    eng.sem_inc(waited, 1)
                    for n, (_, _, m) in enumerate(tiles):
                        eng.bn_aggr(wmv[0:m, 2 * n:2 * n + 2], wstats[0:m, 6 * n:6 * n + 6]).then_inc(v_step if n < 2 else pow_asked, 1)
                        counts.moved(v_step if n < 2 else pow_asked)
                    eng.wait_ge(v_step, counts.after(v_step, 0))
                    return
                if L.cross:
                    eng.tensor_copy(xc[:, :], ctx_all[:, bass.ts(b, D)]).then_inc(v_step, 1)
                    eng.wait_ge(v_step, counts.after(v_step))
                if L.rms:
                    eng.tensor_tensor(sq[:, :], src, src, ALU.mult).then_inc(v_step, 1)
                    eng.wait_ge(v_step, counts.after(v_step))
                    eng.tensor_reduce(ss[:, :], sq[:, :].rearrange("p (t d) -> p t d", d=D), AX_X, ALU.add).then_inc(pow_asked, 1)

            def normed(L, b, par, k):
                src = rows_of(x0 if L.name == "g" else xb, b)
                if L is WIDE:
                    eng.wait_ge(pow_done, counts.after(pow_done))
                    for n, (a, dst, m) in enumerate(wide_tiles(b, par)):
                        eng.tensor_scalar(dst, a, wmv[0:m, 2 * n:2 * n + 1], wrs[0:m, n:n + 1],
                                          ALU.subtract, ALU.mult).then_inc(v_step if n < 2 else x_rows, 1)
                        counts.moved(v_step if n < 2 else x_rows)
                    eng.wait_ge(v_step, counts.after(v_step, 0))
                    return
                if not L.rms:
                    eng.tensor_copy(xs[par][:, :], src).then_inc(x_rows, 1)
                    return
                eng.wait_ge(pow_done, counts.after(pow_done))
                eng.tensor_tensor(xs[par][:, :].rearrange("p (t d) -> p t d", d=D), src.rearrange("p (t d) -> p t d", d=D),
                                  rs[:, :].unsqueeze(2).broadcast_to([P, TILES, D]), ALU.mult).then_inc(x_rows, 1)

            def project(L, b, par, k):
                eng.wait_ge(projected, counts.after(projected))
                q_dst = qk[:, 0:TILES * D].rearrange("p (t d) -> p t d", d=D)
                k_dst = qk[:, TILES * D:L.flat].rearrange("p (t d) -> p t d", d=L.kn)
                src = pre_ps[:, 0:TILES * (D + L.kn)].rearrange("p (t d) -> p t d", t=TILES)
                if L.cross:
                    bi = bias_in[L.name]
                    eng.tensor_tensor(q_dst, pre_ps[:, 0:TILES * D].rearrange("p (t d) -> p t d", d=D),
                                      bi[:, 0:D].unsqueeze(1).broadcast_to([P, TILES, D]), ALU.add)
                    last = eng.tensor_tensor(qk[0:C, TILES * D:L.flat], pre_ps[0:C, 2 * D:3 * D], bi[0:C, D:2 * D], ALU.add)
                elif L.bias:
                    bi = bias_in[L.name]
                    eng.tensor_tensor(q_dst, src[:, :, 0:D], bi[:, 0:D].unsqueeze(1).broadcast_to([P, TILES, D]), ALU.add)
                    last = eng.tensor_tensor(k_dst, src[:, :, D:2 * D], bi[:, D:2 * D].unsqueeze(1).broadcast_to([P, TILES, D]),
                                             ALU.add)
                else:
                    eng.tensor_copy(q_dst, src[:, :, 0:D])
                    last = eng.tensor_copy(k_dst, src[:, :, D:D + L.kn])
                last.then_inc(pre_read, 1)
                counts.moved(pre_read)
                eng.wait_ge(pre_read, counts.after(pre_read, 0))

            def project_v(L, b, par, k):
                eng.wait_ge(projected, counts.after(projected))
                v = vals[par][0:L.keys, :].rearrange("p (t h c) -> p t h c", t=TILES, c=32)
                for n in range(L.key_tiles):
                    src = turn_ps[0:L.keys, n * L.kn:(n + 1) * L.kn].rearrange("p (h c) -> p h c", c=HD)
                    if L.bias:
                        last = eng.tensor_tensor(v[:, n, 0:L.kvh, 0:HD], src, bias_in[L.name][0:L.keys, 2 * D:3 * D]
                                                 .rearrange("p (h c) -> p h c", c=HD), ALU.add)
                    else:
                        last = eng.tensor_copy(v[:, n, 0:L.kvh, 0:HD], src)
                last.then_inc(v_step, 1)
                counts.moved(v_step)

            def cut(L, b, par, k):
                n, m = L.flat, L.flat // HD
                src = qk[:, 0:n]
                by_head = src.rearrange("p (n c) -> p n c", c=HD)
                if k == 0 and L.rope:
                    eng.tensor_tensor(qk2[:, 0:n], src, cos[L.name][:, :], ALU.mult).then_inc(v_step, 1)
                    counts.moved(v_step)
                    eng.tensor_tensor(qk3[:, 0:n].rearrange("p (n two) -> p n two", two=2),
                                      src.rearrange("p (n two) -> p n two", two=2)[:, :, ::-1],
                                      sin[L.name][:, :].rearrange("p (n two) -> p n two", two=2), ALU.mult).then_inc(v_step, 1)
                    eng.wait_ge(v_step, counts.after(v_step))
                    eng.tensor_tensor(src, qk2[:, 0:n], qk3[:, 0:n], ALU.add).then_inc(v_step, 1)
                    eng.wait_ge(v_step, counts.after(v_step))
                if k == 0 and L.qk_norm:
                    eng.tensor_tensor(qk2[:, 0:n], src, src, ALU.mult).then_inc(v_step, 1)
                    eng.wait_ge(v_step, counts.after(v_step))
                    eng.tensor_reduce(nss[:, 0:m], qk2[:, 0:n].rearrange("p (n c) -> p n c", c=HD), AX_X, ALU.add)\
                       .then_inc(pow_asked, 1)
                if k == 1 and L.qk_norm:
                    eng.wait_ge(pow_done, counts.after(pow_done))
                    eng.tensor_tensor(by_head, by_head, nrs[:, 0:m].unsqueeze(2).broadcast_to([P, m, HD]), ALU.mult)\
                       .then_inc(v_step, 1)
                    eng.wait_ge(v_step, counts.after(v_step))
                if k == 1:
                    eng.tensor_copy(cuts[0][:, 0:n], src).then_inc(v_step, 1)
                    eng.wait_ge(v_step, counts.after(v_step))
                    eng.tensor_tensor(qk2[:, 0:n], src, cuts[0][:, 0:n], ALU.subtract).then_inc(v_step, 1)
                    eng.wait_ge(v_step, counts.after(v_step))
                if k == 2:
                    eng.tensor_copy(cuts[1][:, 0:n], qk2[:, 0:n]).then_inc(v_step, 1)
                    eng.wait_ge(v_step, counts.after(v_step))
                    eng.tensor_tensor(cuts[2][:, 0:n], qk2[:, 0:n], cuts[1][:, 0:n], ALU.subtract).then_inc(v_step, 1)
                    eng.wait_ge(v_step, counts.after(v_step))
                if k != 3:
                    return
                if not (L.first and isinstance(b, int) and b == 0):
                    eng.wait_ge(operands, counts.after(operands, L.turns))
                q_slots = (slice(0, 3), slice(3, 6, 2), slice(4, 5))
                k_slots = (slice(2, 5), slice(0, 6, 5), slice(1, 2))
                for stack, slots, first, m in ((q_stack, q_slots, 0, TILES * H),
                                               (k_stack, k_slots, TILES * D, L.key_tiles * L.kvh)):
                    dst = stack[:, 0:m * PART].rearrange("p (n s c) -> p n s c", s=PART // HD, c=HD)
                    for part in range(3):
                        out = dst[:, :, slots[part], :]
                        last = eng.tensor_copy(out, cuts[part][:, first:first + m * HD].rearrange("p (n c) -> p n c", c=HD)
                                               .unsqueeze(2).broadcast_to([P, m, out.shape[2], HD]))
                last.then_inc(stacked, 1)
                counts.moved(stacked)
                eng.wait_ge(stacked, counts.after(stacked, 0))

            def top(L, b, par, k):
                q, side, u0, m, n = L.top_steps[k]
                bank, full, read = ((pre_ps, top_a, pre_read), (turn_ps, top_b, turn_read))[k % 2]
                eng.wait_ge(full, counts.after(full))
                dst = tops[:, q * H:(q + 1) * H].rearrange("p (u s) -> p u s", s=2)[:, u0:u0 + m, side]
                src = bank[:, 0:m * n].rearrange("p (m n) -> p m n", n=n)
                eng.tensor_reduce(dst, src, AX_X, ALU.max).then_inc(read, 1)
                counts.moved(read)

            def shift(L, b, par, k):
                eng.wait_ge(pre_read, counts.after(pre_read, 0))
                eng.wait_ge(turn_read, counts.after(turn_read, 0))
                slot = q_stack[:, :].rearrange("p (n s) -> p n s", s=PART)
                one = [slot[:, :, ROWS + n] for n in range(3)]
                eng.tensor_scalar(tops[:, :], tops[:, :], -1.0, None, ALU.mult).then_inc(v_step, 1)
                eng.wait_ge(v_step, counts.after(v_step))
                eng.tensor_copy(one[0], tops[:, :]).then_inc(v_step, 1)
                eng.wait_ge(v_step, counts.after(v_step))
                eng.tensor_tensor(top2[:, :], tops[:, :], one[0], ALU.subtract).then_inc(v_step, 1)
                eng.wait_ge(v_step, counts.after(v_step))
                eng.tensor_copy(one[1], top2[:, :]).then_inc(v_step, 1)
                eng.wait_ge(v_step, counts.after(v_step))
                ins = eng.tensor_tensor(one[2], top2[:, :], one[1], ALU.subtract)
                ins.then_inc(shifted, 1)
                counts.moved(shifted)
                eng.wait_ge(shifted, counts.after(shifted, 0))

            def values(L, b, par, k):
                eng.wait_ge(probs_free, counts.after(probs_free, len(L.steps) // 4))
                eng.tensor_copy(ot[:, k * S:(k + 1) * S], sums_ps[k % 2][:, 0:S]).then_inc(ot_ready, 1)

            def merge(L, b, par, k):
                for pair in (k,):
                    eng.wait_ge(rows_back, counts.after(rows_back))
                    src = post_ps[:, :].rearrange("p (n c) -> p n c", c=32)
                    eng.reciprocal(rden[:, :].unsqueeze(2), src[:, :, HD:HD + 1]).then_inc(v_step, 1)
                    eng.wait_ge(v_step, counts.after(v_step))
                    dst = on[:, :].rearrange("p (t g n c) -> p t g n c", t=TILES, g=2, c=HD)[:, :, pair, :, :]
                    ins = eng.tensor_tensor(dst, src[:, :, 0:HD].rearrange("p (t n) c -> p t n c", t=TILES),
                                            rden[:, :].rearrange("p (t n) -> p t n", t=TILES).unsqueeze(3)
                                            .broadcast_to([P, TILES, 8, HD]), ALU.mult)
                    ins.then_inc(merged, 1)
                    counts.moved(merged)
                    eng.wait_ge(merged, counts.after(merged, 0))

            def statistics():
                for n in range(TILES):
                    last = eng.bn_stats(stats[:, 6 * n:6 * n + 6], y[:, n * D:(n + 1) * D])
                last.then_inc(v_step, 1)
                eng.wait_ge(v_step, counts.after(v_step))
                eng.sem_inc(waited, 1)
                for n in range(TILES):
                    last = eng.bn_aggr(mv[:, 2 * n:2 * n + 2], stats[:, 6 * n:6 * n + 6])
                last.then_inc(pow_asked, 1)
                counts.moved(pow_asked)
                eng.wait_ge(pow_asked, counts.after(pow_asked, 0))

            def finished(L, b, par, k):
                if L.name == "g":
                    return
                eng.wait_ge(pow_done, counts.after(pow_done))
                dst = rows_of(xb, b)
                for n in range(TILES):
                    last = eng.tensor_scalar(dst[:, n * D:(n + 1) * D], y[:, n * D:(n + 1) * D], mv[:, 2 * n:2 * n + 1],
                                             lrs[:, n:n + 1], ALU.subtract, ALU.mult)
                done = batch_done if L is WIDE else v_step
                last.then_inc(done, 1)
                eng.wait_ge(done, counts.after(done))

            def output(L, b, par, k):
                eng.wait_ge(out_projected, counts.after(out_projected))
                src = rows_of(x0 if L.name == "g" else xb, b)
                acc = post_ps[:, 0:TILES * D]
                if L.name == "g":
                    eng.tensor_tensor(rows_of(xb, b), acc, src, ALU.add).then_inc(post_read, 1)
                    counts.moved(post_read)
                    eng.wait_ge(post_read, counts.after(post_read, 0))
                    return
                eng.tensor_tensor(y[:, :], acc, src, ALU.add).then_inc(post_read, 1)
                counts.moved(post_read)
                eng.wait_ge(post_read, counts.after(post_read, 0))
                if L.name == "l":
                    eng.tensor_tensor(y[:, :], y[:, :], rows_of(x0, b), ALU.add).then_inc(v_step, 1)
                    eng.wait_ge(v_step, counts.after(v_step))
                else:
                    eng.tensor_tensor(y[:, :].rearrange("p (t d) -> p t d", d=D), y[:, :].rearrange("p (t d) -> p t d", d=D),
                                      bias_out[L.name][:, :].unsqueeze(1).broadcast_to([P, TILES, D]), ALU.add).then_inc(v_step, 1)
                    eng.wait_ge(v_step, counts.after(v_step))
                statistics()

            def mixed(L, b, par, k):
                eng.wait_ge(projected, counts.after(projected))
                eng.tensor_tensor(y[:, :], pre_ps[:, 0:TILES * D], rows_of(xb, b), ALU.add).then_inc(pre_read, 1)
                counts.moved(pre_read)
                eng.wait_ge(pre_read, counts.after(pre_read, 0))
                eng.tensor_tensor(y[:, :].rearrange("p (t d) -> p t d", d=D), y[:, :].rearrange("p (t d) -> p t d", d=D),
                                  bias_mix[:, :].unsqueeze(1).broadcast_to([P, TILES, D]), ALU.add).then_inc(v_step, 1)
                eng.wait_ge(v_step, counts.after(v_step))
                statistics()

            def wide_scores(L, b, par, k):
                eng.wait_ge(wide_scored, counts.after(wide_scored))
                at = 2 * (k % WPROBS)
                eng.tensor_reduce(wtop[:, at:at + 2], score_ps[k % 2][:, :, 0:WKEYS], AX_X, ALU.max, negate=True)\
                   .then_inc(topped, 1)

            def wide_scale(L, b, par, k):
                eng.wait_ge(exped, counts.after(exped))
                at = 2 * (k % WPROBS)
                eng.reciprocal(wrden[:, at:at + 2], wden[:, at:at + 2]).then_inc(v_step, 1)
                eng.wait_ge(v_step, counts.after(v_step))
                for n in range(TILES):
                    src = wprobs[k % WPROBS][:, n * WKEYS:(n + 1) * WKEYS]
                    last = eng.tensor_scalar(src, src, wrden[:, at + n:at + n + 1], None, ALU.mult)
                last.then_inc(scaled, 1)

            def wide_turn(L, b, par, k):
                eng.wait_ge(probs_turned, counts.after(probs_turned))
                eng.tensor_copy(wturned[k % WTURNED][0:C, 2 * S:3 * S], post_ps[0:C, 0:S]).then_inc(turned_c, 1)

            def wide_output(L, b, par, k):
                eng.wait_ge(out_projected, counts.after(out_projected))
                eng.tensor_tensor(y[:, :], post_ps[:, 0:TILES * D], rows_of(xb, b), ALU.add).then_inc(post_read, 1)
                counts.moved(post_read)
                eng.wait_ge(post_read, counts.after(post_read, 0))
                statistics()

            def centroids_ready():
                eng.wait_ge(exp_loaded, 16 * 6)
                eng.memset(taken[:, :], 0.0).then_inc(v_step, 1)
                eng.wait_ge(v_step, counts.after(v_step))
                eng.tensor_tensor(cent_sq[:, :], centroids[:, :], centroids[:, :], ALU.mult).then_inc(v_step, 1)
                eng.wait_ge(v_step, counts.after(v_step))
                eng.tensor_reduce(cent_s[:, 0:1], cent_sq[:, :], AX_X, ALU.add).then_inc(pow_asked, 1)
                eng.wait_ge(pow_done, counts.after(pow_done))
                eng.tensor_scalar(cent_s[:, 2:3], cent_s[:, 1:2], 1e-12, None, ALU.max).then_inc(v_step, 1)
                eng.wait_ge(v_step, counts.after(v_step))
                eng.reciprocal(cent_s[:, 3:4], cent_s[:, 2:3]).then_inc(v_step, 1)
                eng.wait_ge(v_step, counts.after(v_step))
                eng.tensor_scalar(centroids[:, :], centroids[:, :], cent_s[:, 3:4], None, ALU.mult).then_inc(r_sb, 1)
                counts.moved(r_sb)
                eng.wait_ge(r_ps, counts.after(r_ps))
                eng.tensor_copy(cent_t[:, :], out_ps[:, 0:G + E]).then_inc(r_sb, 1)
                counts.moved(r_sb)

            def step(instruction):
                instruction.then_inc(v_step, 1)
                eng.wait_ge(v_step, counts.after(v_step))

            def route(L, b, par, k):
                by_group = [P, TILES * G, E // G]
                by_k = gates.rearrange("p (t k) -> p t k", k=K)
                score_groups = e_score.rearrange("p (n m) -> p n m", m=E // G)
                masked_groups = masked.rearrange("p (n m) -> p n m", m=E // G)
                if k == 0:
                    eng.wait_ge(rows_ready, counts.after(rows_ready))
                    step(eng.tensor_tensor(row_sq, rows_cur, rows_cur, ALU.mult))
                    eng.tensor_reduce(small[:, 0:TILES], row_sq.rearrange("p (t d) -> p t d", d=D), AX_X, ALU.add)\
                       .then_inc(pow_asked, 1)
                elif k == 1:
                    eng.wait_ge(pow_done, counts.after(pow_done))
                    step(eng.tensor_scalar(small[:, 2 * TILES:3 * TILES], small[:, TILES:2 * TILES], 1e-12, None, ALU.max))
                    step(eng.reciprocal(small[:, 3 * TILES:4 * TILES], small[:, 2 * TILES:3 * TILES]))
                    inverse = small[:, 3 * TILES:4 * TILES].unsqueeze(2)
                    eng.wait_ge(route_scored, counts.after(route_scored))
                    src = pre_ps[:, 0:TILES * (G + E)].rearrange("p (t n) -> p t n", n=G + E)
                    eng.tensor_tensor(g_score.rearrange("p (t n) -> p t n", n=G), src[:, :, 0:G],
                                      inverse.broadcast_to([P, TILES, G]), ALU.mult)
                    eng.tensor_tensor(e_score.rearrange("p (t n) -> p t n", n=E), src[:, :, G:],
                                      inverse.broadcast_to([P, TILES, E]), ALU.mult).then_inc(route_read, 1)
                    counts.moved(route_read)
                    eng.wait_ge(route_read, counts.after(route_read, 0))
                    by_tile = e_score.rearrange("p (t n) -> p t n", n=E)
                    step(eng.tensor_tensor(by_tile, by_tile, choice_bias[:, :].unsqueeze(1).broadcast_to([P, TILES, E]), ALU.add))
                elif k == 2:
                    for n in range(TILES):
                        one = slice(n * G * G, (n + 1) * G * G)
                        groups = g_score[:, n * G:(n + 1) * G]
                        other = groups.unsqueeze(1).broadcast_to([P, G, G])
                        own = groups.unsqueeze(2).broadcast_to([P, G, G])
                        eng.tensor_tensor(cmp_gt[:, one].rearrange("p (i j) -> p i j", j=G), other, own, ALU.is_gt)
                        last = eng.tensor_tensor(cmp_eq[:, one].rearrange("p (i j) -> p i j", j=G), other, own, ALU.is_equal)
                    step(last)
                    pairs_ = cmp_eq.rearrange("p (t n) -> p t n", n=G * G)
                    step(eng.tensor_tensor(pairs_, pairs_, before[:, :].unsqueeze(1).broadcast_to([P, TILES, G * G]), ALU.mult))
                    step(eng.tensor_tensor(cmp_gt, cmp_gt, cmp_eq, ALU.add))
                elif k == 3:
                    step(eng.tensor_reduce(rank, cmp_gt.rearrange("p (n j) -> p n j", j=G), AX_X, ALU.add))
                    step(eng.tensor_scalar(rank, rank, float(G // 2), None, ALU.is_lt))
                    step(eng.tensor_tensor(score_groups, score_groups, rank.unsqueeze(2).broadcast_to(by_group), ALU.mult))
                    step(eng.tensor_scalar(rank, rank, 1e9, -1e9, ALU.mult, ALU.add))
                    step(eng.tensor_tensor(masked_groups, score_groups, rank.unsqueeze(2).broadcast_to(by_group), ALU.add))
                elif k == 4:
                    eng.sem_inc(waited, 1)
                    for n in range(TILES):
                        last = eng.max(top8[:, n * 8:(n + 1) * 8], masked[:, n * E:(n + 1) * E])
                    step(last)
                    eng.sem_inc(waited, 1)
                    for n in range(TILES):
                        last = eng.max_index(idx8.bitcast(U32)[:, n * 8:(n + 1) * 8], top8[:, n * 8:(n + 1) * 8],
                                             masked[:, n * E:(n + 1) * E])
                    step(last)
                    top4 = top8.rearrange("p (t n) -> p t n", n=8)
                    eng.tensor_tensor(by_k, top4[:, :, 0:K], top4[:, :, 0:1].broadcast_to([P, TILES, K]), ALU.subtract)\
                       .then_inc(exps_asked, 1)
                elif k == 5:
                    step(eng.tensor_copy(idx_f.rearrange("p (t k) -> p t k", k=K),
                                         idx8.bitcast(U32).rearrange("p (t n) -> p t n", n=8)[:, :, 0:K]))
                    step(eng.tensor_tensor(onehot.rearrange("p (n e) -> p n e", e=E), iota_e[:, :].unsqueeze(1).broadcast_to([P, TK, E]),
                                           idx_f.unsqueeze(2).broadcast_to([P, TK, E]), ALU.is_equal))
                    with nc.allow_low_precision(reason="sums of at most one are exact"):
                        eng.tensor_reduce(chosen.rearrange("p (t e) -> p t e", e=E),
                                          onehot.rearrange("p (t k e) -> p t e k", k=K, e=E), AX_X, ALU.add).then_inc(route_chosen, 1)
                elif k == 6:
                    eng.wait_ge(exps_made, counts.after(exps_made))
                    step(eng.tensor_reduce(small[:, 4 * TILES:5 * TILES], by_k, AX_X, ALU.add))
                    step(eng.reciprocal(small[:, 4 * TILES:5 * TILES], small[:, 4 * TILES:5 * TILES]))
                    step(eng.tensor_tensor(by_k, by_k, small[:, 4 * TILES:5 * TILES].unsqueeze(2).broadcast_to([P, TILES, K]), ALU.mult))
                    eng.wait_ge(route_counted, counts.after(route_counted))
                    in_tile, of_tile = pre_ps[:, 0:TILES * E], pre_ps[:, TILES * E:2 * TILES * E]
                    for n in range(TILES):
                        tile = slice(n * E, (n + 1) * E)
                        step(eng.tensor_tensor(totals[:, tile], in_tile[:, tile], taken[:, :], ALU.add))
                        last = eng.tensor_tensor(taken[:, :], of_tile[:, tile], taken[:, :], ALU.add)
                        if n < TILES - 1:
                            step(last)
                    last.then_inc(route_read, 1)
                    counts.moved(route_read)
                    eng.wait_ge(route_read, counts.after(route_read, 0))
                elif k == 7:
                    for n in range(TILES):
                        span = slice(n * K * E, (n + 1) * K * E)
                        last = eng.tensor_tensor(picked[:, span].rearrange("p (k e) -> p k e", k=K),
                                                 onehot[:, span].rearrange("p (k e) -> p k e", k=K),
                                                 totals[:, n * E:(n + 1) * E].unsqueeze(1).broadcast_to([P, K, E]), ALU.mult)
                    step(last)
                    step(eng.tensor_reduce(pos, picked.rearrange("p (n e) -> p n e", e=E), AX_X, ALU.add))
                    step(eng.tensor_scalar(keep, pos, float(CAP), None, ALU.is_lt))
                    step(eng.tensor_tensor(gate[:, bass.ts(b, TK)], gates, keep, ALU.mult))
                elif k == 8:
                    step(eng.tensor_scalar(keep, keep, -BEYOND, BEYOND, ALU.mult, ALU.add))
                    step(eng.tensor_scalar(idx_f, idx_f, float(CAP), None, ALU.mult))
                    step(eng.tensor_tensor(keep, keep, pos, ALU.add))
                    eng.tensor_tensor(slot_cur[:, :], keep, idx_f, ALU.add).then_inc(slots_known, 1)
                    step(eng.tensor_scalar(pos, pos, float(CAP - 1), None, ALU.min))
                    step(eng.tensor_tensor(slot_out[:, bass.ts(b, TK)], pos, idx_f, ALU.add))

            eng.sem_inc(probs_free, PROBS)
            counts.moved(probs_free, PROBS)
            eng.sem_inc(post_read, 1)
            counts.moved(post_read)
            eng.wait_ge(loaded["x"], 16)
            eng.wait_ge(loaded["ctx"], 16)
            for chain in chains:
                for L in chain:
                    eng.wait_ge(loaded["x_" if L.name == "x" else L.name], loads_of(L))
                if L is MIXING:
                    eng.wait_ge(setup_ps, counts.after(setup_ps))
                    eng.tensor_copy(freq_a[:, :], out_ps[:, 0:2 * D]).then_inc(setup_sb, 1)
                    eng.wait_ge(setup_ps, counts.after(setup_ps))
                    eng.tensor_copy(mix_w[:, :], out_ps[:, 0:D]).then_inc(setup_sb, 1)
                pieces = dict(norm=norm, project=project, project_v=project_v, cut=cut, top=top, shift=shift, values=values,
                              merge=merge, output=output, mixed=mixed, wide_scores=wide_scores,
                              wide_scale=wide_scale, wide_turn=wide_turn, wide_output=wide_output, normed=normed,
                              finished=finished)
                if L is WIDE:
                    centroids_ready()
                    pieces.update(route=route)
                run_layers(chain, counts, pieces)
                if L not in (MIXING, WIDE):
                    eng.wait_ge(operands, counts.after(operands, L.turns))
            for q in range(NT // 4):
                eng.wait_ge(r_ps, counts.after(r_ps))
                eng.tensor_copy(xt_all[:, q * 512:(q + 1) * 512], (pre_ps, turn_ps)[q % 2][:, :]).then_inc(r_sb, 1)
                counts.moved(r_sb)

            def shared(q):
                eng.wait_ge(sh_made, counts.after(sh_made, 2))
                eng.wait_ge(sh_silu, q + 1)
                eng.tensor_tensor(sh_hid.rearrange("p (c n) -> p c n", c=2), sh_gate.rearrange("p (c n) -> p c n", c=2),
                                  score_ps[1][:, :, :], ALU.mult).then_inc(sh_gated, 1)
                eng.wait_ge(sh_made, counts.after(sh_made))
                eng.tensor_tensor(acc[:, q * 512:(q + 1) * 512], (pre_ps, turn_ps)[q % 2][:, :],
                                  xb[:, q * 512:(q + 1) * 512], ALU.add).then_inc(sh_summed, 1)
                counts.moved(sh_summed)
                eng.wait_ge(sh_summed, counts.after(sh_summed, 0))

            def copy_rows(n):
                eng.wait_ge(rows_turned, counts.after(rows_turned))
                eng.tensor_copy(ex_t[n % 2], turn_ps[:, 0:CAP]).then_inc(rows_copied, 1)

            def multiply(n):
                eng.wait_ge(silued, counts.after(silued))
                eng.wait_ge(up_made, counts.after(up_made))
                eng.tensor_tensor(ex_h[n % 2].rearrange("p (c n) -> p c n", c=2), ex_g[n % 2].rearrange("p (c n) -> p c n", c=2),
                                  score_ps[1][:, :, 0:CAP], ALU.mult).then_inc(gated, 1)

            copy_rows(0)
            with counts.loop((E - 2) // 2) as i:
                for n in range(2):
                    multiply(n)
                    copy_rows(n + 1)
            multiply(0)
            copy_rows(1)
            multiply(1)

            def combine(q):
                eng.wait_ge(gathered_in[q], 16 * GROUP * K)
                for k in range(K):
                    for m in range(GROUP):
                        tile = q * GROUP + m
                        at = acc[:, tile * D:(tile + 1) * D]
                        last = eng.scalar_tensor_tensor(out=at, in0=gathered[q][:, (m * K + k) * D:(m * K + k + 1) * D],
                                                        scalar=gate[:, tile * K + k:tile * K + k + 1], in1=at,
                                                        op0=ALU.mult, op1=ALU.add)
                    last.then_inc(v_step, 1)
                    eng.wait_ge(v_step, counts.after(v_step))
                for m in range(GROUP):
                    tile = q * GROUP + m
                    last = eng.bn_stats(lstats[:, 6 * m:6 * m + 6], acc[:, tile * D:(tile + 1) * D])
                last.then_inc(v_step, 1)
                eng.wait_ge(v_step, counts.after(v_step))
                for m in range(GROUP):
                    at = 2 * (q % 2 * GROUP + m)
                    last = eng.bn_aggr(lmv[:, at:at + 2], lstats[:, 6 * m:6 * m + 6])
                last.then_inc(pow_asked, 1)
                counts.moved(pow_asked)
                eng.wait_ge(pow_asked, counts.after(pow_asked, 0))

            def last_norm(q):
                eng.wait_ge(pow_done, counts.after(pow_done))
                for m in range(GROUP):
                    tile = slice((q * GROUP + m) * D, (q * GROUP + m + 1) * D)
                    at = q % 2 * GROUP + m
                    last = eng.tensor_scalar(xb[:, tile], acc[:, tile], lmv[:, 2 * at:2 * at + 1], glrs[:, at:at + 1],
                                             ALU.subtract, ALU.mult)
                last.then_inc(written, 1)

            shared(0)
            for q in range(NT // GROUP):
                if q % 2 == 0 and q // 2 + 1 < NT // 4:
                    shared(q // 2 + 1)
                combine(q)
                if q:
                    last_norm(q - 1)
            last_norm(NT // GROUP - 1)


def loads_of(L):
    if L is MIXING:
        return 16 * 8
    if L is WIDE:
        return 16 * 4
    return 16 * ((2 + 2 * L.rope + 2 * L.bias) + L.rms)


def rope_tables(L, base):
    dim = np.arange(HD // 2, dtype=np.float32)
    pos = np.arange(S, dtype=np.float32)[:, None]
    if L.name == "a":
        angle = pos / np.exp(np.float32(2.0) * dim / np.float32(HD) * np.float32(np.log(10000.0)))[None, :]
    else:
        inv = np.float32(1.0) / np.float32(base) ** (np.arange(0, HD, 2, dtype=np.float32) / np.float32(HD))
        angle = pos * inv[None, :]
    angle = angle.astype(np.float32)
    c, s = np.cos(angle), np.sin(angle)
    c2 = np.repeat(c, 2, axis=1)
    s2 = np.stack([-s, s], axis=-1).reshape(S, HD)

    def lay(table):
        q = np.tile(table.reshape(TILES, P, 1, HD), (1, 1, H, 1)).transpose(1, 0, 2, 3).reshape(P, -1)
        k = np.tile(table.reshape(TILES, P, 1, HD), (1, 1, L.kvh, 1)).transpose(1, 0, 2, 3).reshape(P, -1)
        return np.ascontiguousarray(np.concatenate([q, k], axis=1).astype(np.float32))
    return lay(c2), lay(s2)


def merged_rows(w, kv_heads=H):
    return w.reshape(H, HD, D)[[held_heads(kv_heads)[n] for n in MERGED]].reshape(D, D)


def held_columns(w):
    return w.reshape(D, H, HD)[:, held_heads(KVH)].reshape(D, D)


def layout(i):
    cat = np.concatenate
    a = {"x": i["x"], "ctx": i["ctx_1024"], "mask": i["mask_Bx1xSxS2_bf1"].reshape(B, S, C).view(np.uint8),
         "down_t": i["L0_attn_g_kv_down"].T, "ups": cat([i["L0_attn_g_k_up"], i["L0_attn_g_v_up"]], axis=1),
         "w_g": held_columns(i["L0_attn_g_wq"]), "wo_g": merged_rows(i["L0_attn_g_wo"], KVH), "nw_g": i["L0_attn_norm1_w"][:, None],
         "w_l": cat([held_columns(i["L0_attn_l_wq"]), i["L0_attn_l_wk"], i["L0_attn_l_wv"]], axis=1),
         "wo_l": merged_rows(i["L0_attn_l_wo"], KVH), "nw_l": i["L0_attn_norm2_w"][:, None]}
    for name, p, (q, k, v, o) in (("x", "L0_xattn_", ("Wq", "Wk", "Wv", "Wo")), ("a", "L1_attn_", ("wq", "wk", "wv", "wo"))):
        a[f"w_{name}"] = cat([i[p + q].T, i[p + k].T, i[p + v].T], axis=1)
        a[f"wo_{name}"] = merged_rows(i[p + o].T)
        a[f"bi_{name}"] = np.tile(cat([i[p + "bq"], i[p + "bk"], i[p + "bv"]])[None], (P, 1))
        a[f"bo_{name}"] = np.tile(i[p + "bo"][None], (P, 1))
    for L, base in ((NARROW[0], 1e6), (NARROW[1], 1e4), (NARROW[3], 1e4)):
        a[f"cos_{L.name}"], a[f"sin_{L.name}"] = rope_tables(L, base)
    wave = 2.0 * np.pi * (np.outer(np.arange(D), np.arange(D)) % D) / D
    a.update(Fr=np.cos(wave).astype(np.float32), Fi=-np.sin(wave).astype(np.float32), nFi=np.sin(wave).astype(np.float32),
             Gr=(np.cos(wave) / D).astype(np.float32), nGi=-(np.sin(wave) / D).astype(np.float32),
             freq_r=i["L0_ffn_w_freq_real"], freq_i=i["L0_ffn_w_freq_imag"],
             bias_mix=np.tile(i["L0_ffn_bias"][None], (P, 1)),
             wide_q=i["L1_xattn_Wq"], wide_kv=i["L1_xattn_Wkv"], wide_o=i["L1_xattn_Wo"],
             group_c=i["L1_ffn_group_centroids"], expert_c=i["L1_ffn_expert_centroids"],
             choice_bias=np.tile(i["L1_ffn_bias"][None], (P, 1)), sg=i["L1_ffn_sg"], su=i["L1_ffn_su"], sd=i["L1_ffn_sd"],
             wg=i["L1_ffn_wg"].reshape(E * D, HID), wu=i["L1_ffn_wu"].reshape(E * D, HID),
             wd=i["L1_ffn_wd"].reshape(E * P, 2 * D),
             ln_wb=np.stack([i["L1_xattn_ln2_w"], i["L1_xattn_ln2_b"], i["L1_xattn_ln1_w"], i["L1_xattn_ln1_b"]], axis=1))
    return {n: np.ascontiguousarray(v) for n, v in a.items()}


def make_program(nc, arrays, per):
    t = {n: nc.dram_tensor(n, a.shape, mybir.dt.from_np(a.dtype), kind="ExternalInput").ap() for n, a in arrays.items()}
    t["out"] = nc.dram_tensor("out", (B, S, D), F32, kind="ExternalOutput").ap()
    t["slots"] = nc.dram_tensor("slots", (E * CAP, D), F32, kind="Internal").ap()
    t["results"] = nc.dram_tensor("results", (E * CAP, D), F32, kind="Internal").ap()
    build_program(nc, t, per)


def kernel(**inputs):
    import concourse.bacc as bacc
    from concourse.bass_utils import run_bass_kernel_spmd

    arrays = layout({n: np.asarray(a) for n, a in inputs.items()})
    per = {}
    make_program(bacc.Bacc("TRN2", target_bir_lowering=False, num_devices=1), arrays, per)
    nc = bacc.Bacc("TRN2", target_bir_lowering=False, num_devices=1)
    make_program(nc, arrays, per)
    result = run_bass_kernel_spmd(nc, [arrays], core_ids=[0])
    return result.results[0]["out"]
```
